# Optimizing a Trainium2 kernel written in Bass

```python
import numpy as np
import jax
import jax.numpy as jnp

def _softmax(x, axis=-1):
    return jax.nn.softmax(x, axis=axis)

def _gelu(x):
    return jax.nn.gelu(x, approximate=True)

def _silu(x):
    return jax.nn.silu(x)

def _sigmoid(x):
    return jax.nn.sigmoid(x)

def _layernorm(x, axis=-1, eps=1e-05):
    m = jnp.mean(x, axis=axis, keepdims=True)
    v = jnp.var(x, axis=axis, keepdims=True)
    return (x - m) / jnp.sqrt(v + eps)

def _scatter_add(tgt, idx, src, axis=0):
    return tgt.at[idx].add(src)

def _segment_sum(src, seg, n):
    return jax.ops.segment_sum(src, seg, n)
kernel_name = 'mk_sandwich_d2_jaxref_r8_b8299c'

def setup_inputs(seed: int=0):
    np.random.seed(seed)
    _w = jnp.asarray

    def _L0_attn_setup():
        import jax, jax.numpy as jnp
        import numpy as np
        B, S, HID = (2, 512, 512)
        H, HKV, D = (32, 8, 128)
        G = H // HKV
        EPS = 1e-06

        def _reference_tuple_inner(hidden_states, Wq, bq, Wk, bk, Wv, bv, Wo, M, z):
            b, s, _ = hidden_states.shape
            q = (hidden_states @ Wq.T + bq).reshape(b, s, H, D)
            k = (hidden_states @ Wk.T + bk).reshape(b, s, HKV, D)
            v = (hidden_states @ Wv.T + bv).reshape(b, s, HKV, D)
            sig_q = jax.nn.elu(q) + 1.0
            sig_k = jax.nn.elu(k) + 1.0
            q_sel = sig_q[:, :, ::G, :]
            num = jnp.einsum('bshd,hde->bshe', q_sel, M)
            den = jnp.einsum('bshd,hd->bsh', q_sel, z)[..., None] + EPS
            retrieved = num / den
            out_heads = jnp.repeat(retrieved, G, axis=2)
            output = out_heads.reshape(b, s, H * D) @ Wo.T
            M_new = M + jnp.einsum('bshd,bshe->hde', sig_k, v)
            z_new = z + sig_k.sum(axis=(0, 1))
            return (output, M_new, z_new)
        key = jax.random.key(seed)
        ks = jax.random.split(key, 10)
        s = 0.02
        return {'hidden_states': jax.random.normal(ks[0], (B, S, HID), jnp.float32), 'Wq': jax.random.normal(ks[1], (H * D, HID), jnp.float32) * s, 'bq': jnp.zeros((H * D,), jnp.float32), 'Wk': jax.random.normal(ks[2], (HKV * D, HID), jnp.float32) * s, 'bk': jnp.zeros((HKV * D,), jnp.float32), 'Wv': jax.random.normal(ks[3], (HKV * D, HID), jnp.float32) * s, 'bv': jnp.zeros((HKV * D,), jnp.float32), 'Wo': jax.random.normal(ks[4], (HID, H * D), jnp.float32) * s, 'M': jax.random.normal(ks[5], (HKV, D, D), jnp.float32), 'z': jax.random.uniform(ks[6], (HKV, D), jnp.float32) * 100.0 + 1.0}
    _L0_attn_in = _L0_attn_setup()

    def _L0_ffn_setup():
        import jax, jax.numpy as jnp
        import numpy as np
        RMS_EPS = 1e-05
        key = jax.random.key(seed)
        k1, k2, k3, k4 = jax.random.split(key, 4)
        B, S, H, I = (1, 256, 512, 1792)
        x = jax.random.normal(k1, (B, S, H), dtype=jnp.float32)
        ln_w = jnp.ones((H,), dtype=jnp.float32)
        gate_w = jax.random.normal(k2, (I, H), dtype=jnp.float32) * 0.02
        up_w = jax.random.normal(k3, (I, H), dtype=jnp.float32) * 0.02
        down_w = jax.random.normal(k4, (H, I), dtype=jnp.float32) * 0.02
        return {'x': x, 'ln_w': ln_w, 'gate_w': gate_w, 'up_w': up_w, 'down_w': down_w}
    _L0_ffn_in = _L0_ffn_setup()

    def _L1_attn_setup():
        import math
        import jax, jax.numpy as jnp
        import numpy as np
        NUM_HEADS = 32
        HIDDEN = 512
        HEAD_DIM = HIDDEN // NUM_HEADS
        NEG_INF = -1e+30

        def _alibi_slopes(n: int) -> jnp.ndarray:
            cp2 = 2 ** math.floor(math.log2(n))
            base = 2.0 ** (-2.0 ** (-(math.log2(cp2) - 3)))
            slopes = base ** np.arange(1, cp2 + 1, dtype=np.float64)
            if cp2 != n:
                extra_base = 2.0 ** (-2.0 ** (-(math.log2(2 * cp2) - 3)))
                rem = min(cp2, n - cp2)
                extra = extra_base ** np.arange(1, 1 + 2 * rem, 2, dtype=np.float64)
                slopes = np.concatenate([slopes, extra])
            return jnp.asarray(slopes, dtype=jnp.float32)
        key = jax.random.key(seed)
        k1, k2, k3 = jax.random.split(key, 3)
        B, S = (2, 256)
        hidden_states = jax.random.normal(k1, (B, S, HIDDEN), dtype=jnp.float32)
        Wqkv = jax.random.normal(k2, (HIDDEN, NUM_HEADS * HEAD_DIM + 2 * HEAD_DIM), dtype=jnp.float32) * 0.02
        Wo = jax.random.normal(k3, (HIDDEN, HIDDEN), dtype=jnp.float32) * 0.02
        return {'hidden_states': hidden_states, 'Wqkv': Wqkv, 'Wo': Wo}
    _L1_attn_in = _L1_attn_setup()

    def _L1_ffn_setup():
        import jax, jax.numpy as jnp
        import numpy as np
        N_EXPERTS = 28
        TOP_K = 2
        RANK = 8
        LORA_ALPHA = 16
        SCALING = LORA_ALPHA / RANK
        TEMP = 1.0
        key = jax.random.key(seed)
        ks = jax.random.split(key, 5)
        B, S, D_IN, D_OUT = (4, 256, 512, 512)
        x = jax.random.normal(ks[0], (B, S, D_IN), dtype=jnp.float32)
        base_W = jax.random.normal(ks[1], (D_OUT, D_IN), dtype=jnp.float32) * (1.0 / np.sqrt(D_IN))
        gate_W = jax.random.normal(ks[2], (N_EXPERTS, D_IN), dtype=jnp.float32) * (1.0 / np.sqrt(D_IN))
        lora_A = jax.random.normal(ks[3], (N_EXPERTS, RANK, D_IN), dtype=jnp.float32) * (1.0 / np.sqrt(D_IN))
        lora_B = jax.random.normal(ks[4], (N_EXPERTS, D_OUT, RANK), dtype=jnp.float32) * 0.01
        return {'x': x, 'base_W': base_W, 'gate_W': gate_W, 'lora_A': lora_A, 'lora_B': lora_B}
    _L1_ffn_in = _L1_ffn_setup()
    _d = {'L0_attn_hidden_states': _L0_attn_in['hidden_states'], 'L0_attn_Wq': _L0_attn_in['Wq'], 'L0_attn_bq': _L0_attn_in['bq'], 'L0_attn_Wk': _L0_attn_in['Wk'], 'L0_attn_bk': _L0_attn_in['bk'], 'L0_attn_Wv': _L0_attn_in['Wv'], 'L0_attn_bv': _L0_attn_in['bv'], 'L0_attn_Wo': _L0_attn_in['Wo'], 'L0_attn_M': _L0_attn_in['M'], 'L0_attn_z': _L0_attn_in['z'], 'L0_ffn_ln_w': _L0_ffn_in['ln_w'], 'L0_ffn_gate_w': _L0_ffn_in['gate_w'], 'L0_ffn_up_w': _L0_ffn_in['up_w'], 'L0_ffn_down_w': _L0_ffn_in['down_w'], 'L1_attn_Wqkv': _L1_attn_in['Wqkv'], 'L1_attn_Wo': _L1_attn_in['Wo'], 'L1_ffn_base_W': _L1_ffn_in['base_W'], 'L1_ffn_gate_W': _L1_ffn_in['gate_W'], 'L1_ffn_lora_A': _L1_ffn_in['lora_A'], 'L1_ffn_lora_B': _L1_ffn_in['lora_B']}
    _x0 = _d['L0_attn_hidden_states']
    _d['L0_attn_hidden_states'] = jax.random.normal(jax.random.fold_in(jax.random.key(seed), 1), (1, 1024, 512), dtype=_x0.dtype)
    del _x0
    return _d

def reference(L0_attn_hidden_states, L0_attn_Wq, L0_attn_bq, L0_attn_Wk, L0_attn_bk, L0_attn_Wv, L0_attn_bv, L0_attn_Wo, L0_attn_M, L0_attn_z, L0_ffn_ln_w, L0_ffn_gate_w, L0_ffn_up_w, L0_ffn_down_w, L1_attn_Wqkv, L1_attn_Wo, L1_ffn_base_W, L1_ffn_gate_W, L1_ffn_lora_A, L1_ffn_lora_B):

    def _L0_attn_ref(hidden_states, Wq, bq, Wk, bk, Wv, bv, Wo, M, z):
        import jax, jax.numpy as jnp
        import numpy as np
        B, S, HID = (2, 512, 512)
        H, HKV, D = (32, 8, 128)
        G = H // HKV
        EPS = 1e-06

        def _reference_tuple_inner(hidden_states, Wq, bq, Wk, bk, Wv, bv, Wo, M, z):
            b, s, _ = hidden_states.shape
            q = (hidden_states @ Wq.T + bq).reshape(b, s, H, D)
            k = (hidden_states @ Wk.T + bk).reshape(b, s, HKV, D)
            v = (hidden_states @ Wv.T + bv).reshape(b, s, HKV, D)
            sig_q = jax.nn.elu(q) + 1.0
            sig_k = jax.nn.elu(k) + 1.0
            q_sel = sig_q[:, :, ::G, :]
            num = jnp.einsum('bshd,hde->bshe', q_sel, M)
            den = jnp.einsum('bshd,hd->bsh', q_sel, z)[..., None] + EPS
            retrieved = num / den
            out_heads = jnp.repeat(retrieved, G, axis=2)
            output = out_heads.reshape(b, s, H * D) @ Wo.T
            M_new = M + jnp.einsum('bshd,bshe->hde', sig_k, v)
            z_new = z + sig_k.sum(axis=(0, 1))
            return (output, M_new, z_new)
        return _reference_tuple_inner(hidden_states, Wq, bq, Wk, bk, Wv, bv, Wo, M, z)[0]

    def _L0_ffn_ref(x, ln_w, gate_w, up_w, down_w):
        import jax, jax.numpy as jnp
        import numpy as np
        RMS_EPS = 1e-05
        var = jnp.mean(jnp.square(x), axis=-1, keepdims=True)
        nx = x * jax.lax.rsqrt(var + RMS_EPS) * ln_w
        g = jnp.einsum('bsh,ih->bsi', nx, gate_w)
        u = jnp.einsum('bsh,ih->bsi', nx, up_w)
        return jnp.einsum('bsi,hi->bsh', jax.nn.silu(g) * u, down_w)

    def _L1_attn_ref(hidden_states, Wqkv, Wo):
        import math
        import jax, jax.numpy as jnp
        import numpy as np
        NUM_HEADS = 32
        HIDDEN = 512
        HEAD_DIM = HIDDEN // NUM_HEADS
        NEG_INF = -1e+30

        def _alibi_slopes(n: int) -> jnp.ndarray:
            cp2 = 2 ** math.floor(math.log2(n))
            base = 2.0 ** (-2.0 ** (-(math.log2(cp2) - 3)))
            slopes = base ** np.arange(1, cp2 + 1, dtype=np.float64)
            if cp2 != n:
                extra_base = 2.0 ** (-2.0 ** (-(math.log2(2 * cp2) - 3)))
                rem = min(cp2, n - cp2)
                extra = extra_base ** np.arange(1, 1 + 2 * rem, 2, dtype=np.float64)
                slopes = np.concatenate([slopes, extra])
            return jnp.asarray(slopes, dtype=jnp.float32)
        B, S, H = hidden_states.shape
        nH, d = (NUM_HEADS, HEAD_DIM)
        scale = d ** (-0.5)
        qkv = hidden_states @ Wqkv
        q = qkv[..., :nH * d].reshape(B, S, nH, d)
        k = qkv[..., nH * d:nH * d + d]
        v = qkv[..., nH * d + d:]
        scores = jnp.einsum('bqhd,bkd->bhqk', q, k) * scale
        pos_q = jnp.arange(S)[:, None]
        pos_k = jnp.arange(S)[None, :]
        slopes = _alibi_slopes(nH)
        alibi = slopes[:, None, None] * (pos_k - pos_q).astype(jnp.float32)
        causal = pos_k <= pos_q
        scores = jnp.where(causal[None, None], scores + alibi[None], NEG_INF)
        probs = jax.nn.softmax(scores, axis=-1)
        attn = jnp.einsum('bhqk,bkd->bqhd', probs, v).reshape(B, S, H)
        return attn @ Wo

    def _L1_ffn_ref(x, base_W, gate_W, lora_A, lora_B):
        import jax, jax.numpy as jnp
        import numpy as np
        N_EXPERTS = 28
        TOP_K = 2
        RANK = 8
        LORA_ALPHA = 16
        SCALING = LORA_ALPHA / RANK
        TEMP = 1.0
        B, S, D_in = x.shape
        xf = x.reshape(B * S, D_in)
        base = xf @ base_W.T
        logits = xf @ gate_W.T
        top_vals, top_idx = jax.lax.top_k(logits, TOP_K)
        top_probs = jax.nn.softmax(top_vals / TEMP, axis=-1)
        N = xf.shape[0]
        gate_full = jnp.zeros((N, N_EXPERTS), dtype=xf.dtype).at[jnp.arange(N)[:, None], top_idx].add(top_probs)
        h = jnp.einsum('nd,erd->ner', xf, lora_A)
        h = h * (gate_full * SCALING)[:, :, None]
        lora_out = jnp.einsum('ner,eor->no', h, lora_B)
        out = base + lora_out
        return out.reshape(B, S, -1)
    x = L0_attn_hidden_states
    x = x + _layernorm(_L0_attn_ref(_layernorm(x, axis=-1), L0_attn_Wq, L0_attn_bq, L0_attn_Wk, L0_attn_bk, L0_attn_Wv, L0_attn_bv, L0_attn_Wo, L0_attn_M, L0_attn_z), axis=-1)
    x = x + _layernorm(_L0_ffn_ref(_layernorm(x, axis=-1), L0_ffn_ln_w, L0_ffn_gate_w, L0_ffn_up_w, L0_ffn_down_w), axis=-1)
    x = x + _layernorm(_L1_attn_ref(_layernorm(x, axis=-1), L1_attn_Wqkv, L1_attn_Wo), axis=-1)
    x = x + _layernorm(_L1_ffn_ref(_layernorm(x, axis=-1), L1_ffn_base_W, L1_ffn_gate_W, L1_ffn_lora_A, L1_ffn_lora_B), axis=-1)
    return x

_drawn_inputs = setup_inputs


def setup_inputs(seed=0):
    import zlib

    import numpy as np

    out = dict(_drawn_inputs(seed))
    spreads = {'L0_attn_bq': (0.0, 0.1),
     'L0_attn_bk': (0.0, 0.1),
     'L0_attn_bv': (0.0, 0.1),
     'L0_ffn_ln_w': (1.0, 0.2)}
    factors = {'L1_ffn_gate_W': 3.06, 'L1_ffn_lora_A': 2.884, 'L1_ffn_lora_B': 3.004}
    for name, (base, spread) in spreads.items():
        noise = np.random.default_rng([zlib.crc32(name.encode()), seed]).standard_normal(out[name].shape)
        drawn = base * np.exp(spread * noise) if base else spread * noise
        out[name] = jnp.asarray(drawn.astype(out[name].dtype))
    for name, factor in factors.items():
        out[name] = (out[name] * factor).astype(out[name].dtype)
    return out
```

```python
from contextlib import ExitStack

import numpy as np

import concourse.bass as bass
from concourse import mybir

F32 = mybir.dt.float32
F32R = mybir.dt.float32r
BF16 = mybir.dt.bfloat16
U32 = mybir.dt.uint32
ALU = mybir.AluOpType
ACT = mybir.ActivationFunctionType
X = mybir.AxisListType.X

P = 128
S = 1024
HID = 512
NT = S // P
KC = HID // P
BANK = 512
LN_EPS = 1e-5
H0, D0, G0 = 8, 128, 4
DEN_EPS = 1e-6
INNER = 1792
NJ = INNER // P
RMS_EPS = 1e-5
HALF = 4
WCH = 2 * KC * P + HID
GW, UW, DW = 0, KC * P, 2 * KC * P
RAW_BUFS = 3
WBUFS = 3
H1, D1 = 32, 16
PAIRS = H1 // 2
SCALE = float(D1) ** -0.5
STK = 64
BIAS_ROWS = 6
QHI, QLO = BIAS_ROWS, BIAS_ROWS + 2 * D1
VW = 32
S2_BUFS, P_BUFS = 3, 12
NE, RANK, SCALING = 28, 8, 2.0
ER = NE * RANK
LG = NE + ER

PHASES = 4


def split12(v):
    v = np.asarray(v, np.float32)
    hi = ((v.view(np.uint32) + np.uint32(0x800)) & np.uint32(0xFFFFF000)).view(np.float32)
    return hi, (v - hi).astype(np.float32)


def constants():
    slopes = ((2.0 ** (-(2.0 ** -2.0))) ** np.arange(1, H1 + 1, dtype=np.float64)).astype(np.float32)
    s_hi, s_lo = split12(slopes)
    pos = np.arange(S, dtype=np.float32)
    a_hi, a_lo = split12(-(s_hi[None, :] * pos[:, None]))
    w0 = -(s_lo[None, :] * pos[:, None])
    b_hi, b_lo = split12(w0)
    one = np.ones((S, 1), np.float32)
    q_bias = np.stack([one * s_hi, a_hi, a_lo, one * s_lo, b_hi, b_lo], -1)
    q_bias = q_bias.reshape(NT, P, H1 * BIAS_ROWS).transpose(1, 0, 2)
    k_bias = np.stack([pos, one[:, 0], one[:, 0], pos, one[:, 0], one[:, 0]], -1)
    k_bias = k_bias.reshape(NT, P, BIAS_ROWS).transpose(1, 0, 2)
    w0 = w0.reshape(NT, P, PAIRS, 2).transpose(1, 0, 3, 2)
    c = np.arange(P)
    later = np.where(c[None, :] > c[:, None], np.float32(-1e30), np.float32(0))
    masks = np.stack([np.eye(P, dtype=np.float32), later, later.T])
    return {
        "c_ident": np.eye(P, dtype=np.float32),
        "c_masks": masks.transpose(1, 0, 2),
        "c_qbias": q_bias,
        "c_kbias": k_bias,
        "c_w0": w0,
        "c_iota": np.tile(np.arange(NE, dtype=np.float32), (P, 1)),
    }


def score_pieces(t):
    kw = (t + 1) * P
    out = []
    if kw <= BANK:
        n = BANK // kw
        for j in range(0, PAIRS, n):
            out += [(p, j, n, 0, kw, 0) for p in range(2)]
    else:
        rest = kw - BANK
        n = BANK // rest
        for j in range(0, PAIRS, n):
            out += [(p, j + i, 1, 0, BANK, 0) for i in range(n) for p in range(2)]
            out += [(p, j, n, BANK, rest, 1) for p in range(2)]
    return out


def attention_slots():
    slots = []
    for t in range(NT):
        items = len(score_pieces(t + 1)) + 1 if t + 1 < NT else 0
        span = 8 * max(t, 1)
        done = 0
        n = 0
        for kb in range(t + 1):
            for p in range(2):
                after = []
                for g in range(4):
                    n += 1
                    upto = min(items, -(-items * n // span))
                    after.append(list(range(done, upto)))
                    done = upto
                slots.append([t, kb, p, after, []])
        assert done == items
    at = 0
    for t in range(NT):
        end = (t + 1) * (t + 2) - 1
        for step in range(4):
            at = max(at + 1, end + 2)
            while at >= len(slots):
                slots.append([None, None, None, [[], [], [], []], []])
            slots[at][4].append((t, step))
    return slots


def build(nc, A, out):
    ctx = ExitStack()
    with ctx:
        def sb(name, shape, dt=F32):
            return ctx.enter_context(nc.sbuf_tensor(name, shape, dt))

        def sem(name):
            return ctx.enter_context(nc.semaphore(name))

        def sems(name, n):
            return [sem(f"{name}{i}") for i in range(n)]

        x = sb("x", [P, NT, HID])
        nx = sb("nx", [P, 2, 2, HID])
        nt_hi = sb("nt_hi", [P, 2, KC, P], F32R)
        nt_lo = sb("nt_lo", [P, 2, KC, P], F32R)
        delta = sb("delta", [P, 2, HID])
        lnw = sb("lnw", [P, HID])
        ident = sb("ident", [P, P])
        masks = sb("masks", [P, 3, P], BF16)
        w0 = sb("w0", [P, NT, 2, PAIRS])
        kbias = sb("kbias", [P, NT, BIAS_ROWS])
        iota = sb("iota", [P, NE])
        bn = sb("bn", [P, 2, PHASES * NT, 6])
        mv = sb("mv", [P, 2, PHASES * NT, 2])
        ve = sb("ve", [P, 2, PHASES * NT])
        rstd = sb("rstd", [P, 2, PHASES * NT])
        rms = sb("rms", [P, NT, 4])
        mhalf = sb("mhalf", [P, 1])
        den = sb("den", [P, NT, 3, H0])
        rowmax = sb("rowmax", [P, 2, 2, 2, PAIRS])
        wshift = sb("wshift", [P, 2, 2, 2, PAIRS])
        shift = sb("shift", [P, 2, 2, 2, PAIRS])
        shift_t = sb("shift_t", [STK, 2, P], F32R)
        rsum = sb("rsum", [P, 2, 2, PAIRS])
        top = sb("top", [P, NT, 8])
        topi = sb("topi", [P, NT, 8], U32)
        prob = sb("prob", [P, NT, 8])
        gate = sb("gate", [P, 2, 3, NE])
        logit = sb("logit", [P, 2, NE])

        kib = 1024
        b_at = nc.sbuf_base
        c_at = b_at + 32 * kib + 512
        room = 158 * kib + 512
        sb("arena", [P, room // 4])

        def at(name, start, kb, shape, dt=F32):
            size = int(np.prod(shape[1:])) * mybir.dt.size(dt)
            assert start + int(kb * kib) + size <= b_at + room, (name, start + kb * kib + size - b_at - room)
            return nc.alloc_sbuf_tensor_at(name, shape, dt, offset=start + int(kb * kib))

        mt_hi = at("mt_hi", b_at, 0, [P, KC, S], F32R)
        mt_lo = at("mt_lo", b_at, 16, [P, KC, S], F32R)
        we_hi = at("we_hi", b_at, 0, [P, KC, HID + LG], F32R)
        we_lo = at("we_lo", b_at, 12, [P, KC, HID + LG], F32R)
        lb_hi = at("lb_hi", b_at, 24, [ER // 2, 2, HID], F32R)
        lb_lo = at("lb_lo", b_at, 28, [ER // 2, 2, HID], F32R)
        wq_hi = at("wq_hi", c_at, 0, [P, KC, H0 * D0], F32R)
        wq_lo = at("wq_lo", c_at, 16, [P, KC, H0 * D0], F32R)
        wo0_raw = at("wo0_raw", c_at, 32, [P, G0, HID])
        m_raw = at("m_raw", c_at, 40, [P, H0, D0])
        m_hi = at("m_hi", c_at, 44, [P, H0, D0], F32R)
        m_lo = at("m_lo", c_at, 48, [P, H0, D0], F32R)
        wsum = at("wsum", c_at, 52, [P, HID])
        wsum_hi = at("wsum_hi", c_at, 54, [P, HID], F32R)
        wsum_lo = at("wsum_lo", c_at, 56, [P, HID], F32R)
        bq_b = at("bq_b", c_at, 58, [P, H0 * D0])
        z_b = at("z_b", c_at, 62, [P, H0 * D0])
        q0 = at("q0", c_at, 66, [P, H0 * D0])
        e0 = at("e0", c_at, 70, [P, H0 * D0])
        sig = at("sig", c_at, 74, [P, 2, H0 * D0])
        prod = at("prod", c_at, 82, [P, H0 * D0])
        sigt_hi = at("sigt_hi", c_at, 86, [P, H0, P], F32R)
        sigt_lo = at("sigt_lo", c_at, 90, [P, H0, P], F32R)
        mw_hi = at("mw_hi", c_at, 94, [P, H0, HID], F32R)
        mw_lo = at("mw_lo", c_at, 110, [P, H0, HID], F32R)
        wq_raw = at("wq_raw", c_at, 110, [P, KC, H0 * D0])
        mask_raw = at("mask_raw", c_at, 94, [P, 3, P])
        wf_hi = at("wf_hi", c_at, 0, [P, WBUFS, WCH], F32R)
        wf_lo = at("wf_lo", c_at, 18, [P, WBUFS, WCH], F32R)
        wf_raw = at("wf_raw", c_at, 36, [P, RAW_BUFS, WCH])
        silu = at("silu", c_at, 58, [P, 2, HALF * P])
        hid = at("hid", c_at, 62, [P, 2, HALF * P])
        hid_hi = at("hid_hi", c_at, 66, [P, 2, HALF * P], F32R)
        hid_lo = at("hid_lo", c_at, 70, [P, 2, HALF * P], F32R)
        wkv_raw = at("wkv_raw", c_at, 80, [P, KC, HID + 2 * D1])
        wkv_hi = at("wkv_hi", c_at, 89, [P, KC, HID + 2 * D1], F32R)
        wkv_lo = at("wkv_lo", c_at, 97.5, [P, KC, HID + 2 * D1], F32R)
        qbias = at("qbias", c_at, 74, [P, NT, H1, BIAS_ROWS])
        qs = at("qs", c_at, 106, [P, 2, H1, STK], F32R)
        qt = at("qt", c_at, 0, [P, PAIRS, S], F32R)
        kt = at("kt", c_at, 64, [P, S], F32R)
        vals = at("vals", c_at, 68, [P, NT, VW])
        ks = at("ks", c_at, 69, [P, 2, 2, STK], F32R)
        wo1_raw = at("wo1_raw", c_at, 72, [P, KC, HID])
        wo1_hi = at("wo1_hi", c_at, 80, [P, KC, HID], F32R)
        wo1_lo = at("wo1_lo", c_at, 88, [P, KC, HID], F32R)
        probs = at("probs", c_at, 98, [P, P_BUFS, BANK])
        o_sb = at("o_sb", c_at, 122, [P, 2, BANK])
        we_raw = at("we_raw", c_at, 72, [P, 2, HID + LG])
        lb_raw = at("lb_raw", c_at, 70, [ER // 2, HID])
        hs = at("hs", c_at, 98, [P, 2, ER])
        ht_hi = at("ht_hi", c_at, 102, [ER // 2, 2, 2, P], F32R)
        ht_lo = at("ht_lo", c_at, 106, [ER // 2, 2, 2, P], F32R)
        attn = nx[:, 1, 0, :]
        at_hi, at_lo = nt_hi[:, 0], nt_lo[:, 0]

        psum = ctx.enter_context(nc.psum_tensor("psum", [P, 8, BANK], F32))
        TR = [psum[:, 6, :], psum[:, 7, :]]
        Q0, SIGT, Y0 = psum[:, 0:2, :], psum[:, 2:4, :], [psum[:, 4, :], psum[:, 5, :]]
        Y1, GATE, UP = psum[:, 0:4, :], psum[:, 4, :], psum[:, 5, :]
        QP, KVP, STKT = psum[:, 2, :], psum[:, 3, 0:2 * D1], [psum[:, 4, :], psum[:, 5, :]]
        S1 = [psum[:, 0, :], psum[:, 1, :]]
        S2 = [psum[:, 2, :], psum[:, 3, :], psum[:, 4, :]]
        PV, BG = psum[:, 5:7, :], psum[:, 7, :]
        O3, L3 = [psum[:, b, :] for b in (0, 1, 5)], [psum[:, 2, 0:LG], psum[:, 3, 0:LG]]
        HT = psum[:, 4, 0:2 * P]

        x_in = sems("x_in", NT)
        id_in, mask_in, bz_in, m_in, tab_in, lnw_in = map(sem, ("id_in", "mask_in", "bz_in", "m_in", "tab_in", "lnw_in"))
        wq_in = sems("wq_in", KC)
        wo0_in = sem("wo0_in")
        wf_in = sems("wf_in", RAW_BUFS)
        wkv_in, wo1_in, lb_in = sem("wkv_in"), sem("wo1_in"), sem("lb_in")
        we_in = sems("we_in", 2)
        pre_var, pre_rstd, nx_ready, tr_done, nt_hi_ready, nt_ready = (
            sems(n, PHASES) for n in ("pre_var", "pre_rstd", "nx_ready", "tr_done", "nt_hi_ready", "nt_ready"))
        nx_unscaled = sem("nx_unscaled")
        y_done, post_var, post_rstd, delta_ready, x_ready = (
            sems(n, PHASES) for n in ("y_done", "post_var", "post_rstd", "delta_ready", "x_ready"))
        dve_step, act_step, pool_step = sem("dve_step"), sem("act_step"), sem("pool_step")
        mask_ready, mhalf_ready = sem("mask_ready"), sem("mhalf_ready")
        wq_hi_ready, wq_ready, m_hi_ready, m_ready = map(sem, ("wq_hi_ready", "wq_ready", "m_hi_ready", "m_ready"))
        wsum_ready, wsum_hi_ready, wsum_lo_ready, mw_done, mw_hi_ready, mw_ready = map(
            sem, ("wsum_ready", "wsum_hi_ready", "wsum_lo_ready", "mw_done", "mw_hi_ready", "mw_ready"))
        q0_done, q0_min, q0_exp, sig_ready, prod_ready, den_ready, sig_scaled = map(
            sem, ("q0_done", "q0_min", "q0_exp", "sig_ready", "prod_ready", "den_ready", "sig_scaled"))
        sigt_done, sigt_hi_ready, sigt_ready = map(sem, ("sigt_done", "sigt_hi_ready", "sigt_ready"))
        wf_hi_ready, wf_ready, g_done, u_done, silu_ready, hid_f_ready, hid_hi_ready, hid_ready, down_done = map(
            sem, ("wf_hi_ready", "wf_ready", "g_done", "u_done", "silu_ready", "hid_f_ready", "hid_hi_ready",
                  "hid_ready", "down_done"))
        wkv_hi_ready, wkv_ready, wo1_hi_ready, wo1_ready = map(
            sem, ("wkv_hi_ready", "wkv_ready", "wo1_hi_ready", "wo1_ready"))
        qkv_done, q_hi_ready, k_hi_ready, v_ready, qs_ready, ks_ready, pads_ready, qs_bias = map(
            sem, ("qkv_done", "q_hi_ready", "k_hi_ready", "v_ready", "qs_ready", "ks_ready", "pads_ready", "qs_bias"))
        ktr_done, kt_ready, qtr_done, qt_act, qt_dve = map(sem, ("ktr_done", "kt_ready", "qtr_done", "qt_act", "qt_dve"))
        s1_done, s1_read, shift_ready, shift_t_ready = map(sem, ("s1_done", "s1_read", "shift_ready", "shift_t_ready"))
        shift_in = sems("shift_in", 2)
        s2_done, p_ready, pv_done, o_read = map(sem, ("s2_done", "p_ready", "pv_done", "o_read"))
        bg_o, bg_o_read, bg_a, at_hi_ready, bg_a_read = map(sem, ("bg_o", "bg_o_read", "bg_a", "at_hi_ready", "bg_a_read"))
        we_hi_ready, we_ready, lb_hi_ready, lb_ready = map(sem, ("we_hi_ready", "we_ready", "lb_hi_ready", "lb_ready"))
        l3_done, gap_ready, gap_exp, hs_ready, ht_done, ht_hi_ready, ht_ready = map(
            sem, ("l3_done", "gap_ready", "gap_exp", "hs_ready", "ht_done", "ht_hi_ready", "ht_ready"))
        out_sem = sem("out_sem")

        slots = attention_slots()
        pieces = [score_pieces(t) for t in range(NT)]
        s1_base = [sum(len(pieces[u]) + 1 for u in range(t)) for t in range(NT)]
        batch_base = [t * (t + 1) for t in range(NT)]

        def cols(t):
            return slice(t * P, (t + 1) * P)

        def tile_transpose(p, t):
            if p == 1:
                return mt_hi[:, :, cols(t)], mt_lo[:, :, cols(t)]
            return nt_hi[:, t % 2], nt_lo[:, t % 2]

        def f32(ap):
            return ap.bitcast(F32)

        block = ctx.enter_context(nc.Block())

        @block.sync
        def _(sp):
            sp.dma_start(x[:, 0, :], A["x"][0, 0:P, :]).then_inc(x_in[0], 16)
            sp.dma_start(ident[:], A["c_ident"]).then_inc(id_in, 16)
            sp.dma_start(mask_raw[:], A["c_masks"]).then_inc(mask_in, 16)
            for k in range(KC):
                sp.dma_start(wq_raw[:, k, :], A["wq"][:, k, :]).then_inc(wq_in[k], 16)
            sp.dma_start(bq_b[:], A["bq"].broadcast_to([P, H0 * D0])).then_inc(bz_in, 16)
            sp.dma_start(z_b[:], A["z"].broadcast_to([P, H0 * D0])).then_inc(bz_in, 16)
            sp.dma_start(x[:, 1, :], A["x"][0, P:2 * P, :]).then_inc(x_in[1], 16)
            sp.dma_start(m_raw[:], A["m"]).then_inc(m_in, 16)
            sp.dma_start(lnw[:], A["lnw"].broadcast_to([P, HID])).then_inc(lnw_in, 16)
            for h in range(H0):
                if h < NT - 2:
                    sp.dma_start(x[:, h + 2, :], A["x"][0, (h + 2) * P:(h + 3) * P, :]).then_inc(x_in[h + 2], 16)
                if h:
                    sp.wait_ge(wsum_ready, h)
                sp.dma_start(wo0_raw[:], A["wo0"][h].rearrange("p (g n) -> p g n", g=G0)).then_inc(wo0_in, 16)
            sp.dma_start(kbias[:], A["c_kbias"]).then_inc(tab_in, 16)
            sp.dma_start(w0[:], A["c_w0"]).then_inc(tab_in, 16)
            sp.dma_start(iota[:], A["c_iota"]).then_inc(tab_in, 16)
            for c in range(2 * NJ):
                if c == 0:
                    sp.wait_ge(mw_ready, H0)
                    sp.wait_ge(wsum_lo_ready, H0)
                if c >= RAW_BUFS:
                    sp.wait_ge(wf_ready, c - RAW_BUFS + 1)
                sp.dma_start(wf_raw[:, c % RAW_BUFS, :], A["wf"][c % NJ]).then_inc(wf_in[c % RAW_BUFS], 16)
                if c == 4:
                    sp.wait_ge(y_done[0], NT)
                    sp.dma_start(wkv_raw[:], A["wkv"]).then_inc(wkv_in, 16)
                    sp.dma_start(qbias[:].rearrange("p t h b -> p t (h b)"), A["c_qbias"]).then_inc(tab_in, 16)
            sp.wait_ge(qs_bias, 2 * NT)
            sp.dma_start(wo1_raw[:], A["wo1"]).then_inc(wo1_in, 16)
            for t in range(NT):
                sp.wait_ge(shift_t_ready, t + 1)
                for p in range(2):
                    for part in range(2):
                        row = STK * p + BIAS_ROWS - 2 + part
                        src = (2 * p + part) * PAIRS
                        sp.dma_start(f32(qt[row:row + 1, :, cols(t)]), f32(shift_t[src:src + PAIRS, t % 2, :]))\
                          .then_inc(shift_in[t % 2], 16)
                if t == 1:
                    sp.wait_ge(wo1_ready, 1)
                    for k in range(2):
                        sp.dma_start(we_raw[:, k, :], A["we"][k]).then_inc(we_in[k], 16)
                if t == 6:
                    sp.wait_ge(we_ready, 2)
                    for k in range(2):
                        sp.dma_start(we_raw[:, k, :], A["we"][k + 2]).then_inc(we_in[k], 16)
                    sp.dma_start(lb_raw[:], A["lb"][:, 0, :]).then_inc(lb_in, 16)
            sp.wait_ge(lb_ready, 1)
            sp.dma_start(lb_raw[:], A["lb"][:, 1, :]).then_inc(lb_in, 16)
            for t in range(NT):
                sp.wait_ge(x_ready[3], t + 1)
                sp.dma_start(out[0, cols(t), :], x[:, t, :]).then_inc(out_sem, 16)
            sp.wait_ge(out_sem, 16 * NT)

        @block.vector
        def _(dve):
            steps = [0]

            def link(ins):
                steps[0] += 1
                ins.then_inc(dve_step, 1)
                dve.wait_ge(dve_step, steps[0])

            def stats(kind, i, src, ready):
                link(dve.bn_stats(bn[:, kind, i, :], src))
                link(dve.bn_aggr(mv[:, kind, i, :], bn[:, kind, i, :]))
                dve.tensor_scalar(ve[:, kind, i:i + 1], mv[:, kind, i, 1:2], LN_EPS, None, ALU.add).then_inc(ready, 1)

            def pre_stats(p, t):
                if p == 0:
                    dve.wait_ge(x_in[t], 16)
                else:
                    dve.wait_ge(x_ready[p - 1], t + 1)
                stats(0, p * NT + t, x[:, t, :], pre_var[p])

            def pre_norm(p, t):
                i = p * NT + t
                dve.wait_ge(pre_rstd[p], t + 1)
                if t >= 2:
                    dve.wait_ge(tr_done[p], t - 1)
                dve.tensor_scalar(nx[:, p % 2, t % 2, :], x[:, t, :], mv[:, 0, i, 0:1], rstd[:, 0, i:i + 1],
                                  ALU.subtract, ALU.mult).then_inc(nx_unscaled if p == 1 else nx_ready[p], 1)

            def pre_lo(p, t):
                hi, lo = tile_transpose(p, t)
                dve.wait_ge(nt_hi_ready[p], t + 1)
                dve.tensor_tensor(lo, TR[p % 2].rearrange("p (k n) -> p k n", k=KC), f32(hi), ALU.subtract)\
                   .then_inc(nt_ready[p], 1)

            def post_stats(p, t, y):
                dve.wait_ge(y_done[p], t + 1 if p != 1 else t // HALF + 1)
                stats(1, p * NT + t, y, post_var[p])

            def post_apply(p, t, y):
                i = p * NT + t
                dve.wait_ge(post_rstd[p], t + 1)
                if t >= 2:
                    dve.wait_ge(x_ready[p], t - 1)
                dve.tensor_scalar(delta[:, t % 2, :], y, mv[:, 1, i, 0:1], rstd[:, 1, i:i + 1],
                                  ALU.subtract, ALU.mult).then_inc(delta_ready[p], 1)

            def wq_low(k):
                dve.wait_ge(wq_hi_ready, k + 1)
                dve.tensor_tensor(wq_lo[:, k, :], wq_raw[:, k, :], f32(wq_hi[:, k, :]), ALU.subtract)\
                   .then_inc(wq_ready, 1)

            def wo_sum(h):
                dve.wait_ge(wo0_in, 16 * (h + 1))
                if h:
                    dve.wait_ge(wsum_lo_ready, h)
                dve.tensor_reduce(wsum[:], wo0_raw[:].rearrange("p g n -> p n g"), X, ALU.add)\
                   .then_inc(wsum_ready, 1)
                dve.wait_ge(wsum_hi_ready, h + 1)
                if h:
                    dve.wait_ge(mw_done, h)
                dve.tensor_tensor(wsum_lo[:], wsum[:], f32(wsum_hi[:]), ALU.subtract).then_inc(wsum_lo_ready, 1)

            def mw_low(h):
                dve.wait_ge(mw_hi_ready, h + 1)
                dve.tensor_tensor(mw_lo[:, h, :], Y0[h % 2], f32(mw_hi[:, h, :]), ALU.subtract).then_inc(mw_ready, 1)

            def q_bias(t):
                dve.wait_ge(q0_done, t + 1)
                if t == 0:
                    dve.wait_ge(bz_in, 32)
                if t:
                    dve.wait_ge(sig_ready, t)
                link(dve.tensor_tensor(q0[:], Q0.rearrange("p a n -> p (a n)"), bq_b[:], ALU.add))
                dve.tensor_scalar(e0[:], q0[:], 0.0, None, ALU.min).then_inc(q0_min, 1)

            def sigma(t):
                dve.wait_ge(q0_exp, t + 1)
                if t >= 2:
                    dve.wait_ge(sigt_done, t - 1)
                dve.scalar_tensor_tensor(sig[:, t % 2, :], q0[:], 0.0, e0[:], ALU.max, ALU.add).then_inc(sig_ready, 1)

            def denominator(t):
                dve.wait_ge(prod_ready, t + 1)
                link(dve.tensor_reduce(den[:, t, 0, :], prod[:].rearrange("p (h d) -> p h d", h=H0), X, ALU.add))
                link(dve.tensor_scalar(den[:, t, 1, :], den[:, t, 0, :], DEN_EPS, None, ALU.add))
                dve.reciprocal(den[:, t, 2, :], den[:, t, 1, :]).then_inc(den_ready, 1)

            def sig_low(t):
                dve.wait_ge(sigt_hi_ready, t + 1)
                dve.tensor_tensor(sigt_lo[:], SIGT.rearrange("p a (h n) -> p (a h) n", h=H0 // 2), f32(sigt_hi[:]),
                                  ALU.subtract).then_inc(sigt_ready, 1)

            dve.wait_ge(mask_in, 16)
            dve.tensor_copy(masks[:], mask_raw[:]).then_inc(mask_ready, 1)
            pre_stats(0, 0)
            pre_norm(0, 0)
            for k in range(KC):
                wq_low(k)
            pre_lo(0, 0)
            dve.wait_ge(m_hi_ready, 1)
            dve.tensor_tensor(m_lo[:], m_raw[:], f32(m_hi[:]), ALU.subtract).then_inc(m_ready, 1)
            for i in range(NT + 2):
                if i + 1 < NT:
                    pre_stats(0, i + 1)
                if i < NT:
                    q_bias(i)
                if i + 1 < NT:
                    pre_norm(0, i + 1)
                if i < NT:
                    sigma(i)
                if i + 1 < NT:
                    pre_lo(0, i + 1)
                if i < 2:
                    for h in range(H0 // 2 * i, H0 // 2 * (i + 1)):
                        wo_sum(h)
                        mw_low(h)
                if i >= 3:
                    post_stats(0, i - 3, Y0[(i - 3) % 2])
                if i < NT:
                    denominator(i)
                if i >= 3:
                    post_apply(0, i - 3, Y0[(i - 3) % 2])
                if i >= 4:
                    pre_stats(1, i - 4)
                if 1 <= i <= NT:
                    sig_low(i - 1)
                if i >= 4:
                    pre_norm(1, i - 4)
                    pre_lo(1, i - 4)
            post_stats(0, NT - 1, Y0[(NT - 1) % 2])
            post_apply(0, NT - 1, Y0[(NT - 1) % 2])

            def hidden(c):
                dve.wait_ge(silu_ready, c + 1)
                dve.wait_ge(u_done, c + 1)
                if c >= 2:
                    dve.wait_ge(hid_ready, c - 1)
                dve.tensor_tensor(hid[:, c % 2, :], silu[:, c % 2, :], UP, ALU.mult).then_inc(hid_f_ready, 1)

            def hidden_low(c):
                dve.wait_ge(hid_hi_ready, c + 1)
                dve.tensor_tensor(hid_lo[:, c % 2, :], hid[:, c % 2, :], f32(hid_hi[:, c % 2, :]), ALU.subtract)\
                   .then_inc(hid_ready, 1)

            def y1(t):
                return Y1[:, t % HALF, :]

            for c in range(2 * NJ):
                hidden(c)
                if c == NJ:
                    for t in range(HALF):
                        post_stats(1, t, y1(t))
                    for t in range(HALF):
                        post_apply(1, t, y1(t))
                if c < 2:
                    pre_stats(1, NT - 2 + c)
                    pre_norm(1, NT - 2 + c)
                if NJ + 1 <= c < NJ + 3:
                    pre_stats(2, c - NJ - 1)
                    pre_norm(2, c - NJ - 1)
                hidden_low(c)
                if c < 2:
                    pre_lo(1, NT - 2 + c)
                if NJ + 1 <= c < NJ + 3:
                    pre_lo(2, c - NJ - 1)
            for t in range(HALF, NT):
                post_stats(1, t, y1(t))
            for t in range(HALF, NT):
                post_apply(1, t, y1(t))

            def q_low(t):
                dve.wait_ge(q_hi_ready, t + 1)
                s = qs[:, t % 2, :, :]
                dve.scalar_tensor_tensor(s[:, :, QLO:QLO + D1], QP.rearrange("p (h d) -> p h d", d=D1), SCALE,
                                         f32(s[:, :, QHI:QHI + D1]), ALU.mult, ALU.subtract).then_inc(qs_ready, 1)

            def k_low(t):
                dve.wait_ge(k_hi_ready, t + 1)
                for r in range(2):
                    ins = dve.tensor_tensor(ks[:, t % 2, r, QHI + D1:QLO], KVP[:, 0:D1],
                                            f32(ks[:, t % 2, r, QHI:QHI + D1]), ALU.subtract)
                    ins.then_inc(ks_ready, 1)

            def q_turned(t):
                for g in (1, 3):
                    dve.wait_ge(qtr_done, 4 * t + g + 1)
                    dve.tensor_copy(qt[:, 4 * g:4 * g + 4, cols(t)],
                                    STKT[g % 2].rearrange("p (j n) -> p j n", j=4)).then_inc(qt_dve, 1)

            for t in range(NT + 1):
                if t < NT:
                    if t + 2 < NT:
                        pre_stats(2, t + 2)
                        pre_norm(2, t + 2)
                    q_low(t)
                    k_low(t)
                    if t + 2 < NT:
                        pre_lo(2, t + 2)
                if t >= 1:
                    q_turned(t - 1)

            def row_maxima(t, n):
                b = t % 2
                use = s1_base[t] + n
                if n < len(pieces[t]):
                    q, j, nh, k0, kw, part = pieces[t][n]
                    dve.wait_ge(s1_done, use + 1)
                    if n == 0 and t >= 2:
                        dve.wait_ge(shift_ready, t - 1)
                    dve.tensor_reduce(rowmax[:, b, part, q, j:j + nh],
                                      S1[use % 2][:, 0:nh * kw].rearrange("p (h k) -> p h k", h=nh), X, ALU.max)\
                       .then_inc(s1_read, 1)
                    if n < len(pieces[t]) - 1:
                        return
                    dve.wait_ge(s1_read, use + 1)
                    m = rowmax[:, b, 0, :]
                    if (t + 1) * P > BANK:
                        link(dve.tensor_tensor(wshift[:, b, 0, :], rowmax[:, b, 0, :], rowmax[:, b, 1, :], ALU.max))
                        m = wshift[:, b, 0, :]
                    link(dve.tensor_tensor(wshift[:, b, 1, :], w0[:, t, :], m, ALU.subtract))
                    w = wshift[:, b, 1, :]
                    link(dve.tensor_copy(shift[:, b, :, 0, :].bitcast(F32R), w))
                    dve.tensor_tensor(shift[:, b, :, 1, :], w, shift[:, b, :, 0, :], ALU.subtract)\
                       .then_inc(shift_ready, 1)
                else:
                    dve.wait_ge(s1_done, use + 1)
                    if t >= 2:
                        dve.wait_ge(shift_in[b], 64 * (t // 2))
                    dve.tensor_copy(shift_t[:, b, :], S1[use % 2][0:STK, 0:P]).then_inc(s1_read, 1)
                    dve.wait_ge(s1_read, use + 1)
                    dve.sem_inc(shift_t_ready, 1)

            def back(t, step):
                if step < 2:
                    dve.wait_ge(bg_o, 2 * t + step + 1)
                    o = BG.rearrange("p (i g v) -> p i g v", i=4, g=4)
                    r = rsum[:, t % 2, step, :].rearrange("p (i g) -> p i g", i=4)
                    link(dve.reciprocal(r, o[:, :, :, D1]))
                    to = attn.rearrange("p (g i q d) -> p i g q d", g=4, i=4, q=2)[:, :, :, step, :]
                    dve.tensor_tensor(to, o[:, :, :, 0:D1], r.unsqueeze(3).broadcast_to([P, 4, 4, D1]), ALU.mult)\
                       .then_inc(bg_o_read, 1)
                elif step == 2:
                    dve.wait_ge(at_hi_ready, t + 1)
                    dve.tensor_tensor(at_lo, BG.rearrange("p (k n) -> p k n", k=KC), f32(at_hi), ALU.subtract)\
                       .then_inc(bg_a_read, 1)
                else:
                    post_stats(2, t, BG)

            for n in range(len(pieces[0]) + 1):
                row_maxima(0, n)
            for t, kb, p, after, steps_back in slots:
                for items in after:
                    for n in items:
                        row_maxima(t + 1, n)
                for u, step in steps_back:
                    back(u, step)

            def gates(t):
                dve.wait_ge(l3_done, t + 1)
                l = logit[:, t % 2, :]
                link(dve.tensor_copy(l, L3[t % 2][:, 0:NE]))
                link(dve.max(top[:, t, :], l))
                dve.tensor_tensor(prob[:, t, 0:1], top[:, t, 1:2], top[:, t, 0:1], ALU.subtract).then_inc(gap_ready, 1)
                link(dve.max_index(topi[:, t, :], top[:, t, :], l))
                link(dve.tensor_copy(top[:, t, 0:2], topi[:, t, 0:2]))
                dve.wait_ge(gap_exp, t + 1)
                pr = prob[:, t, :]
                link(dve.tensor_scalar(pr[:, 2:3], pr[:, 1:2], 1.0, None, ALU.add))
                link(dve.reciprocal(pr[:, 3:4], pr[:, 2:3]))
                link(dve.tensor_scalar(pr[:, 4:5], pr[:, 3:4], SCALING, None, ALU.mult))
                link(dve.tensor_scalar(pr[:, 5:6], pr[:, 1:2], pr[:, 4:5], None, ALU.mult))
                link(dve.tensor_scalar(gate[:, t % 2, 0, :], iota[:], top[:, t, 0:1], pr[:, 4:5], ALU.is_equal, ALU.mult))
                link(dve.tensor_scalar(gate[:, t % 2, 1, :], iota[:], top[:, t, 1:2], pr[:, 5:6], ALU.is_equal, ALU.mult))
                link(dve.tensor_tensor(gate[:, t % 2, 2, :], gate[:, t % 2, 0, :], gate[:, t % 2, 1, :], ALU.add))
                if t >= 2:
                    dve.wait_ge(ht_done, t - 1)
                dve.tensor_tensor(hs[:, t % 2, :].rearrange("p (e r) -> p e r", e=NE),
                                  L3[t % 2][:, NE:LG].rearrange("p (e r) -> p e r", e=NE),
                                  gate[:, t % 2, 2, :].unsqueeze(2).broadcast_to([P, NE, RANK]), ALU.mult)\
                   .then_inc(hs_ready, 1)

            def h_low(t):
                dve.wait_ge(ht_hi_ready, t + 1)
                dve.tensor_tensor(ht_lo[:, t % 2], HT[0:ER // 2, :].rearrange("p (c n) -> p c n", c=2),
                                  f32(ht_hi[:, t % 2]), ALU.subtract).then_inc(ht_ready, 1)

            for i in range(NT + 2):
                if i < NT:
                    pre_stats(3, i)
                    pre_norm(3, i)
                    pre_lo(3, i)
                if 1 <= i <= NT:
                    gates(i - 1)
                    h_low(i - 1)
                if i >= 2:
                    post_stats(3, i - 2, O3[(i - 2) % 3])
                    post_apply(3, i - 2, O3[(i - 2) % 3])

        @block.scalar
        def _(act):
            def split_hi(dst, src, sem_, scale=1.0):
                act.activation(dst, src, ACT.Copy, scale=scale).then_inc(sem_, 1)

            def pre_hi(p, t):
                hi, _ = tile_transpose(p, t)
                act.wait_ge(tr_done[p], t + 1)
                if p == 0 and t >= 2:
                    act.wait_ge(q0_done, t - 1)
                if p == 2 and t >= 2:
                    act.wait_ge(qkv_done, t - 1)
                if p == 3 and t >= 2:
                    act.wait_ge(l3_done, t - 1)
                split_hi(hi, TR[p % 2].rearrange("p (k n) -> p k n", k=KC), nt_hi_ready[p])

            for k in range(KC):
                act.wait_ge(wq_in[k], 16)
                split_hi(wq_hi[:, k, :], wq_raw[:, k, :], wq_hi_ready)
                if k == 0:
                    pre_hi(0, 0)
            act.wait_ge(m_in, 16)
            split_hi(m_hi[:], m_raw[:], m_hi_ready)

            def q_exp(t):
                act.wait_ge(q0_min, t + 1)
                act.activation(e0[:], e0[:], ACT.Exp).then_inc(q0_exp, 1)

            def sig_high(t):
                act.wait_ge(sigt_done, t + 1)
                if t:
                    act.wait_ge(y_done[0], t)
                split_hi(sigt_hi[:], SIGT.rearrange("p a (h n) -> p (a h) n", h=H0 // 2), sigt_hi_ready)

            for i in range(NT + 2):
                if i < NT:
                    q_exp(i)
                if i + 1 < NT:
                    pre_hi(0, i + 1)
                if i < 2:
                    for h in range(H0 // 2 * i, H0 // 2 * (i + 1)):
                        act.wait_ge(wsum_ready, h + 1)
                        if h:
                            act.wait_ge(mw_done, h)
                        split_hi(wsum_hi[:], wsum[:], wsum_hi_ready)
                        act.wait_ge(mw_done, h + 1)
                        split_hi(mw_hi[:, h, :], Y0[h % 2], mw_hi_ready)
                if 1 <= i <= NT:
                    sig_high(i - 1)
                if i >= 4:
                    pre_hi(1, i - 4)

            def weight_hi(c):
                act.wait_ge(wf_in[c % RAW_BUFS], 16 * (c // RAW_BUFS + 1))
                if c >= WBUFS:
                    act.wait_ge(down_done, c - WBUFS + 1)
                elif c == 0:
                    act.wait_ge(q0_done, NT)
                split_hi(wf_hi[:, c % WBUFS, :], wf_raw[:, c % RAW_BUFS, :], wf_hi_ready)

            weight_hi(0)
            weight_hi(1)
            for c in range(2 * NJ):
                act.wait_ge(g_done, c + 1)
                if c >= 2:
                    act.wait_ge(hid_f_ready, c - 1)
                act.activation(silu[:, c % 2, :], GATE, ACT.Silu).then_inc(silu_ready, 1)
                if c + 2 < 2 * NJ:
                    weight_hi(c + 2)
                act.wait_ge(hid_f_ready, c + 1)
                if c >= 2:
                    act.wait_ge(down_done, c - 1)
                split_hi(hid_hi[:, c % 2, :], hid[:, c % 2, :], hid_hi_ready)
                if c < 2:
                    pre_hi(1, NT - 2 + c)
                if c == 8:
                    act.wait_ge(wkv_in, 16)
                    split_hi(wkv_hi[:], wkv_raw[:], wkv_hi_ready)
                if NJ + 1 <= c < NJ + 3:
                    pre_hi(2, c - NJ - 1)

            for t in range(NT + 1):
                if t < NT:
                    s = qs[:, t % 2, :, :]
                    act.wait_ge(qkv_done, t + 1)
                    if t == 0:
                        act.wait_ge(pads_ready, 3)
                    if t >= 2:
                        act.wait_ge(qtr_done, 4 * (t - 1))
                    q = QP.rearrange("p (h d) -> p h d", d=D1)
                    act.activation(s[:, :, QHI:QHI + 2 * D1].rearrange("p h (r d) -> p h r d", r=2),
                                   q.unsqueeze(2).broadcast_to([P, H1, 2, D1]), ACT.Copy, scale=SCALE)\
                       .then_inc(q_hi_ready, 1)
                    if t >= 2:
                        act.wait_ge(ktr_done, t - 1)
                    kk = ks[:, t % 2, :, :]
                    act.activation(vals[:, t, 0:D1], KVP[:, D1:2 * D1], ACT.Copy).then_inc(v_ready, 1)
                    act.activation(kk[:, :, QHI:QHI + D1], KVP[:, 0:D1].unsqueeze(1).broadcast_to([P, 2, D1]), ACT.Copy)\
                       .then_inc(act_step, 1)
                    act.activation(kk[:, :, QLO:QLO + D1], KVP[:, 0:D1].unsqueeze(1).broadcast_to([P, 2, D1]), ACT.Copy)\
                       .then_inc(k_hi_ready, 1)
                    if t + 2 < NT:
                        pre_hi(2, t + 2)
                if t >= 1:
                    u = t - 1
                    act.wait_ge(ktr_done, u + 1)
                    act.activation(kt[:, cols(u)], STKT[0][:, 0:P], ACT.Copy).then_inc(kt_ready, 1)
                    for g in (0, 2):
                        act.wait_ge(qtr_done, 4 * u + g + 1)
                        act.activation(qt[:, 4 * g:4 * g + 4, cols(u)],
                                       STKT[g % 2].rearrange("p (j n) -> p j n", j=4), ACT.Copy).then_inc(qt_act, 1)
            act.wait_ge(wo1_in, 16)
            act.wait_ge(qkv_done, NT)
            split_hi(wo1_hi[:], wo1_raw[:], wo1_hi_ready)

            batch = 0
            for t, kb, p, after, steps_back in slots:
                if t is not None:
                    for g in range(4):
                        use = 4 * batch + g
                        act.wait_ge(s2_done, use + 1)
                        if batch >= P_BUFS // 4 and g == 0:
                            act.wait_ge(pv_done, batch - P_BUFS // 4 + 1)
                        act.activation(probs[:, use % P_BUFS, :], S2[use % S2_BUFS], ACT.Exp).then_inc(p_ready, 1)
                    batch += 1
                for u, step in steps_back:
                    if step == 0:
                        act.wait_ge(pv_done, batch_base[u] + 2 * (u + 1))
                        if u:
                            act.wait_ge(bg_o, 2 * u)
                        act.activation(o_sb[:], PV, ACT.Copy).then_inc(o_read, 1)
                    elif step == 2:
                        act.wait_ge(bg_a, u + 1)
                        if u:
                            act.wait_ge(y_done[2], u)
                        split_hi(at_hi, BG.rearrange("p (k n) -> p k n", k=KC), at_hi_ready)
                    elif step == 3:
                        i = 2 * NT + u
                        act.wait_ge(post_rstd[2], u + 1)
                        if u >= 2:
                            act.wait_ge(x_ready[2], u - 1)
                        act.activation(delta[:, u % 2, :], BG, ACT.Identity, bias=mv[:, 1, i, 0:1],
                                       scale=rstd[:, 1, i:i + 1]).then_inc(delta_ready[2], 1)

            for i in range(NT + 1):
                if i < NT:
                    pre_hi(3, i)
                if i >= 1:
                    t = i - 1
                    act.wait_ge(gap_ready, t + 1)
                    act.activation(prob[:, t, 1:2], prob[:, t, 0:1], ACT.Exp).then_inc(gap_exp, 1)
                    act.wait_ge(ht_done, t + 1)
                    if t >= 2:
                        act.wait_ge(y_done[3], t - 1)
                    split_hi(ht_hi[:, t % 2], HT[0:ER // 2, :].rearrange("p (c n) -> p c n", c=2), ht_hi_ready)

        @block.gpsimd
        def _(pool):
            steps = [0]

            def link(ins):
                steps[0] += 1
                ins.then_inc(pool_step, 1)
                pool.wait_ge(pool_step, steps[0])

            def power(dst, src):
                return pool.tensor_tensor(dst, src, mhalf[:], ALU.pow)

            def pre_scale(p, t):
                i = p * NT + t
                r = rstd[:, 0, i:i + 1]
                pool.wait_ge(pre_var[p], t + 1)
                if p != 1:
                    power(r, ve[:, 0, i:i + 1]).then_inc(pre_rstd[p], 1)
                    return
                link(power(r, ve[:, 0, i:i + 1]))
                a = rms[:, t, :]
                link(pool.tensor_tensor(a[:, 0:1], r, r, ALU.mult))
                link(pool.tensor_tensor(a[:, 1:2], a[:, 0:1], mv[:, 0, i, 1:2], ALU.mult))
                link(pool.tensor_scalar(a[:, 2:3], a[:, 1:2], RMS_EPS, None, ALU.add))
                link(power(a[:, 3:4], a[:, 2:3]))
                pool.tensor_tensor(r, r, a[:, 3:4], ALU.mult).then_inc(pre_rstd[p], 1)

            def weigh(t):
                pool.wait_ge(nx_unscaled, t + 1)
                n = nx[:, 1, t % 2, :]
                pool.tensor_tensor(n, n, lnw[:], ALU.mult).then_inc(nx_ready[1], 1)

            def post_scale(p, t):
                i = p * NT + t
                pool.wait_ge(post_var[p], t + 1)
                if p != 2:
                    power(rstd[:, 1, i:i + 1], ve[:, 1, i:i + 1]).then_inc(post_rstd[p], 1)
                    return
                link(power(rstd[:, 1, i:i + 1], ve[:, 1, i:i + 1]))
                m = mv[:, 1, i, 0:1]
                link(pool.tensor_tensor(m, m, rstd[:, 1, i:i + 1], ALU.mult))
                pool.tensor_scalar(m, m, -1.0, None, ALU.mult).then_inc(post_rstd[p], 1)

            def add(p, t):
                pool.wait_ge(delta_ready[p], t + 1)
                pool.tensor_tensor(x[:, t, :], x[:, t, :], delta[:, t % 2, :], ALU.add).then_inc(x_ready[p], 1)

            link(pool.memset(mhalf[:], -0.5))
            pool.wait_ge(lnw_in, 16)
            pre_scale(0, 0)
            for i in range(NT + 2):
                if i + 1 < NT:
                    pre_scale(0, i + 1)
                if i < NT:
                    pool.wait_ge(sig_ready, i + 1)
                    if i:
                        pool.wait_ge(den_ready, i)
                    pool.tensor_tensor(prod[:], sig[:, i % 2, :], z_b[:], ALU.mult).then_inc(prod_ready, 1)
                if i >= 3:
                    post_scale(0, i - 3)
                if i < NT:
                    pool.wait_ge(den_ready, i + 1)
                    v = sig[:, i % 2, :].rearrange("p (h d) -> p h d", h=H0)
                    pool.tensor_tensor(v, v, den[:, i, 2, :].unsqueeze(2).broadcast_to([P, H0, D0]), ALU.mult)\
                        .then_inc(sig_scaled, 1)
                if i >= 3:
                    add(0, i - 3)
                if i >= 4:
                    pre_scale(1, i - 4)
                    weigh(i - 4)
            post_scale(0, NT - 1)
            add(0, NT - 1)

            for c in range(2 * NJ):
                pool.wait_ge(wf_hi_ready, c + 1)
                b, r = c % WBUFS, c % RAW_BUFS
                pool.tensor_tensor(wf_lo[:, b, :], wf_raw[:, r, :], f32(wf_hi[:, b, :]), ALU.subtract)\
                    .then_inc(wf_ready, 1)
                if c == NJ + 1:
                    for t in range(HALF):
                        post_scale(1, t)
                    for t in range(HALF):
                        add(1, t)
                if c < 2:
                    pre_scale(1, NT - 2 + c)
                    weigh(NT - 2 + c)
                if c == 9:
                    pool.wait_ge(wkv_hi_ready, 1)
                    pool.tensor_tensor(wkv_lo[:], wkv_raw[:], f32(wkv_hi[:]), ALU.subtract).then_inc(wkv_ready, 1)
                if c == 11:
                    pool.memset(f32(qs[:]), 0.0).then_inc(pads_ready, 1)
                if NJ + 1 <= c < NJ + 3:
                    pre_scale(2, c - NJ - 1)

            for t in range(HALF, NT):
                post_scale(1, t)
            for t in range(HALF, NT):
                add(1, t)

            link(pool.memset(vals[:], 0.0))
            pool.memset(vals[:, :, D1:D1 + 1], 1.0).then_inc(pads_ready, 1)
            link(pool.memset(f32(ks[:]), 0.0))
            pool.sem_inc(pads_ready, 1)
            for t in range(NT):
                b = t % 2
                if t >= 2:
                    pool.wait_ge(qtr_done, 4 * (t - 1))
                    pool.wait_ge(ktr_done, t - 1)
                if t == 0:
                    pool.wait_ge(tab_in, 64)
                pool.tensor_copy(qs[:, b, :, 0:BIAS_ROWS], qbias[:, t]).then_inc(qs_bias, 1)
                pool.tensor_copy(ks[:, b, :, 0:BIAS_ROWS],
                                 kbias[:, t, :].unsqueeze(1).broadcast_to([P, 2, BIAS_ROWS])).then_inc(qs_bias, 1)
                if t + 2 < NT:
                    pre_scale(2, t + 2)
            pool.wait_ge(wo1_hi_ready, 1)
            pool.tensor_tensor(wo1_lo[:], wo1_raw[:], f32(wo1_hi[:]), ALU.subtract).then_inc(wo1_ready, 1)

            def expert_weights(k):
                pool.wait_ge(we_in[k % 2], 16 * (k // 2 + 1))
                pool.tensor_copy(we_hi[:, k, :], we_raw[:, k % 2, :]).then_inc(we_hi_ready, 1)
                pool.wait_ge(we_hi_ready, k + 1)
                pool.tensor_tensor(we_lo[:, k, :], we_raw[:, k % 2, :], f32(we_hi[:, k, :]), ALU.subtract)\
                    .then_inc(we_ready, 1)

            def adapter_weights(c):
                pool.wait_ge(lb_in, 16 * (c + 1))
                pool.tensor_copy(lb_hi[:, c, :], lb_raw[:]).then_inc(lb_hi_ready, 1)
                pool.wait_ge(lb_hi_ready, c + 1)
                pool.tensor_tensor(lb_lo[:, c, :], lb_raw[:], f32(lb_hi[:, c, :]), ALU.subtract).then_inc(lb_ready, 1)

            for t, kb, p, after, steps_back in slots:
                for u, step in steps_back:
                    if step == 3:
                        post_scale(2, u)
                        add(2, u)
                        if u in (2, 3):
                            expert_weights(u - 2)
                        if u in (5, 6):
                            expert_weights(u - 3)
                        if u in (6, 7):
                            adapter_weights(u - 6)

            for i in range(NT + 2):
                if i < NT:
                    pre_scale(3, i)
                if i >= 2:
                    post_scale(3, i - 2)
                    add(3, i - 2)

        @block.tensor
        def _(pe):
            def product(dst, hi, lo, w_hi, w_lo, first, last):
                pe.matmul(dst, hi, w_hi, start=first, stop=False, skip_group_check=True)
                pe.matmul(dst, hi, w_lo, start=False, stop=False, skip_group_check=True)
                return pe.matmul(dst, lo, w_hi, start=False, stop=last, skip_group_check=True)

            def turn(dst, src):
                return pe.transpose(dst, src, ident[:])

            def pre_turn(p, t):
                pe.wait_ge(nx_ready[p], t + 1)
                if t:
                    pe.wait_ge(nt_ready[p], t)
                for k in range(KC):
                    ins = turn(TR[p % 2][:, k * P:(k + 1) * P], nx[:, p % 2, t % 2, k * P:(k + 1) * P])
                ins.then_inc(tr_done[p], 1)

            pe.wait_ge(id_in, 16)
            pre_turn(0, 0)
            pe.wait_ge(wq_ready, KC)
            for i in range(NT + 2):
                if i < NT:
                    pe.wait_ge(nt_ready[0], i + 1)
                    if i:
                        pe.wait_ge(q0_min, i)
                    for n in range(2):
                        for k in range(KC):
                            w = slice(n * HID, (n + 1) * HID)
                            ins = product(Q0[:, n, :], nt_hi[:, i % 2, k], nt_lo[:, i % 2, k],
                                          wq_hi[:, k, w], wq_lo[:, k, w], k == 0, k == KC - 1)
                    ins.then_inc(q0_done, 1)
                if i + 1 < NT:
                    pre_turn(0, i + 1)
                if i < 2:
                    if i == 0:
                        pe.wait_ge(m_ready, 1)
                    for h in range(H0 // 2 * i, H0 // 2 * (i + 1)):
                        pe.wait_ge(wsum_lo_ready, h + 1)
                        if h >= 2:
                            pe.wait_ge(mw_ready, h - 1)
                        product(Y0[h % 2], m_hi[:, h], m_lo[:, h], wsum_hi[:], wsum_lo[:], True, True)\
                            .then_inc(mw_done, 1)
                if i >= 2:
                    t = i - 2
                    pe.wait_ge(sigt_ready, t + 1)
                    if t == 0:
                        pe.wait_ge(mw_ready, H0)
                    if t >= 2:
                        pe.wait_ge(delta_ready[0], t - 1)
                    for h in range(H0):
                        ins = product(Y0[t % 2], sigt_hi[:, h], sigt_lo[:, h], mw_hi[:, h], mw_lo[:, h],
                                      h == 0, h == H0 - 1)
                    ins.then_inc(y_done[0], 1)
                if 1 <= i <= NT:
                    t = i - 1
                    pe.wait_ge(sig_scaled, t + 1)
                    if t:
                        pe.wait_ge(sigt_ready, t)
                    for h in range(H0):
                        ins = turn(SIGT[:, h // 4, (h % 4) * P:(h % 4 + 1) * P], sig[:, t % 2, h * D0:(h + 1) * D0])
                    ins.then_inc(sigt_done, 1)
                if i >= 4:
                    pre_turn(1, i - 4)

            def down(c):
                b, j = c % WBUFS, c % NJ
                pe.wait_ge(hid_ready, c + 1)
                if c == NJ:
                    pe.wait_ge(delta_ready[1], HALF)
                w = slice(DW, DW + HID)
                for m in range(HALF):
                    ins = product(Y1[:, m, :], hid_hi[:, c % 2, m * P:(m + 1) * P], hid_lo[:, c % 2, m * P:(m + 1) * P],
                                  wf_hi[:, b, w], wf_lo[:, b, w], j == 0, j == NJ - 1)
                ins.then_inc(down_done, 1)
                if j == NJ - 1:
                    pe.wait_ge(down_done, c + 1)
                    pe.sem_inc(y_done[1], 1)

            pe.wait_ge(delta_ready[0], NT)
            for c in range(2 * NJ):
                b = c % WBUFS
                tok = slice(c // NJ * HALF * P, (c // NJ + 1) * HALF * P)
                pe.wait_ge(wf_ready, c + 1)
                if c % NJ == 0:
                    pe.wait_ge(nt_ready[1], HALF * (c // NJ + 1))
                for dst, start, free, done in ((GATE, GW, silu_ready, g_done), (UP, UW, hid_f_ready, u_done)):
                    if c:
                        pe.wait_ge(free, c)
                    for k in range(KC):
                        w = slice(start + k * P, start + (k + 1) * P)
                        pe.matmul(dst, wf_hi[:, b, w], mt_hi[:, k, tok], start=(k == 0), stop=False)
                        pe.matmul(dst, wf_hi[:, b, w], mt_lo[:, k, tok], start=False, stop=False)
                        ins = pe.matmul(dst, wf_lo[:, b, w], mt_hi[:, k, tok], start=False, stop=(k == KC - 1))
                    ins.then_inc(done, 1)
                if c:
                    down(c - 1)
                if c < 2:
                    pre_turn(1, NT - 2 + c)
                if NJ + 1 <= c < NJ + 3:
                    pre_turn(2, c - NJ - 1)
            down(2 * NJ - 1)

            pe.wait_ge(wkv_ready, 1)
            for t in range(NT + 1):
                if t < NT:
                    pe.wait_ge(nt_ready[2], t + 1)
                    if t == 0:
                        pe.wait_ge(delta_ready[1], NT)
                    else:
                        pe.wait_ge(qs_ready, t)
                        pe.wait_ge(ks_ready, 2 * t)
                        pe.wait_ge(v_ready, t)
                    for dst, w in ((QP, slice(0, HID)), (KVP, slice(HID, HID + 2 * D1))):
                        for k in range(KC):
                            ins = product(dst, nt_hi[:, t % 2, k], nt_lo[:, t % 2, k], wkv_hi[:, k, w], wkv_lo[:, k, w],
                                          k == 0, k == KC - 1)
                    ins.then_inc(qkv_done, 1)
                    if t + 2 < NT:
                        pre_turn(2, t + 2)
                if t >= 1:
                    u = t - 1
                    pe.wait_ge(qs_bias, 2 * t)
                    pe.wait_ge(ks_ready, 2 * t)
                    if u:
                        pe.wait_ge(qt_act, 2 * u)
                    turn(STKT[0][:, 0:P], f32(ks[:, u % 2].rearrange("p r c -> p (r c)"))).then_inc(ktr_done, 1)
                    pe.wait_ge(qs_ready, t)
                    if u:
                        pe.wait_ge(qt_dve, 2 * u)
                    for g in range(4):
                        if g == 0:
                            pe.wait_ge(kt_ready, u + 1)
                        if g == 2:
                            pe.wait_ge(qt_act, 2 * u + 1)
                        if g == 3:
                            pe.wait_ge(qt_dve, 2 * u + 1)
                        for j in range(4):
                            pair = 4 * g + j
                            ins = turn(STKT[g % 2][:, j * P:(j + 1) * P],
                                       f32(qs[:, u % 2, 2 * pair:2 * pair + 2, :].rearrange("p q c -> p (q c)")))
                        ins.then_inc(qtr_done, 1)

            def s1_item(t, n):
                use = s1_base[t] + n
                dst = S1[use % 2]
                if use >= 2:
                    pe.wait_ge(s1_read, use - 1)
                if n == len(pieces[t]):
                    pe.wait_ge(shift_ready, t + 1)
                    pe.transpose(dst[0:STK, 0:P], shift[:, t % 2].rearrange("p q s j -> p (q s j)"), ident[:])\
                      .then_inc(s1_done, 1)
                    return
                q, j, nh, k0, kw, part = pieces[t][n]
                r = slice(STK * q, STK * (q + 1))
                diagonal = k0 + kw == (t + 1) * P
                for i in range(nh):
                    ins = pe.matmul(dst[:, i * kw:(i + 1) * kw], qt[r, j + i, cols(t)], kt[r, k0:k0 + kw],
                                    start=(i == 0), stop=not diagonal, skip_group_check=True)
                if diagonal:
                    ins = pe.matmul(dst[:, 0:nh * kw].rearrange("p (h k) -> p h k", h=nh)[:, :, kw - P:kw],
                                    masks[:, 0, :], masks[:, 1, :].unsqueeze(1).broadcast_to([P, nh, P]),
                                    start=False, stop=True, skip_group_check=True)
                ins.then_inc(s1_done, 1)

            def s2_piece(use, t, kb, p, g):
                dst = S2[use % S2_BUFS]
                if use >= S2_BUFS:
                    pe.wait_ge(p_ready, use - S2_BUFS + 1)
                r = slice(STK * p, STK * (p + 1))
                diagonal = kb == t
                ins = pe.matmul(dst, kt[r, cols(kb)], qt[r, 4 * g:4 * g + 4, cols(t)],
                                start=True, stop=not diagonal, skip_group_check=True)
                if diagonal:
                    ins = pe.matmul(dst, masks[:, 0, :], masks[:, 2, :].unsqueeze(1).broadcast_to([P, 4, P]),
                                    start=False, stop=True, skip_group_check=True)
                ins.then_inc(s2_done, 1)

            def values(batch, t, kb, p):
                pe.wait_ge(p_ready, 4 * batch + 4)
                if kb == 0 and p == 0 and t:
                    pe.wait_ge(o_read, t)
                for g in range(4):
                    ins = pe.matmul(PV[VW * g:VW * (g + 1), p, :], vals[:, kb, :],
                                    probs[:, (4 * batch + g) % P_BUFS, :], start=(kb == 0), stop=(kb == t),
                                    skip_group_check=True)
                ins.then_inc(pv_done, 1)

            def back(t, step):
                if step < 2:
                    if step == 0:
                        pe.wait_ge(o_read, t + 1)
                        if t:
                            pe.wait_ge(delta_ready[2], t)
                    else:
                        pe.wait_ge(bg_o_read, 2 * t + 1)
                    for i in range(4):
                        ins = turn(BG[:, i * P:(i + 1) * P], o_sb[:, step, i * P:(i + 1) * P])
                    ins.then_inc(bg_o, 1)
                elif step == 2:
                    pe.wait_ge(bg_o_read, 2 * t + 2)
                    for k in range(KC):
                        ins = turn(BG[:, k * P:(k + 1) * P], attn[:, k * P:(k + 1) * P])
                    ins.then_inc(bg_a, 1)
                else:
                    pe.wait_ge(bg_a_read, t + 1)
                    if t == 0:
                        pe.wait_ge(wo1_ready, 1)
                    for k in range(KC):
                        ins = product(BG, at_hi[:, k], at_lo[:, k], wo1_hi[:, k], wo1_lo[:, k], k == 0, k == KC - 1)
                    ins.then_inc(y_done[2], 1)

            pe.wait_ge(mask_ready, 1)
            pe.wait_ge(kt_ready, NT)
            pe.wait_ge(qt_act, 2 * NT)
            pe.wait_ge(qt_dve, 2 * NT)
            pe.wait_ge(pads_ready, 3)
            for n in range(len(pieces[0]) + 1):
                s1_item(0, n)
            batch = 0
            before = None
            for t, kb, p, after, steps_back in slots:
                if t is not None:
                    if kb == 0 and p == 0:
                        pe.wait_ge(shift_in[t % 2], 64 * (t // 2 + 1))
                    for g in range(4):
                        s2_piece(4 * batch + g, t, kb, p, g)
                        for n in after[g]:
                            s1_item(t + 1, n)
                if before is not None:
                    values(*before)
                before = (batch, t, kb, p) if t is not None else None
                batch += t is not None
                for u, step in steps_back:
                    back(u, step)

            for i in range(NT + 2):
                if i < NT:
                    pre_turn(3, i)
                    pe.wait_ge(nt_ready[3], i + 1)
                    if i == 0:
                        pe.wait_ge(we_ready, KC)
                    if i >= 2:
                        pe.wait_ge(hs_ready, i - 1)
                    if i >= 3:
                        pe.wait_ge(delta_ready[3], i - 2)
                    for dst, w, last in ((L3[i % 2], slice(HID, HID + LG), True), (O3[i % 3], slice(0, HID), False)):
                        for k in range(KC):
                            ins = product(dst, nt_hi[:, i % 2, k], nt_lo[:, i % 2, k], we_hi[:, k, w], we_lo[:, k, w],
                                          k == 0, last and k == KC - 1)
                        if last:
                            ins.then_inc(l3_done, 1)
                if i >= 2:
                    t = i - 2
                    pe.wait_ge(ht_ready, t + 1)
                    if t == 0:
                        pe.wait_ge(lb_ready, 2)
                    for c in range(2):
                        ins = product(O3[t % 3], ht_hi[:, t % 2, c], ht_lo[:, t % 2, c], lb_hi[:, c], lb_lo[:, c],
                                      False, c == 1)
                    ins.then_inc(y_done[3], 1)
                if 1 <= i <= NT:
                    t = i - 1
                    pe.wait_ge(hs_ready, t + 1)
                    if t:
                        pe.wait_ge(ht_ready, t)
                    for c in range(2):
                        ins = turn(HT[0:ER // 2, c * P:(c + 1) * P], hs[:, t % 2, c * (ER // 2):(c + 1) * (ER // 2)])
                    ins.then_inc(ht_done, 1)


def layouts(i):
    def hidden_major(w):
        return w.T.reshape(KC, P, w.shape[0]).transpose(1, 0, 2)

    heads = i["L0_attn_Wq"].reshape(H0, G0, D0, HID)[:, 0].reshape(H0 * D0, HID)
    gate, up = (i[f"L0_ffn_{n}_w"].reshape(NJ, P, KC, P).transpose(0, 3, 2, 1).reshape(NJ, P, KC * P)
                for n in ("gate", "up"))
    down = i["L0_ffn_down_w"].T.reshape(NJ, P, HID)
    experts = np.concatenate([i["L1_ffn_base_W"], i["L1_ffn_gate_W"], i["L1_ffn_lora_A"].reshape(ER, HID)])
    return {
        "x": i["L0_attn_hidden_states"],
        "wq": hidden_major(heads),
        "bq": i["L0_attn_bq"].reshape(H0, G0, D0)[:, 0].reshape(1, H0 * D0),
        "z": i["L0_attn_z"].reshape(1, H0 * D0),
        "m": i["L0_attn_M"].transpose(2, 0, 1),
        "wo0": i["L0_attn_Wo"].reshape(HID, H0, G0, D0).transpose(1, 3, 2, 0).reshape(H0, D0, G0 * HID),
        "lnw": i["L0_ffn_ln_w"].reshape(1, HID),
        "wf": np.concatenate([gate, up, down], axis=2),
        "wkv": i["L1_attn_Wqkv"].reshape(KC, P, HID + 2 * D1).transpose(1, 0, 2),
        "wo1": i["L1_attn_Wo"].reshape(KC, P, HID).transpose(1, 0, 2),
        "we": experts.T.reshape(KC, P, HID + LG),
        "lb": i["L1_ffn_lora_B"].transpose(0, 2, 1).reshape(2, ER // 2, HID).transpose(1, 0, 2),
    }


def kernel(**inputs):
    import concourse.bacc as _bacc
    from concourse.bass_utils import run_bass_kernel_spmd as _run

    nc = _bacc.Bacc("TRN2", target_bir_lowering=False, num_devices=1)
    arrays, aps = {}, {}
    for name, a in {**layouts({n: np.asarray(v) for n, v in inputs.items()}), **constants()}.items():
        a = np.ascontiguousarray(a)
        arrays[f"in_{name}"] = a
        aps[name] = nc.dram_tensor(f"in_{name}", a.shape, mybir.dt.from_np(a.dtype), kind="ExternalInput").ap()
    out = nc.dram_tensor("out_0", (1, S, HID), F32, kind="ExternalOutput").ap()
    build(nc, aps, out)
    r = _run(nc, [arrays], core_ids=[0])
    return r.results[0]["out_0"]
```

```python
from contextlib import ExitStack

import numpy as np

import concourse.bass as bass
from concourse import mybir

F32 = mybir.dt.float32
F32R = mybir.dt.float32r
BF16 = mybir.dt.bfloat16
U32 = mybir.dt.uint32
ALU = mybir.AluOpType
ACT = mybir.ActivationFunctionType
X = mybir.AxisListType.X

P = 128
S = 1024
HID = 512
NT = S // P
KC = HID // P
BANK = 512
LN_EPS = 1e-5
H0, D0, G0 = 8, 128, 4
DEN_EPS = 1e-6
INNER = 1792
NJ = INNER // P
RMS_EPS = 1e-5
HALF = 4
WCH = 2 * KC * P + HID
GW, UW, DW = 0, KC * P, 2 * KC * P
RAW_BUFS = 3
WO_BUFS = 4
HEADS_AT = (0, 2, 5, 8)
WBUFS = 3
H1, D1 = 32, 16
PAIRS = H1 // 2
SCALE = float(D1) ** -0.5
STK = 64
BIAS_ROWS = 6
QHI, QLO = BIAS_ROWS, BIAS_ROWS + 2 * D1
VW = 32
S1_BUFS, S2_BUFS, P_BUFS = 3, 2, 12
LEAD = 2
EARLY_FROM = 3
NE, RANK, SCALING = 28, 8, 2.0
ER = NE * RANK
LG = NE + ER

PHASES = 4


def split12(v):
    v = np.asarray(v, np.float32)
    hi = ((v.view(np.uint32) + np.uint32(0x800)) & np.uint32(0xFFFFF000)).view(np.float32)
    return hi, (v - hi).astype(np.float32)


def constants():
    slopes = ((2.0 ** (-(2.0 ** -2.0))) ** np.arange(1, H1 + 1, dtype=np.float64)).astype(np.float32)
    s_hi, s_lo = split12(slopes)
    pos = np.arange(S, dtype=np.float32)
    a_hi, a_lo = split12(-(s_hi[None, :] * pos[:, None]))
    w0 = -(s_lo[None, :] * pos[:, None])
    b_hi, b_lo = split12(w0)
    one = np.ones((S, 1), np.float32)
    q_bias = np.stack([one * s_hi, a_hi, a_lo, one * s_lo, b_hi, b_lo], -1)
    q_bias = q_bias.reshape(NT, P, H1 * BIAS_ROWS).transpose(1, 0, 2)
    k_bias = np.stack([pos, one[:, 0], one[:, 0], pos, one[:, 0], one[:, 0]], -1)
    k_bias = k_bias.reshape(NT, P, BIAS_ROWS).transpose(1, 0, 2)
    w0 = w0.reshape(NT, P, PAIRS, 2).transpose(1, 0, 3, 2)
    c = np.arange(P)
    later = np.where(c[None, :] > c[:, None], np.float32(-1e30), np.float32(0))
    masks = np.stack([np.eye(P, dtype=np.float32), later, later.T])
    return {
        "c_ident": np.eye(P, dtype=np.float32),
        "c_masks": masks.transpose(1, 0, 2),
        "c_qbias": q_bias,
        "c_kbias": k_bias,
        "c_w0": w0,
        "c_iota": np.tile(np.arange(NE, dtype=np.float32), (P, 1)),
    }


def score_pieces(t):
    kw = (t + 1) * P
    out = []
    if kw <= BANK:
        n = BANK // kw
        for j in range(0, PAIRS, n):
            out += [(p, j, n, 0, kw, 0) for p in range(2)]
    else:
        rest = kw - BANK
        n = BANK // rest
        for j in range(0, PAIRS, n):
            out += [(p, j + i, 1, 0, BANK, 0) for i in range(n) for p in range(2)]
            out += [(p, j, n, BANK, rest, 1) for p in range(2)]
    return out


def attention_slots():
    slots = [[t, kb, p, None, None, None] for t in range(NT) for kb in range(t + 1) for p in range(2)]
    scores = len(slots)
    for e in range(2 * (NT + 3)):
        slots.append([None, None, None, None, None, e])
    for slot in slots:
        slot[3] = [[] for g in range(4)]
        slot[4] = [[] for g in range(5)]

    start = [t * (t + 1) for t in range(NT)]
    left = [(t, n) for t in range(2, NT) for n in range(len(score_pieces(t)) + 1)]
    due = [sum(len(score_pieces(u)) + 1 for u in range(2, t + 1)) for t in range(NT)]
    done, credit = 0, 0.0
    for n in range(4 * (start[NT - 1] - LEAD)):
        even = max((due[t] - done) / (4 * (start[t] - LEAD) - n) for t in range(2, NT) if 4 * (start[t] - LEAD) > n)
        credit += even
        take = min(int(credit + 1e-6), len(left))
        credit -= take
        slots[n // 4][3][n % 4] = left[:take]
        left = left[take:]
        done += take
    for last in left:
        slots[start[NT - 1] - LEAD][3][0].append(last)

    enter, busy, at = [], set(), 0
    for t in range(NT):
        at = max(at, (t + 1) * (t + 2) - 1 + 2)
        enter.append(at)
        busy |= set(range(at, at + 6))
        at += 6
    turn3 = []
    for t in range(NT):
        at = enter[t] + 8
        while at in busy:
            at += 1
        busy.add(at)
        turn3.append(at)

    for t in range(NT):
        slots[(t + 1) * (t + 2) + 1][4][0].append((t, "copy"))
        for step, after, place in (("turn0", 0, 4), ("norm0", 1, 2), ("turn1", 1, 4), ("norm1", 2, 2), ("turn2", 2, 4),
                                   ("high", 3, 1), ("low", 3, 3), ("project0", 4, 0), ("project1", 4, 1),
                                   ("project2", 4, 2), ("project3", 4, 3), ("stats", 5, 1), ("apply", 6, 0)):
            slots[enter[t] + after][4][place].append((t, step))
        for step, after, place in (("stats3", -1, 1), ("norm3", 0, 0), ("turn3", 0, 4), ("high3", 1, 1), ("low3", 1, 3)):
            slots[turn3[t] + after][4][place].append((t, step))
    assert turn3[NT - 1] + 1 < scores + 2 * (NT - 1)
    return (slots, [sum(at < e for at in turn3) for e in enter], [sum(e < at for e in enter) for at in turn3])


def build(nc, A, out):
    ctx = ExitStack()
    with ctx:
        def sb(name, shape, dt=F32):
            return ctx.enter_context(nc.sbuf_tensor(name, shape, dt))

        def sem(name):
            return ctx.enter_context(nc.semaphore(name))

        def sems(name, n):
            return [sem(f"{name}{i}") for i in range(n)]

        x = sb("x", [P, NT, HID])
        nx = sb("nx", [P, 2, 2, HID])
        nt_hi = sb("nt_hi", [P, 2, KC, P], F32R)
        nt_lo = sb("nt_lo", [P, 2, KC, P], F32R)
        delta = sb("delta", [P, 2, HID])
        lnw = sb("lnw", [P, HID])
        ident = sb("ident", [P, P])
        masks = sb("masks", [P, 3, P], BF16)
        w0 = sb("w0", [P, NT, 2, PAIRS])
        kbias = sb("kbias", [P, NT, BIAS_ROWS])
        iota = sb("iota", [P, NE])
        bn = sb("bn", [P, 2, PHASES * NT, 6])
        mv = sb("mv", [P, 2, PHASES * NT, 2])
        ve = sb("ve", [P, 2, PHASES * NT])
        rstd = sb("rstd", [P, 2, PHASES * NT])
        mhalf = sb("mhalf", [P, 1])
        den = sb("den", [P, NT, 3, H0])
        rowmax = sb("rowmax", [P, 2, 2, 2, PAIRS])
        wshift = sb("wshift", [P, 2, 2, 2, PAIRS])
        shift = sb("shift", [P, 2, 2, 2, PAIRS])
        shift_t = sb("shift_t", [STK, 2, P], F32R)
        rsum = sb("rsum", [P, 2, 2, PAIRS])
        top = sb("top", [P, NT, 8])
        vals = sb("vals", [P, NT, VW])
        topi = sb("topi", [P, NT, 8], U32)
        prob = sb("prob", [P, NT, 8])
        gate = sb("gate", [P, 2, 3, NE])
        logit = sb("logit", [P, 2, NE])

        kib = 1024
        b_at = nc.sbuf_base
        c_at = b_at + 32 * kib + 512
        room = 158 * kib + 512
        sb("arena", [P, room // 4])

        def at(name, start, kb, shape, dt=F32):
            size = int(np.prod(shape[1:])) * mybir.dt.size(dt)
            assert start + int(kb * kib) + size <= b_at + room, (name, start + kb * kib + size - b_at - room)
            return nc.alloc_sbuf_tensor_at(name, shape, dt, offset=start + int(kb * kib))

        mt_hi = at("mt_hi", b_at, 0, [P, KC, S], F32R)
        mt_lo = at("mt_lo", b_at, 16, [P, KC, S], F32R)
        we_hi = at("we_hi", b_at, 0, [P, KC, HID + LG], F32R)
        we_lo = at("we_lo", b_at, 12, [P, KC, HID + LG], F32R)
        lb_hi = at("lb_hi", b_at, 24, [ER // 2, 2, HID], F32R)
        lb_lo = at("lb_lo", b_at, 28, [ER // 2, 2, HID], F32R)
        wq_hi = at("wq_hi", c_at, 0, [P, KC, H0 * D0], F32R)
        wq_lo = at("wq_lo", c_at, 16, [P, KC, H0 * D0], F32R)
        wo0_raw = at("wo0_raw", b_at, 0, [P, WO_BUFS, G0, HID])
        m_raw = at("m_raw", c_at, 40, [P, H0, D0])
        m_hi = at("m_hi", c_at, 44, [P, H0, D0], F32R)
        m_lo = at("m_lo", c_at, 48, [P, H0, D0], F32R)
        wsum = at("wsum", c_at, 32, [P, 2, HID])
        wsum_hi = at("wsum_hi", c_at, 36, [P, 2, HID], F32R)
        wsum_lo = at("wsum_lo", c_at, 52, [P, 2, HID], F32R)
        bq_b = at("bq_b", c_at, 58, [P, H0 * D0])
        z_b = at("z_b", c_at, 62, [P, H0 * D0])
        q0 = at("q0", c_at, 66, [P, H0 * D0])
        e0 = at("e0", c_at, 70, [P, H0 * D0])
        sig = at("sig", c_at, 74, [P, 2, H0 * D0])
        prod = at("prod", c_at, 82, [P, H0 * D0])
        sigt_hi = at("sigt_hi", c_at, 86, [P, H0, P], F32R)
        sigt_lo = at("sigt_lo", c_at, 90, [P, H0, P], F32R)
        mw_hi = at("mw_hi", c_at, 94, [P, H0, HID], F32R)
        mw_lo = at("mw_lo", c_at, 110, [P, H0, HID], F32R)
        wq_raw = at("wq_raw", c_at, 110, [P, KC, H0 * D0])
        mask_raw = at("mask_raw", c_at, 94, [P, 3, P])
        wf_hi = at("wf_hi", c_at, 0, [P, WBUFS, WCH], F32R)
        wf_lo = at("wf_lo", c_at, 18, [P, WBUFS, WCH], F32R)
        wf_raw = at("wf_raw", c_at, 36, [P, RAW_BUFS, WCH])
        silu = at("silu", c_at, 58, [P, 2, HALF * P])
        hid = at("hid", c_at, 62, [P, 2, HALF * P])
        hid_hi = at("hid_hi", c_at, 66, [P, 2, HALF * P], F32R)
        hid_lo = at("hid_lo", c_at, 70, [P, 2, HALF * P], F32R)
        wkv_raw = at("wkv_raw", c_at, 80, [P, KC, HID + 2 * D1])
        wkv_hi = at("wkv_hi", c_at, 89, [P, KC, HID + 2 * D1], F32R)
        wkv_lo = at("wkv_lo", c_at, 97.5, [P, KC, HID + 2 * D1], F32R)
        qbias = at("qbias", c_at, 74, [P, NT, H1, BIAS_ROWS])
        qs = at("qs", c_at, 106, [P, 2, H1, STK], F32R)
        qt = at("qt", c_at, 0, [P, PAIRS, S], F32R)
        kt = at("kt", c_at, 64, [P, 2, S], F32R)
        ks = at("ks", c_at, 72, [P, 2, 2, STK], F32R)
        wo1_raw = at("wo1_raw", c_at, 72, [P, KC, HID])
        wo1_hi = at("wo1_hi", c_at, 80, [P, KC, HID], F32R)
        wo1_lo = at("wo1_lo", c_at, 88, [P, KC, HID], F32R)
        probs = at("probs", c_at, 98, [P, P_BUFS, BANK])
        o_sb = at("o_sb", c_at, 122, [P, 2, BANK])
        we_raw = at("we_raw", c_at, 72, [P, 2, HID + LG])
        lb_raw = at("lb_raw", c_at, 78, [ER // 2, HID])
        hs = at("hs", c_at, 98, [P, 2, ER])
        ht_hi = at("ht_hi", c_at, 102, [ER // 2, 2, 2, P], F32R)
        ht_lo = at("ht_lo", c_at, 106, [ER // 2, 2, 2, P], F32R)
        attn = nx[:, 1, 0, :]
        at_hi, at_lo = nt_hi[:, 0], nt_lo[:, 0]
        delta3 = at("delta3", c_at, 110, [P, 2, HID])

        psum = ctx.enter_context(nc.psum_tensor("psum", [P, 8, BANK], F32))
        TR = [psum[:, b, :] for b in (6, 7, 6, 4)]
        Q0, SIGT, Y0 = psum[:, 0:2, :], psum[:, 2:4, :], [psum[:, 4, :], psum[:, 5, :]]
        GATE, UP, Y1 = psum[:, 0, :], psum[:, 1, :], psum[:, 2:6, :]
        QP, KVP, STKT = psum[:, 0, :], psum[:, 1, 0:2 * D1], [psum[:, 4, :], psum[:, 5, :]]
        S1 = [psum[:, b, :] for b in (2, 3, 7)]
        S2 = [psum[:, b, :] for b in range(4)]
        PV, BG = psum[:, 5:7, :], psum[:, 4, :]
        O3, L3 = [psum[:, b, :] for b in (0, 1, 5, 6)], [psum[:, 2, 0:LG], psum[:, 3, 0:LG]]
        HT = psum[:, 7, 0:2 * P]

        x_in = sems("x_in", NT)
        id_in, mask_in, bz_in, m_in, tab_in, lnw_in = map(sem, ("id_in", "mask_in", "bz_in", "m_in", "tab_in", "lnw_in"))
        wq_in = sems("wq_in", KC)
        wo0_in = sems("wo0_in", WO_BUFS)
        wf_in = sems("wf_in", RAW_BUFS)
        wkv_in, wo1_in, lb_in = sem("wkv_in"), sem("wo1_in"), sem("lb_in")
        we_in = sems("we_in", 2)
        pre_var, pre_rstd, nx_ready, tr_done, nt_hi_ready, nt_ready = (
            sems(n, PHASES) for n in ("pre_var", "pre_rstd", "nx_ready", "tr_done", "nt_hi_ready", "nt_ready"))
        nx_unscaled = sem("nx_unscaled")
        y_done, post_var, post_rstd, delta_ready, x_ready = (
            sems(n, PHASES) for n in ("y_done", "post_var", "post_rstd", "delta_ready", "x_ready"))
        dve_step, act_step, pool_step = sem("dve_step"), sem("act_step"), sem("pool_step")
        mask_ready, mhalf_ready = sem("mask_ready"), sem("mhalf_ready")
        wq_hi_ready, wq_ready, m_hi_ready, m_ready = map(sem, ("wq_hi_ready", "wq_ready", "m_hi_ready", "m_ready"))
        wsum_hi_ready, wsum_lo_ready, mw_done, mw_hi_ready, mw_ready = map(
            sem, ("wsum_hi_ready", "wsum_lo_ready", "mw_done", "mw_hi_ready", "mw_ready"))
        q0_done, q0_ready, q0_exp, q0_relu, sig_ready, prod_ready, den_ready, sig_scaled = map(
            sem, ("q0_done", "q0_ready", "q0_exp", "q0_relu", "sig_ready", "prod_ready", "den_ready", "sig_scaled"))
        sigt_done, sigt_hi_ready, sigt_ready = map(sem, ("sigt_done", "sigt_hi_ready", "sigt_ready"))
        wf_hi_ready, wf_ready, g_done, u_done, silu_ready, hid_f_ready, hid_hi_ready, hid_ready, down_done = map(
            sem, ("wf_hi_ready", "wf_ready", "g_done", "u_done", "silu_ready", "hid_f_ready", "hid_hi_ready",
                  "hid_ready", "down_done"))
        wsum_ready, wo_half = sems("wsum_ready", 2), sem("wo_half")
        wkv_hi_ready, wkv_ready, wo1_hi_ready, wo1_ready = map(
            sem, ("wkv_hi_ready", "wkv_ready", "wo1_hi_ready", "wo1_ready"))
        qkv_done, q_hi_ready, k_hi_ready, v_ready, qs_ready, ks_ready, pads_ready, qs_bias = map(
            sem, ("qkv_done", "q_hi_ready", "k_hi_ready", "v_ready", "qs_ready", "ks_ready", "pads_ready", "qs_bias"))
        ktr_done, kt_ready, qtr_done, qt_act, qt_dve = map(sem, ("ktr_done", "kt_ready", "qtr_done", "qt_act", "qt_dve"))
        s1_done, s1_read, shift_ready, shift_t_ready = map(sem, ("s1_done", "s1_read", "shift_ready", "shift_t_ready"))
        shift_in = sems("shift_in", 2)
        s2_done, p_ready, pv_done, o_read = map(sem, ("s2_done", "p_ready", "pv_done", "o_read"))
        bg_o, bg_o_read, bg_a, at_hi_ready, bg_a_read = map(sem, ("bg_o", "bg_o_read", "bg_a", "at_hi_ready", "bg_a_read"))
        we_hi_ready, we_ready, lb_hi_ready, lb_ready = map(sem, ("we_hi_ready", "we_ready", "lb_hi_ready", "lb_ready"))
        l3_done, gap_ready, gap_exp, hs_ready, ht_done, ht_hi_ready, ht_ready = map(
            sem, ("l3_done", "gap_ready", "gap_exp", "hs_ready", "ht_done", "ht_hi_ready", "ht_ready"))
        out_sem = sem("out_sem")

        slots, turned3_before, projected_before = attention_slots()
        pieces = [score_pieces(t) for t in range(NT)]
        s1_base = [sum(len(pieces[u]) + 1 for u in range(t)) for t in range(NT)]
        batch_base = [t * (t + 1) for t in range(NT)]

        early = [(t, n) for t in range(2) for n in range(len(pieces[t]) + 1)]
        share = -(-len(early) // (NT - EARLY_FROM))
        early = [[] for t in range(EARLY_FROM)] + [early[i:i + share] for i in range(0, len(early), share)]
        early += [[] for t in range(NT + 1 - len(early))]

        last_use = 4 * batch_base[NT - 1]

        def s2_bank(use):
            return S2[use % (S2_BUFS if use < last_use else 4)]

        def cols(t):
            return slice(t * P, (t + 1) * P)

        def tile_transpose(p, t):
            if p in (1, 2):
                return mt_hi[:, :, cols(t)], mt_lo[:, :, cols(t)]
            if p == 3:
                return qt[:, 0:KC, cols(t)], qt[:, KC:2 * KC, cols(t)]
            return nt_hi[:, t % 2], nt_lo[:, t % 2]

        def delta_of(p, t):
            if p == 1 and t % HALF >= 2:
                return nx[:, 1, t % 2, :]
            return (delta3 if p == 3 else delta)[:, t % 2, :]

        def f32(ap):
            return ap.bitcast(F32)

        block = ctx.enter_context(nc.Block())

        @block.sync
        def _(sp):
            sp.dma_start(x[:, 0, :], A["x"][0, 0:P, :]).then_inc(x_in[0], 16)
            sp.dma_start(ident[:], A["c_ident"]).then_inc(id_in, 16)
            sp.dma_start(mask_raw[:], A["c_masks"]).then_inc(mask_in, 16)
            for k in range(KC):
                sp.dma_start(wq_raw[:, k, :], A["wq"][:, k, :]).then_inc(wq_in[k], 16)
            sp.dma_start(bq_b[:], A["bq"].broadcast_to([P, H0 * D0])).then_inc(bz_in, 16)
            sp.dma_start(z_b[:], A["z"].broadcast_to([P, H0 * D0])).then_inc(bz_in, 16)
            sp.dma_start(x[:, 1, :], A["x"][0, P:2 * P, :]).then_inc(x_in[1], 16)
            sp.dma_start(m_raw[:], A["m"]).then_inc(m_in, 16)
            sp.dma_start(lnw[:], A["lnw"].broadcast_to([P, HID])).then_inc(lnw_in, 16)
            for h in range(H0):
                if h < NT - 2:
                    sp.dma_start(x[:, h + 2, :], A["x"][0, (h + 2) * P:(h + 3) * P, :]).then_inc(x_in[h + 2], 16)
                if h >= WO_BUFS:
                    sp.wait_ge(wsum_ready[h % 2], (h - WO_BUFS) // 2 + 1)
                sp.dma_start(wo0_raw[:, h % WO_BUFS], A["wo0"][h].rearrange("p (g n) -> p g n", g=G0))\
                  .then_inc(wo0_in[h % WO_BUFS], 16)
            sp.dma_start(kbias[:], A["c_kbias"]).then_inc(tab_in, 16)
            sp.dma_start(w0[:], A["c_w0"]).then_inc(tab_in, 16)
            sp.dma_start(iota[:], A["c_iota"]).then_inc(tab_in, 16)
            for c in range(2 * NJ):
                if c == 0:
                    sp.wait_ge(mw_ready, H0)
                    sp.wait_ge(wsum_lo_ready, H0)
                if c >= RAW_BUFS:
                    sp.wait_ge(wf_ready, c - RAW_BUFS + 1)
                sp.dma_start(wf_raw[:, c % RAW_BUFS, :], A["wf"][c % NJ]).then_inc(wf_in[c % RAW_BUFS], 16)
                if c == 4:
                    sp.wait_ge(y_done[0], NT)
                    sp.dma_start(wkv_raw[:], A["wkv"]).then_inc(wkv_in, 16)
                    sp.dma_start(qbias[:].rearrange("p t h b -> p t (h b)"), A["c_qbias"]).then_inc(tab_in, 16)
            for t in range(NT):
                sp.wait_ge(shift_t_ready, t + 1)
                for p in range(2):
                    for part in range(2):
                        row = STK * p + BIAS_ROWS - 2 + part
                        src = (2 * p + part) * PAIRS
                        sp.dma_start(f32(qt[row:row + 1, :, cols(t)]), f32(shift_t[src:src + PAIRS, t % 2, :]))\
                          .then_inc(shift_in[t % 2], 16)
                if t == 1:
                    sp.wait_ge(qs_bias, 2 * NT)
                    sp.wait_ge(ktr_done, NT)
                    sp.dma_start(wo1_raw[:], A["wo1"]).then_inc(wo1_in, 16)
                if t == 2:
                    sp.wait_ge(wo1_ready, 1)
                    for k in range(2):
                        sp.dma_start(we_raw[:, k, :], A["we"][k]).then_inc(we_in[k], 16)
                if t == 4:
                    sp.wait_ge(we_ready, 2)
                    for k in range(2):
                        sp.dma_start(we_raw[:, k, :], A["we"][k + 2]).then_inc(we_in[k], 16)
                    sp.dma_start(lb_raw[:], A["lb"][:, 0, :]).then_inc(lb_in, 16)
                if t == NT - 1:
                    sp.wait_ge(lb_ready, 1)
                    sp.dma_start(lb_raw[:], A["lb"][:, 1, :]).then_inc(lb_in, 16)
            for t in range(NT):
                sp.wait_ge(x_ready[3], t + 1)
                sp.dma_start(out[0, cols(t), :], x[:, t, :]).then_inc(out_sem, 16)
            sp.wait_ge(out_sem, 16 * NT)

        @block.vector
        def _(dve):
            steps = [0]

            def link(ins):
                steps[0] += 1
                ins.then_inc(dve_step, 1)
                dve.wait_ge(dve_step, steps[0])

            def stats(kind, i, src, ready):
                link(dve.bn_stats(bn[:, kind, i, :], src))
                link(dve.bn_aggr(mv[:, kind, i, :], bn[:, kind, i, :]))
                v = mv[:, kind, i, 1:2]
                if kind == 0 and i // NT == 1:
                    ins = dve.tensor_scalar(ve[:, kind, i:i + 1], v, 1.0 + RMS_EPS, LN_EPS * RMS_EPS, ALU.mult, ALU.add)
                else:
                    ins = dve.tensor_scalar(ve[:, kind, i:i + 1], v, LN_EPS, None, ALU.add)
                ins.then_inc(ready, 1)

            def pre_stats(p, t):
                if p == 0:
                    dve.wait_ge(x_in[t], 16)
                else:
                    dve.wait_ge(x_ready[p - 1], t + 1)
                stats(0, p * NT + t, x[:, t, :], pre_var[p])

            def pre_norm(p, t):
                i = p * NT + t
                dve.wait_ge(pre_rstd[p], t + 1)
                if t >= 2:
                    dve.wait_ge(tr_done[p], t - 1)
                dve.tensor_scalar(nx[:, int(p == 1), t % 2, :], x[:, t, :], mv[:, 0, i, 0:1], rstd[:, 0, i:i + 1],
                                  ALU.subtract, ALU.mult).then_inc(nx_unscaled if p == 1 else nx_ready[p], 1)

            def pre_lo(p, t):
                hi, lo = tile_transpose(p, t)
                dve.wait_ge(nt_hi_ready[p], t + 1)
                dve.tensor_tensor(lo, TR[p].rearrange("p (k n) -> p k n", k=KC), f32(hi), ALU.subtract)\
                   .then_inc(nt_ready[p], 1)

            def post_stats(p, t, y):
                dve.wait_ge(y_done[p], t + 1 if p != 1 else t // HALF + 1)
                stats(1, p * NT + t, y, post_var[p])

            def wq_low(k):
                dve.wait_ge(wq_hi_ready, k + 1)
                dve.tensor_tensor(wq_lo[:, k, :], wq_raw[:, k, :], f32(wq_hi[:, k, :]), ALU.subtract)\
                   .then_inc(wq_ready, 1)

            def wo_sum(h):
                dve.wait_ge(wo0_in[h % WO_BUFS], 16 * (h // WO_BUFS + 1))
                if h >= 2:
                    dve.wait_ge(wsum_lo_ready, h - 1)
                dve.tensor_reduce(wsum[:, 0], wo0_raw[:, h % WO_BUFS].rearrange("p g n -> p n g"), X, ALU.add)\
                   .then_inc(wsum_ready[0], 1)

            def wo_low(h):
                dve.wait_ge(wsum_hi_ready, h + 1)
                if h >= 2:
                    dve.wait_ge(mw_done, h - 1)
                dve.tensor_tensor(wsum_lo[:, h % 2], wsum[:, h % 2], f32(wsum_hi[:, h % 2]), ALU.subtract)\
                   .then_inc(wsum_lo_ready, 1)

            def mw_low(h):
                dve.wait_ge(mw_hi_ready, h + 1)
                dve.tensor_tensor(mw_lo[:, h, :], Y0[h % 2], f32(mw_hi[:, h, :]), ALU.subtract).then_inc(mw_ready, 1)

            def q_bias(t):
                dve.wait_ge(q0_done, t + 1)
                if t == 0:
                    dve.wait_ge(bz_in, 32)
                if t:
                    dve.wait_ge(q0_exp, t)
                    dve.wait_ge(q0_relu, t)
                dve.tensor_tensor(q0[:], Q0.rearrange("p a n -> p (a n)"), bq_b[:], ALU.add).then_inc(q0_ready, 1)

            def sigma(t):
                dve.wait_ge(q0_exp, t + 1)
                dve.wait_ge(q0_relu, t + 1)
                if t >= 2:
                    dve.wait_ge(sigt_done, t - 1)
                dve.scalar_tensor_tensor(sig[:, t % 2, :], e0[:], 1.0, q0[:], ALU.min, ALU.add).then_inc(sig_ready, 1)

            def denominator(t):
                dve.wait_ge(prod_ready, t + 1)
                link(dve.tensor_reduce(den[:, t, 0, :], prod[:].rearrange("p (h d) -> p h d", h=H0), X, ALU.add))
                link(dve.tensor_scalar(den[:, t, 1, :], den[:, t, 0, :], DEN_EPS, None, ALU.add))
                dve.reciprocal(den[:, t, 2, :], den[:, t, 1, :]).then_inc(den_ready, 1)

            def sig_low(t):
                dve.wait_ge(sigt_hi_ready, t + 1)
                dve.tensor_tensor(sigt_lo[:], SIGT.rearrange("p a (h n) -> p (a h) n", h=H0 // 2), f32(sigt_hi[:]),
                                  ALU.subtract).then_inc(sigt_ready, 1)

            def hidden(c):
                dve.wait_ge(silu_ready, c + 1)
                dve.wait_ge(u_done, c + 1)
                if c >= 2:
                    dve.wait_ge(hid_ready, c - 1)
                dve.tensor_tensor(hid[:, c % 2, :], silu[:, c % 2, :], UP, ALU.mult).then_inc(hid_f_ready, 1)

            def hidden_low(c):
                dve.wait_ge(hid_hi_ready, c + 1)
                dve.tensor_tensor(hid_lo[:, c % 2, :], hid[:, c % 2, :], f32(hid_hi[:, c % 2, :]), ALU.subtract)\
                   .then_inc(hid_ready, 1)

            pre_stats(0, 0)
            pre_norm(0, 0)
            pre_stats(0, 1)
            wq_low(0)
            pre_lo(0, 0)
            pre_norm(0, 1)
            for k in range(1, KC):
                wq_low(k)
            pre_lo(0, 1)
            dve.wait_ge(m_hi_ready, 1)
            dve.tensor_tensor(m_lo[:], m_raw[:], f32(m_hi[:]), ALU.subtract).then_inc(m_ready, 1)
            dve.wait_ge(mask_in, 16)
            dve.tensor_copy(masks[:], mask_raw[:]).then_inc(mask_ready, 1)
            for i in range(NT + 2):
                if 2 <= i:
                    sig_low(i - 2)
                if 3 <= i:
                    pre_stats(1, i - 3)
                if i + 2 < NT:
                    pre_stats(0, i + 2)
                if 3 <= i:
                    pre_norm(1, i - 3)
                if i == NT + 1:
                    hidden(0)
                first, last = (HEADS_AT[i], HEADS_AT[i + 1]) if i < 3 else (0, 0)
                for h in range(first, last):
                    if h % 2 == 0:
                        wo_sum(h)
                    if h - first < 2:
                        wo_low(h)
                if i < NT:
                    q_bias(i)
                if i + 2 < NT:
                    pre_norm(0, i + 2)
                if i < NT:
                    sigma(i)
                for h in range(first, last):
                    mw_low(h)
                    if h + 2 < last:
                        wo_low(h + 2)
                if 2 <= i:
                    post_stats(0, i - 2, Y0[i % 2])
                if 3 <= i:
                    pre_lo(1, i - 3)
                if i + 2 < NT:
                    pre_lo(0, i + 2)
                if i < NT:
                    denominator(i)

            def y1(t):
                return Y1[:, t % HALF, :]

            hidden_low(0)
            for c in range(1, 2 * NJ):
                turned = c - NJ - 4
                if c == 1:
                    pre_stats(1, NT - 1)
                    pre_norm(1, NT - 1)
                hidden(c)
                if c == 1:
                    pre_lo(1, NT - 1)
                if 0 <= turned + 1 < HALF:
                    pre_norm(2, turned + 1)
                if 0 <= turned < HALF:
                    pre_lo(2, turned)
                hidden_low(c)
                if c == NJ:
                    for t in range(HALF):
                        post_stats(1, t, y1(t))
                if 0 <= turned + 2 < HALF:
                    pre_stats(2, turned + 2)
            for t in range(HALF, NT):
                post_stats(1, t, y1(t))
            for p in range(2):
                dve.memset(f32(kt[STK * (1 - p):STK * (2 - p), p, :]), 0.0).then_inc(pads_ready, 1)

            def q_low(t):
                dve.wait_ge(q_hi_ready, t + 1)
                s = qs[:, t % 2, :, :]
                dve.scalar_tensor_tensor(s[:, :, QLO:QLO + D1], QP.rearrange("p (h d) -> p h d", d=D1), SCALE,
                                         f32(s[:, :, QHI:QHI + D1]), ALU.mult, ALU.subtract).then_inc(qs_ready, 1)

            def k_low(t):
                dve.wait_ge(k_hi_ready, t + 1)
                for r in range(2):
                    ins = dve.tensor_tensor(ks[:, t % 2, r, QHI + D1:QLO], KVP[:, 0:D1],
                                            f32(ks[:, t % 2, r, QHI:QHI + D1]), ALU.subtract)
                    ins.then_inc(ks_ready, 1)

            def q_turned(t):
                for g in (1, 3):
                    dve.wait_ge(qtr_done, 4 * t + g + 1)
                    dve.tensor_copy(qt[:, 4 * g:4 * g + 4, cols(t)],
                                    STKT[g % 2].rearrange("p (j n) -> p j n", j=4)).then_inc(qt_dve, 1)

            def row_maxima(t, n):
                b = t % 2
                use = s1_base[t] + n
                if n < len(pieces[t]):
                    q, j, nh, k0, kw, part = pieces[t][n]
                    dve.wait_ge(s1_done, use + 1)
                    if n == 0 and t >= 2:
                        dve.wait_ge(shift_ready, t - 1)
                    dve.tensor_reduce(rowmax[:, b, part, q, j:j + nh],
                                      S1[use % S1_BUFS][:, 0:nh * kw].rearrange("p (h k) -> p h k", h=nh), X, ALU.max)\
                       .then_inc(s1_read, 1)
                    if n < len(pieces[t]) - 1:
                        return
                    dve.wait_ge(s1_read, use + 1)
                    m = rowmax[:, b, 0, :]
                    if (t + 1) * P > BANK:
                        link(dve.tensor_tensor(wshift[:, b, 0, :], rowmax[:, b, 0, :], rowmax[:, b, 1, :], ALU.max))
                        m = wshift[:, b, 0, :]
                    link(dve.tensor_tensor(wshift[:, b, 1, :], w0[:, t, :], m, ALU.subtract))
                    w = wshift[:, b, 1, :]
                    link(dve.tensor_copy(shift[:, b, :, 0, :].bitcast(F32R), w))
                    dve.tensor_tensor(shift[:, b, :, 1, :], w, shift[:, b, :, 0, :], ALU.subtract)\
                       .then_inc(shift_ready, 1)
                else:
                    dve.wait_ge(s1_done, use + 1)
                    if t >= 2:
                        dve.wait_ge(shift_in[b], 64 * (t // 2))
                    dve.tensor_copy(shift_t[:, b, :], S1[use % S1_BUFS][0:STK, 0:P]).then_inc(s1_read, 1)
                    dve.wait_ge(s1_read, use + 1)
                    dve.sem_inc(shift_t_ready, 1)

            for t in range(NT + 1):
                if t < NT:
                    if 1 <= t <= HALF:
                        pre_stats(2, t + HALF - 1)
                    q_low(t)
                    k_low(t)
                    if 1 <= t <= HALF:
                        pre_norm(2, t + HALF - 1)
                if t >= 1:
                    q_turned(t - 1)
                if 1 <= t <= HALF:
                    pre_lo(2, t + HALF - 1)
                for item in early[t]:
                    row_maxima(*item)

            def back(t, step):
                if step in ("norm0", "norm1"):
                    q = int(step == "norm1")
                    dve.wait_ge(bg_o, 2 * t + q + 1)
                    o = BG.rearrange("p (i g v) -> p i g v", i=4, g=4)
                    r = rsum[:, t % 2, q, :].rearrange("p (i g) -> p i g", i=4)
                    link(dve.reciprocal(r, o[:, :, :, D1]))
                    to = attn.rearrange("p (g i q d) -> p i g q d", g=4, i=4, q=2)[:, :, :, q, :]
                    dve.tensor_tensor(to, o[:, :, :, 0:D1], r.unsqueeze(3).broadcast_to([P, 4, 4, D1]), ALU.mult)\
                       .then_inc(bg_o_read, 1)
                elif step == "low":
                    dve.wait_ge(at_hi_ready, t + 1)
                    dve.tensor_tensor(at_lo, BG.rearrange("p (k n) -> p k n", k=KC), f32(at_hi), ALU.subtract)\
                       .then_inc(bg_a_read, 1)
                elif step == "stats":
                    post_stats(2, t, BG)
                elif step == "stats3":
                    pre_stats(3, t)
                elif step == "norm3":
                    pre_norm(3, t)
                elif step == "low3":
                    pre_lo(3, t)

            def gates(t):
                dve.wait_ge(l3_done, t + 1)
                l = logit[:, t % 2, :]
                link(dve.tensor_copy(l, L3[t % 2][:, 0:NE]))
                link(dve.max(top[:, t, :], l))
                dve.tensor_tensor(prob[:, t, 0:1], top[:, t, 1:2], top[:, t, 0:1], ALU.subtract).then_inc(gap_ready, 1)
                link(dve.max_index(topi[:, t, :], top[:, t, :], l))
                link(dve.tensor_copy(top[:, t, 0:2], topi[:, t, 0:2]))
                dve.wait_ge(gap_exp, t + 1)
                pr = prob[:, t, :]
                link(dve.tensor_scalar(pr[:, 2:3], pr[:, 1:2], 1.0, None, ALU.add))
                link(dve.reciprocal(pr[:, 3:4], pr[:, 2:3]))
                link(dve.tensor_scalar(pr[:, 4:5], pr[:, 3:4], SCALING, None, ALU.mult))
                link(dve.tensor_scalar(pr[:, 5:6], pr[:, 1:2], pr[:, 4:5], None, ALU.mult))
                link(dve.tensor_scalar(gate[:, t % 2, 0, :], iota[:], top[:, t, 0:1], pr[:, 4:5], ALU.is_equal, ALU.mult))
                link(dve.tensor_scalar(gate[:, t % 2, 1, :], iota[:], top[:, t, 1:2], pr[:, 5:6], ALU.is_equal, ALU.mult))
                link(dve.tensor_tensor(gate[:, t % 2, 2, :], gate[:, t % 2, 0, :], gate[:, t % 2, 1, :], ALU.add))
                if t >= 2:
                    dve.wait_ge(ht_done, t - 1)
                dve.tensor_tensor(hs[:, t % 2, :].rearrange("p (e r) -> p e r", e=NE),
                                  L3[t % 2][:, NE:LG].rearrange("p (e r) -> p e r", e=NE),
                                  gate[:, t % 2, 2, :].unsqueeze(2).broadcast_to([P, NE, RANK]), ALU.mult)\
                   .then_inc(hs_ready, 1)

            def h_low(t):
                dve.wait_ge(ht_hi_ready, t + 1)
                dve.tensor_tensor(ht_lo[:, t % 2], HT[0:ER // 2, :].rearrange("p (c n) -> p c n", c=2),
                                  f32(ht_hi[:, t % 2]), ALU.subtract).then_inc(ht_ready, 1)

            def experts(e):
                i = e // 2
                if e % 2 == 0:
                    if i < NT:
                        gates(i)
                else:
                    if 3 <= i:
                        post_stats(3, i - 3, O3[(i - 3) % 4])
                    if 1 <= i <= NT:
                        h_low(i - 1)

            for t, kb, p, after, steps_back, e in slots:
                for g in range(4):
                    for u, step in steps_back[g]:
                        back(u, step)
                    for item in after[g]:
                        row_maxima(*item)
                for u, step in steps_back[4]:
                    back(u, step)
                if e is not None:
                    experts(e)

        @block.scalar
        def _(act):
            def split_hi(dst, src, sem_, scale=1.0):
                act.activation(dst, src, ACT.Copy, scale=scale).then_inc(sem_, 1)

            def pre_hi(p, t):
                hi, _ = tile_transpose(p, t)
                act.wait_ge(tr_done[p], t + 1)
                if p == 0 and t >= 2:
                    act.wait_ge(q0_done, t - 1)
                split_hi(hi, TR[p].rearrange("p (k n) -> p k n", k=KC), nt_hi_ready[p])

            def post_apply(p, t, y):
                i = p * NT + t
                act.wait_ge(post_rstd[p], t + 1)
                if p == 1:
                    if t >= HALF:
                        act.wait_ge(x_ready[p], t - HALF + 1)
                elif t >= 2:
                    act.wait_ge(x_ready[p], t - 1)
                act.activation(delta_of(p, t), y, ACT.Identity, bias=mv[:, 1, i, 0:1],
                               scale=rstd[:, 1, i:i + 1]).then_inc(delta_ready[p], 1)

            act.wait_ge(wq_in[0], 16)
            split_hi(wq_hi[:, 0, :], wq_raw[:, 0, :], wq_hi_ready)
            pre_hi(0, 0)
            for k in range(1, KC):
                act.wait_ge(wq_in[k], 16)
                split_hi(wq_hi[:, k, :], wq_raw[:, k, :], wq_hi_ready)
            pre_hi(0, 1)
            act.wait_ge(m_in, 16)
            split_hi(m_hi[:], m_raw[:], m_hi_ready)

            def sig_high(t):
                act.wait_ge(sigt_done, t + 1)
                if t:
                    act.wait_ge(y_done[0], t)
                split_hi(sigt_hi[:], SIGT.rearrange("p a (h n) -> p (a h) n", h=H0 // 2), sigt_hi_ready)

            def weight_hi(c):
                act.wait_ge(wf_in[c % RAW_BUFS], 16 * (c // RAW_BUFS + 1))
                if c >= WBUFS:
                    act.wait_ge(down_done, c - WBUFS + 1)
                elif c == 0:
                    act.wait_ge(q0_done, NT)
                split_hi(wf_hi[:, c % WBUFS, :], wf_raw[:, c % RAW_BUFS, :], wf_hi_ready)

            def gate_silu(c):
                act.wait_ge(g_done, c + 1)
                if c >= 2:
                    act.wait_ge(hid_f_ready, c - 1)
                act.activation(silu[:, c % 2, :], GATE, ACT.Silu).then_inc(silu_ready, 1)

            for i in range(NT + 2):
                if 2 <= i:
                    sig_high(i - 2)
                if 1 <= i <= NT:
                    act.wait_ge(den_ready, i)
                    for h in range(H0):
                        w = slice(h * D0, (h + 1) * D0)
                        s = sig[:, (i - 1) % 2, w]
                        ins = act.activation(s, s, ACT.Copy, scale=den[:, i - 1, 2, h:h + 1])
                    ins.then_inc(sig_scaled, 1)
                first, last = (HEADS_AT[i], HEADS_AT[i + 1]) if i < 3 else (0, 0)

                def wsum_high(h):
                    act.wait_ge(wsum_ready[h % 2], h // 2 + 1)
                    if h >= 2:
                        act.wait_ge(mw_done, h - 1)
                    split_hi(wsum_hi[:, h % 2], wsum[:, h % 2], wsum_hi_ready)

                for h in range(first, min(first + 2, last)):
                    wsum_high(h)
                if i < NT:
                    act.wait_ge(q0_ready, i + 1)
                    if i:
                        act.wait_ge(sig_ready, i)
                    act.activation(e0[:], q0[:], ACT.Exp).then_inc(q0_exp, 1)
                    act.activation(q0[:], q0[:], ACT.Relu).then_inc(q0_relu, 1)
                for h in range(first, last):
                    act.wait_ge(mw_done, h + 1)
                    split_hi(mw_hi[:, h, :], Y0[h % 2], mw_hi_ready)
                    if h + 2 < last:
                        wsum_high(h + 2)
                if i == NT + 1:
                    gate_silu(0)
                if 3 <= i:
                    pre_hi(1, i - 3)
                if i + 2 < NT:
                    pre_hi(0, i + 2)
                if 2 <= i:
                    post_apply(0, i - 2, Y0[i % 2])
                if NT - 1 <= i <= NT:
                    weight_hi(i - NT + 1)

            for c in range(2 * NJ):
                if c:
                    gate_silu(c)
                if c == 1:
                    pre_hi(1, NT - 1)
                if c + 2 < 2 * NJ:
                    weight_hi(c + 2)
                if 0 <= c - NJ - 4 < HALF:
                    pre_hi(2, c - NJ - 4)
                act.wait_ge(hid_f_ready, c + 1)
                if c >= 2:
                    act.wait_ge(down_done, c - 1)
                split_hi(hid_hi[:, c % 2, :], hid[:, c % 2, :], hid_hi_ready)
                if 8 <= c < 8 + KC:
                    act.wait_ge(wkv_in, 16)
                    split_hi(wkv_hi[:, c - 8], wkv_raw[:, c - 8], wkv_hi_ready)
                if c == NJ:
                    for t in range(HALF):
                        post_apply(1, t, Y1[:, t, :])

            for t in range(HALF, NT):
                post_apply(1, t, Y1[:, t - HALF, :])
            for t in range(NT + 1):
                if t < NT:
                    s = qs[:, t % 2, :, :]
                    act.wait_ge(qkv_done, t + 1)
                    if t == 0:
                        act.wait_ge(pads_ready, 5)
                    if t >= 2:
                        act.wait_ge(qtr_done, 4 * (t - 1))
                    q = QP.rearrange("p (h d) -> p h d", d=D1)
                    act.activation(s[:, :, QHI:QHI + 2 * D1].rearrange("p h (r d) -> p h r d", r=2),
                                   q.unsqueeze(2).broadcast_to([P, H1, 2, D1]), ACT.Copy, scale=SCALE)\
                       .then_inc(q_hi_ready, 1)
                    if t >= 2:
                        act.wait_ge(ktr_done, t - 1)
                    kk = ks[:, t % 2, :, :]
                    act.activation(vals[:, t, 0:D1], KVP[:, D1:2 * D1], ACT.Copy).then_inc(v_ready, 1)
                    act.activation(kk[:, :, QHI:QHI + D1], KVP[:, 0:D1].unsqueeze(1).broadcast_to([P, 2, D1]), ACT.Copy)\
                       .then_inc(act_step, 1)
                    act.activation(kk[:, :, QLO:QLO + D1], KVP[:, 0:D1].unsqueeze(1).broadcast_to([P, 2, D1]), ACT.Copy)\
                       .then_inc(k_hi_ready, 1)
                if t >= 1:
                    u = t - 1
                    act.wait_ge(ktr_done, u + 1)
                    for p in range(2):
                        r = slice(STK * p, STK * (p + 1))
                        act.activation(kt[r, p, cols(u)], STKT[0][r, 0:P], ACT.Copy).then_inc(kt_ready, 1)
                    for g in (0, 2):
                        act.wait_ge(qtr_done, 4 * u + g + 1)
                        act.activation(qt[:, 4 * g:4 * g + 4, cols(u)],
                                       STKT[g % 2].rearrange("p (j n) -> p j n", j=4), ACT.Copy).then_inc(qt_act, 1)
                if 1 <= t <= HALF:
                    pre_hi(2, t + HALF - 1)

            def back(t, step):
                if step == "copy":
                    act.wait_ge(pv_done, batch_base[t] + 2 * (t + 1))
                    if t:
                        act.wait_ge(bg_o, 2 * t)
                    act.activation(o_sb[:], PV, ACT.Copy).then_inc(o_read, 1)
                elif step == "high":
                    act.wait_ge(bg_a, t + 1)
                    if t:
                        act.wait_ge(y_done[2], t)
                    split_hi(at_hi, BG.rearrange("p (k n) -> p k n", k=KC), at_hi_ready)
                elif step == "apply":
                    post_apply(2, t, BG)
                elif step == "high3":
                    pre_hi(3, t)

            def experts(e):
                i = e // 2
                if e % 2 == 0:
                    if i < NT:
                        act.wait_ge(gap_ready, i + 1)
                        act.activation(prob[:, i, 1:2], prob[:, i, 0:1], ACT.Exp).then_inc(gap_exp, 1)
                else:
                    if 1 <= i <= NT:
                        t = i - 1
                        act.wait_ge(ht_done, t + 1)
                        if t >= 2:
                            act.wait_ge(y_done[3], t - 1)
                        split_hi(ht_hi[:, t % 2], HT[0:ER // 2, :].rearrange("p (c n) -> p c n", c=2), ht_hi_ready)
                    if 3 <= i:
                        post_apply(3, i - 3, O3[(i - 3) % 4])

            batch = 0
            for t, kb, p, after, steps_back, e in slots:
                for g in range(4):
                    for u, step in steps_back[g]:
                        back(u, step)
                    if t is not None:
                        use = 4 * batch + g
                        act.wait_ge(s2_done, use + 1)
                        if batch >= P_BUFS // 4 and g == 0:
                            act.wait_ge(pv_done, batch - P_BUFS // 4 + 1)
                        act.activation(probs[:, use % P_BUFS, :], s2_bank(use), ACT.Exp).then_inc(p_ready, 1)
                batch += t is not None
                if e is not None:
                    experts(e)

        @block.gpsimd
        def _(pool):
            steps = [0]

            def link(ins):
                steps[0] += 1
                ins.then_inc(pool_step, 1)
                pool.wait_ge(pool_step, steps[0])

            def power(dst, src):
                return pool.tensor_tensor(dst, src, mhalf[:], ALU.pow)

            def pre_scale(p, t):
                i = p * NT + t
                pool.wait_ge(pre_var[p], t + 1)
                power(rstd[:, 0, i:i + 1], ve[:, 0, i:i + 1]).then_inc(pre_rstd[p], 1)

            def weigh(t):
                pool.wait_ge(nx_unscaled, t + 1)
                n = nx[:, 1, t % 2, :]
                pool.tensor_tensor(n, n, lnw[:], ALU.mult).then_inc(nx_ready[1], 1)

            def post_scale(p, t):
                i = p * NT + t
                pool.wait_ge(post_var[p], t + 1)
                link(power(rstd[:, 1, i:i + 1], ve[:, 1, i:i + 1]))
                m = mv[:, 1, i, 0:1]
                pool.tensor_scalar(m, m, rstd[:, 1, i:i + 1], -1.0, ALU.mult, ALU.mult).then_inc(post_rstd[p], 1)

            def add(p, t):
                pool.wait_ge(delta_ready[p], t + 1)
                pool.tensor_tensor(x[:, t, :], x[:, t, :], delta_of(p, t), ALU.add).then_inc(x_ready[p], 1)

            link(pool.memset(mhalf[:], -0.5))
            link(pool.memset(vals[:], 0.0))
            pool.memset(vals[:, :, D1:D1 + 1], 1.0).then_inc(pads_ready, 1)
            pool.wait_ge(lnw_in, 16)
            pre_scale(0, 0)
            pre_scale(0, 1)

            def weight_lo(c):
                pool.wait_ge(wf_hi_ready, c + 1)
                b, r = c % WBUFS, c % RAW_BUFS
                pool.tensor_tensor(wf_lo[:, b, :], wf_raw[:, r, :], f32(wf_hi[:, b, :]), ALU.subtract)\
                    .then_inc(wf_ready, 1)

            def wo_sum(h):
                b = h % WO_BUFS
                pool.wait_ge(wo0_in[b], 16 * (h // WO_BUFS + 1))
                w = wo0_raw[:, b]
                pool.tensor_tensor(w[:, 0:2], w[:, 0:2], w[:, 2:4], ALU.add).then_inc(wo_half, 1)
                pool.wait_ge(wo_half, h // 2 + 1)
                if h >= 2:
                    pool.wait_ge(wsum_lo_ready, h - 1)
                pool.tensor_tensor(wsum[:, 1], w[:, 0], w[:, 1], ALU.add).then_inc(wsum_ready[1], 1)

            for i in range(NT + 2):
                for h in range(HEADS_AT[min(i, 3)], HEADS_AT[min(i + 1, 3)]):
                    if h % 2:
                        wo_sum(h)
                if 3 <= i:
                    pre_scale(1, i - 3)
                if i + 2 < NT:
                    pre_scale(0, i + 2)
                if 3 <= i:
                    weigh(i - 3)
                if i < NT:
                    pool.wait_ge(sig_ready, i + 1)
                    if i:
                        pool.wait_ge(den_ready, i)
                    pool.tensor_tensor(prod[:], sig[:, i % 2, :], z_b[:], ALU.mult).then_inc(prod_ready, 1)
                if 2 <= i:
                    post_scale(0, i - 2)
                    add(0, i - 2)
                if NT - 1 <= i <= NT:
                    weight_lo(i - NT + 1)

            for c in range(2 * NJ):
                if c == 1:
                    pre_scale(1, NT - 1)
                    weigh(NT - 1)
                if c >= 2:
                    weight_lo(c)
                if c == NJ + 1:
                    for t in range(HALF):
                        post_scale(1, t)
                if 0 <= c - NJ - 2 < HALF:
                    add(1, c - NJ - 2)
                if 9 <= c < 9 + KC:
                    k = c - 9
                    pool.wait_ge(wkv_hi_ready, k + 1)
                    pool.tensor_tensor(wkv_lo[:, k], wkv_raw[:, k], f32(wkv_hi[:, k]), ALU.subtract)\
                        .then_inc(wkv_ready, 1)
                if c == 9 + KC:
                    pool.memset(f32(qs[:, :, :, QLO + D1:STK]), 0.0).then_inc(pads_ready, 1)
                if 0 <= c - NJ - 4 < HALF:
                    pre_scale(2, c - NJ - 4)

            pool.wait_ge(hid_ready, 2 * NJ)
            pool.wait_ge(down_done, 2 * NJ)
            pool.memset(f32(ks[:, :, :, QLO + D1:STK]), 0.0).then_inc(pads_ready, 1)
            for t in range(HALF, NT):
                post_scale(1, t)
            for t in range(HALF, NT):
                add(1, t)
            for t in range(NT):
                b = t % 2
                if t >= 2:
                    pool.wait_ge(qtr_done, 4 * (t - 1))
                    pool.wait_ge(ktr_done, t - 1)
                if t == 0:
                    pool.wait_ge(tab_in, 64)
                pool.tensor_copy(qs[:, b, :, 0:BIAS_ROWS], qbias[:, t]).then_inc(qs_bias, 1)
                pool.tensor_copy(ks[:, b, :, 0:BIAS_ROWS],
                                 kbias[:, t, :].unsqueeze(1).broadcast_to([P, 2, BIAS_ROWS])).then_inc(qs_bias, 1)
                if 1 <= t <= HALF:
                    pre_scale(2, t + HALF - 1)
            pool.wait_ge(wo1_in, 16)
            pool.wait_ge(qkv_done, NT)
            pool.tensor_copy(wo1_hi[:], wo1_raw[:]).then_inc(wo1_hi_ready, 1)
            pool.wait_ge(wo1_hi_ready, 1)
            pool.tensor_tensor(wo1_lo[:], wo1_raw[:], f32(wo1_hi[:]), ALU.subtract).then_inc(wo1_ready, 1)

            def expert_weights(k):
                pool.wait_ge(we_in[k % 2], 16 * (k // 2 + 1))
                pool.tensor_copy(we_hi[:, k, :], we_raw[:, k % 2, :]).then_inc(we_hi_ready, 1)
                pool.wait_ge(we_hi_ready, k + 1)
                pool.tensor_tensor(we_lo[:, k, :], we_raw[:, k % 2, :], f32(we_hi[:, k, :]), ALU.subtract)\
                    .then_inc(we_ready, 1)

            def adapter_weights(c):
                pool.wait_ge(lb_in, 16 * (c + 1))
                pool.tensor_copy(lb_hi[:, c, :], lb_raw[:]).then_inc(lb_hi_ready, 1)
                pool.wait_ge(lb_hi_ready, c + 1)
                pool.tensor_tensor(lb_lo[:, c, :], lb_raw[:], f32(lb_hi[:, c, :]), ALU.subtract).then_inc(lb_ready, 1)

            for t, kb, p, after, steps_back, e in slots:
                for g in range(5):
                    for u, step in steps_back[g]:
                        if step == "stats":
                            post_scale(2, u)
                        elif step == "apply":
                            add(2, u)
                            if u in (1, 2, 4, 5):
                                expert_weights((1, 2, 4, 5).index(u))
                            if u in (5, 6):
                                adapter_weights(u - 5)
                        elif step == "stats3":
                            pre_scale(3, u)
                if e is not None and e % 2 and e // 2 >= 3:
                    post_scale(3, e // 2 - 3)
                    add(3, e // 2 - 3)

        @block.tensor
        def _(pe):
            def product(dst, hi, lo, w_hi, w_lo, first, last):
                pe.matmul(dst, hi, w_hi, start=first, stop=False, skip_group_check=True)
                pe.matmul(dst, hi, w_lo, start=False, stop=False, skip_group_check=True)
                return pe.matmul(dst, lo, w_hi, start=False, stop=last, skip_group_check=True)

            def turn(dst, src):
                return pe.transpose(dst, src, ident[:])

            def pre_turn(p, t):
                pe.wait_ge(nx_ready[p], t + 1)
                if t:
                    pe.wait_ge(nt_ready[p], t)
                for k in range(KC):
                    ins = turn(TR[p][:, k * P:(k + 1) * P], nx[:, int(p == 1), t % 2, k * P:(k + 1) * P])
                ins.then_inc(tr_done[p], 1)

            def gate_up(c, part):
                b = c % WBUFS
                tok = slice(c // NJ * HALF * P, (c // NJ + 1) * HALF * P)
                pe.wait_ge(wf_ready, c + 1)
                if c % NJ == 0:
                    pe.wait_ge(nt_ready[1], HALF * (c // NJ + 1))
                dst, start, free, done = ((GATE, GW, silu_ready, g_done), (UP, UW, hid_f_ready, u_done))[part]
                if c:
                    pe.wait_ge(free, c)
                else:
                    pe.wait_ge(q0_ready, NT)
                for k in range(KC):
                    w = slice(start + k * P, start + (k + 1) * P)
                    pe.matmul(dst, wf_hi[:, b, w], mt_hi[:, k, tok], start=(k == 0), stop=False)
                    pe.matmul(dst, wf_hi[:, b, w], mt_lo[:, k, tok], start=False, stop=False)
                    ins = pe.matmul(dst, wf_lo[:, b, w], mt_hi[:, k, tok], start=False, stop=(k == KC - 1))
                ins.then_inc(done, 1)

            pe.wait_ge(id_in, 16)
            pre_turn(0, 0)
            pre_turn(0, 1)
            for i in range(NT + 2):
                if i < NT:
                    pe.wait_ge(nt_ready[0], i + 1)
                    if i:
                        pe.wait_ge(q0_ready, i)
                    for n in range(2):
                        for k in range(KC):
                            if i == 0 and n == 0:
                                pe.wait_ge(wq_ready, k + 1)
                            w = slice(n * HID, (n + 1) * HID)
                            ins = product(Q0[:, n, :], nt_hi[:, i % 2, k], nt_lo[:, i % 2, k],
                                          wq_hi[:, k, w], wq_lo[:, k, w], k == 0, k == KC - 1)
                    ins.then_inc(q0_done, 1)
                if i < 3:
                    if i == 0:
                        pe.wait_ge(m_ready, 1)
                    for h in range(HEADS_AT[i], HEADS_AT[i + 1]):
                        pe.wait_ge(wsum_lo_ready, h + 1)
                        if h >= 2:
                            pe.wait_ge(mw_ready, h - 1)
                        product(Y0[h % 2], m_hi[:, h], m_lo[:, h], wsum_hi[:, h % 2], wsum_lo[:, h % 2], True, True)\
                            .then_inc(mw_done, 1)
                if 2 <= i < NT + 2:
                    t = i - 2
                    pe.wait_ge(sigt_ready, t + 1)
                    if t == 0:
                        pe.wait_ge(mw_ready, H0)
                    if t >= 2:
                        pe.wait_ge(delta_ready[0], t - 1)
                    for h in range(H0):
                        ins = product(Y0[t % 2], sigt_hi[:, h], sigt_lo[:, h], mw_hi[:, h], mw_lo[:, h],
                                      h == 0, h == H0 - 1)
                    ins.then_inc(y_done[0], 1)
                if 3 <= i:
                    pre_turn(1, i - 3)
                if i + 2 < NT:
                    pre_turn(0, i + 2)
                if i == NT:
                    gate_up(0, 0)
                if 1 <= i <= NT:
                    t = i - 1
                    pe.wait_ge(sig_scaled, t + 1)
                    if t:
                        pe.wait_ge(sigt_ready, t)
                    for h in range(H0):
                        ins = turn(SIGT[:, h // 4, (h % 4) * P:(h % 4 + 1) * P], sig[:, t % 2, h * D0:(h + 1) * D0])
                    ins.then_inc(sigt_done, 1)
                if i == NT:
                    gate_up(0, 1)

            def down(c):
                b, j = c % WBUFS, c % NJ
                pe.wait_ge(hid_ready, c + 1)
                w = slice(DW, DW + HID)
                for m in range(HALF):
                    if c == NJ:
                        pe.wait_ge(delta_ready[1], m + 1)
                    ins = product(Y1[:, m, :], hid_hi[:, c % 2, m * P:(m + 1) * P], hid_lo[:, c % 2, m * P:(m + 1) * P],
                                  wf_hi[:, b, w], wf_lo[:, b, w], j == 0, j == NJ - 1)
                ins.then_inc(down_done, 1)
                if j == NJ - 1:
                    pe.wait_ge(down_done, c + 1)
                    pe.sem_inc(y_done[1], 1)

            for c in range(2 * NJ):
                if c:
                    gate_up(c, 0)
                    gate_up(c, 1)
                if c == 1:
                    pe.wait_ge(delta_ready[0], NT)
                    pre_turn(1, NT - 1)
                if 0 <= c - NJ - 4 < HALF:
                    pre_turn(2, c - NJ - 4)
                if c:
                    down(c - 1)
            down(2 * NJ - 1)

            def s1_item(t, n):
                use = s1_base[t] + n
                dst = S1[use % S1_BUFS]
                if use >= S1_BUFS:
                    pe.wait_ge(s1_read, use - S1_BUFS + 1)
                if n == len(pieces[t]):
                    pe.wait_ge(shift_ready, t + 1)
                    pe.transpose(dst[0:STK, 0:P], shift[:, t % 2].rearrange("p q s j -> p (q s j)"), ident[:])\
                      .then_inc(s1_done, 1)
                    return
                q, j, nh, k0, kw, part = pieces[t][n]
                diagonal = k0 + kw == (t + 1) * P
                for i in range(nh):
                    ins = pe.matmul(dst[:, i * kw:(i + 1) * kw], qt[:, j + i, cols(t)], kt[:, q, k0:k0 + kw],
                                    start=(i == 0), stop=not diagonal, skip_group_check=True)
                if diagonal:
                    ins = pe.matmul(dst[:, 0:nh * kw].rearrange("p (h k) -> p h k", h=nh)[:, :, kw - P:kw],
                                    masks[:, 0, :], masks[:, 1, :].unsqueeze(1).broadcast_to([P, nh, P]),
                                    start=False, stop=True, skip_group_check=True)
                ins.then_inc(s1_done, 1)

            pe.wait_ge(wkv_ready, KC)
            for t in range(NT + 1):
                if t < NT:
                    pe.wait_ge(nt_ready[2], t + 1)
                    if t:
                        pe.wait_ge(qs_ready, t)
                        pe.wait_ge(ks_ready, 2 * t)
                        pe.wait_ge(v_ready, t)
                    for dst, w in ((QP, slice(0, HID)), (KVP, slice(HID, HID + 2 * D1))):
                        for k in range(KC):
                            ins = product(dst, mt_hi[:, k, cols(t)], mt_lo[:, k, cols(t)], wkv_hi[:, k, w], wkv_lo[:, k, w],
                                          k == 0, k == KC - 1)
                    ins.then_inc(qkv_done, 1)
                if t >= 1:
                    u = t - 1
                    if u == 0:
                        pe.wait_ge(delta_ready[1], NT)
                    pe.wait_ge(qs_bias, 2 * t)
                    pe.wait_ge(ks_ready, 2 * t)
                    if u:
                        pe.wait_ge(qt_act, 2 * u)
                    turn(STKT[0][:, 0:P], f32(ks[:, u % 2].rearrange("p r c -> p (r c)"))).then_inc(ktr_done, 1)
                    pe.wait_ge(qs_ready, t)
                    if u:
                        pe.wait_ge(qt_dve, 2 * u)
                    for g in range(4):
                        if g == 0:
                            pe.wait_ge(kt_ready, 2 * (u + 1))
                        if g == 2:
                            pe.wait_ge(qt_act, 2 * u + 1)
                        if g == 3:
                            pe.wait_ge(qt_dve, 2 * u + 1)
                        for j in range(4):
                            pair = 4 * g + j
                            ins = turn(STKT[g % 2][:, j * P:(j + 1) * P],
                                       f32(qs[:, u % 2, 2 * pair:2 * pair + 2, :].rearrange("p q c -> p (q c)")))
                        ins.then_inc(qtr_done, 1)
                if 1 <= t <= HALF:
                    pre_turn(2, t + HALF - 1)
                if early[t]:
                    pe.wait_ge(mask_ready, 1)
                    pe.wait_ge(delta_ready[1], NT)
                    last = early[t][-1][0]
                    pe.wait_ge(qt_act, 2 * (last + 1))
                    pe.wait_ge(qt_dve, 2 * (last + 1))
                for item in early[t]:
                    s1_item(*item)

            def s2_piece(use, t, kb, p, g):
                dst = s2_bank(use)
                if use < last_use + 2:
                    if use >= S2_BUFS:
                        pe.wait_ge(p_ready, use - S2_BUFS + 1)
                elif use < last_use + 4:
                    pe.wait_ge(s1_read, s1_base[NT - 1] + len(pieces[NT - 1]) + 1)
                else:
                    pe.wait_ge(p_ready, use - 4 + 1)
                diagonal = kb == t
                ins = pe.matmul(dst, kt[:, p, cols(kb)], qt[:, 4 * g:4 * g + 4, cols(t)],
                                start=True, stop=not diagonal, skip_group_check=True)
                if diagonal:
                    ins = pe.matmul(dst, masks[:, 0, :], masks[:, 2, :].unsqueeze(1).broadcast_to([P, 4, P]),
                                    start=False, stop=True, skip_group_check=True)
                ins.then_inc(s2_done, 1)

            def values(batch, t, kb, p):
                pe.wait_ge(p_ready, 4 * batch + 4)
                if kb == 0 and p == 0 and t:
                    pe.wait_ge(o_read, t)
                for g in range(4):
                    ins = pe.matmul(PV[VW * g:VW * (g + 1), p, :], vals[:, kb, :],
                                    probs[:, (4 * batch + g) % P_BUFS, :], start=(kb == 0), stop=(kb == t),
                                    skip_group_check=True)
                ins.then_inc(pv_done, 1)

            def back(t, step):
                if step in ("turn0", "turn1"):
                    q = int(step == "turn1")
                    if q == 0:
                        pe.wait_ge(o_read, t + 1)
                        if t:
                            pe.wait_ge(delta_ready[2], t)
                        if turned3_before[t]:
                            pe.wait_ge(nt_ready[3], turned3_before[t])
                    else:
                        pe.wait_ge(bg_o_read, 2 * t + 1)
                    for i in range(4):
                        ins = turn(BG[:, i * P:(i + 1) * P], o_sb[:, q, i * P:(i + 1) * P])
                    ins.then_inc(bg_o, 1)
                elif step == "turn2":
                    pe.wait_ge(bg_o_read, 2 * t + 2)
                    for k in range(KC):
                        ins = turn(BG[:, k * P:(k + 1) * P], attn[:, k * P:(k + 1) * P])
                    ins.then_inc(bg_a, 1)
                elif step[:-1] == "project":
                    k = int(step[-1])
                    if k == 0:
                        pe.wait_ge(bg_a_read, t + 1)
                        if t == 0:
                            pe.wait_ge(wo1_ready, 1)
                    ins = product(BG, at_hi[:, k], at_lo[:, k], wo1_hi[:, k], wo1_lo[:, k], k == 0, k == KC - 1)
                    if k == KC - 1:
                        ins.then_inc(y_done[2], 1)
                elif step == "turn3":
                    pe.wait_ge(delta_ready[2], projected_before[t])
                    pre_turn(3, t)

            def experts(e):
                i = e // 2
                if e % 2 == 0 and i < NT:
                    pe.wait_ge(nt_ready[3], i + 1)
                    hi, lo = tile_transpose(3, i)
                    if i == 0:
                        pe.wait_ge(we_ready, KC)
                    if i >= 2:
                        pe.wait_ge(hs_ready, i - 1)
                    for k in range(KC):
                        ins = product(L3[i % 2], hi[:, k], lo[:, k], we_hi[:, k, HID:], we_lo[:, k, HID:],
                                      k == 0, k == KC - 1)
                    ins.then_inc(l3_done, 1)
                    if i >= 4:
                        pe.wait_ge(delta_ready[3], i - 3)
                    for k in range(KC):
                        product(O3[i % 4], hi[:, k], lo[:, k], we_hi[:, k, 0:HID], we_lo[:, k, 0:HID], k == 0, False)
                if e % 2 and 2 <= i < NT + 2:
                    t = i - 2
                    pe.wait_ge(ht_ready, t + 1)
                    if t == 0:
                        pe.wait_ge(lb_ready, 2)
                    for c in range(2):
                        ins = product(O3[t % 4], ht_hi[:, t % 2, c], ht_lo[:, t % 2, c], lb_hi[:, c], lb_lo[:, c],
                                      False, c == 1)
                    ins.then_inc(y_done[3], 1)
                if e % 2 and 1 <= i <= NT:
                    t = i - 1
                    pe.wait_ge(hs_ready, t + 1)
                    if t:
                        pe.wait_ge(ht_ready, t)
                    for c in range(2):
                        ins = turn(HT[0:ER // 2, c * P:(c + 1) * P], hs[:, t % 2, c * (ER // 2):(c + 1) * (ER // 2)])
                    ins.then_inc(ht_done, 1)

            pe.wait_ge(qt_act, 2 * NT)
            pe.wait_ge(qt_dve, 2 * NT)
            batch = 0
            before = None
            for t, kb, p, after, steps_back, e in slots:
                if kb == 0 and p == 0:
                    pe.wait_ge(shift_in[t % 2], 64 * (t // 2 + 1))
                for g in range(4):
                    if g == 3 and before is not None:
                        values(*before)
                    for u, step in steps_back[g]:
                        back(u, step)
                    if t is not None:
                        s2_piece(4 * batch + g, t, kb, p, g)
                    for item in after[g]:
                        s1_item(*item)
                before = (batch, t, kb, p) if t is not None else None
                batch += t is not None
                for u, step in steps_back[4]:
                    back(u, step)
                if e is not None:
                    experts(e)


def layouts(i):
    def hidden_major(w):
        return w.T.reshape(KC, P, w.shape[0]).transpose(1, 0, 2)

    heads = i["L0_attn_Wq"].reshape(H0, G0, D0, HID)[:, 0].reshape(H0 * D0, HID)
    gate, up = (i[f"L0_ffn_{n}_w"].reshape(NJ, P, KC, P).transpose(0, 3, 2, 1).reshape(NJ, P, KC * P)
                for n in ("gate", "up"))
    down = i["L0_ffn_down_w"].T.reshape(NJ, P, HID)
    experts = np.concatenate([i["L1_ffn_base_W"], i["L1_ffn_gate_W"], i["L1_ffn_lora_A"].reshape(ER, HID)])
    return {
        "x": i["L0_attn_hidden_states"],
        "wq": hidden_major(heads),
        "bq": i["L0_attn_bq"].reshape(H0, G0, D0)[:, 0].reshape(1, H0 * D0),
        "z": i["L0_attn_z"].reshape(1, H0 * D0),
        "m": i["L0_attn_M"].transpose(2, 0, 1),
        "wo0": i["L0_attn_Wo"].reshape(HID, H0, G0, D0).transpose(1, 3, 2, 0).reshape(H0, D0, G0 * HID),
        "lnw": i["L0_ffn_ln_w"].reshape(1, HID),
        "wf": np.concatenate([gate, up, down], axis=2),
        "wkv": i["L1_attn_Wqkv"].reshape(KC, P, HID + 2 * D1).transpose(1, 0, 2),
        "wo1": i["L1_attn_Wo"].reshape(KC, P, HID).transpose(1, 0, 2),
        "we": experts.T.reshape(KC, P, HID + LG),
        "lb": i["L1_ffn_lora_B"].transpose(0, 2, 1).reshape(2, ER // 2, HID).transpose(1, 0, 2),
    }


def kernel(**inputs):
    import concourse.bacc as _bacc
    from concourse.bass_utils import run_bass_kernel_spmd as _run

    nc = _bacc.Bacc("TRN2", target_bir_lowering=False, num_devices=1)
    arrays, aps = {}, {}
    for name, a in {**layouts({n: np.asarray(v) for n, v in inputs.items()}), **constants()}.items():
        a = np.ascontiguousarray(a)
        arrays[f"in_{name}"] = a
        aps[name] = nc.dram_tensor(f"in_{name}", a.shape, mybir.dt.from_np(a.dtype), kind="ExternalInput").ap()
    out = nc.dram_tensor("out_0", (1, S, HID), F32, kind="ExternalOutput").ap()
    build(nc, aps, out)
    r = _run(nc, [arrays], core_ids=[0])
    return r.results[0]["out_0"]
```

```python
from contextlib import ExitStack

import numpy as np

import concourse.bass as bass
from concourse import mybir

F32 = mybir.dt.float32
F32R = mybir.dt.float32r
BF16 = mybir.dt.bfloat16
U32 = mybir.dt.uint32
ALU = mybir.AluOpType
ACT = mybir.ActivationFunctionType
X = mybir.AxisListType.X

P = 128
S = 1024
HID = 512
NT = S // P
KC = HID // P
BANK = 512
LN_EPS = 1e-5
H0, D0, G0 = 8, 128, 4
DEN_EPS = 1e-6
INNER = 1792
NJ = INNER // P
RMS_EPS = 1e-5
HALF = 4
WCH = 2 * KC * P + HID
GW, UW, DW = 0, KC * P, 2 * KC * P
RAW_BUFS = 3
WBUFS = 3
WO_BUFS = 4
WSUM_BUFS = 3
HEADS_AT = (0, 2, 5, 8)
H1, D1 = 32, 16
PAIRS = H1 // 2
SCALE = float(D1) ** -0.5
STK = 64
BIAS_ROWS = 6
QHI, QLO = BIAS_ROWS, BIAS_ROWS + 2 * D1
VW = 32
S1_BUFS, S2_BUFS, P_BUFS = 3, 2, 12
LEAD, DELAY = 3, 3
EARLY_FROM = 3
NE, RANK, SCALING = 28, 8, 2.0
ER = NE * RANK
LG = NE + ER

PHASES = 4


def split12(v):
    v = np.asarray(v, np.float32)
    hi = ((v.view(np.uint32) + np.uint32(0x800)) & np.uint32(0xFFFFF000)).view(np.float32)
    return hi, (v - hi).astype(np.float32)


def constants():
    slopes = ((2.0 ** (-(2.0 ** -2.0))) ** np.arange(1, H1 + 1, dtype=np.float64)).astype(np.float32)
    s_hi, s_lo = split12(slopes)
    pos = np.arange(S, dtype=np.float32)
    a_hi, a_lo = split12(-(s_hi[None, :] * pos[:, None]))
    w0 = -(s_lo[None, :] * pos[:, None])
    b_hi, b_lo = split12(w0)
    one = np.ones((S, 1), np.float32)
    q_bias = np.stack([one * s_hi, a_hi, a_lo, one * s_lo, b_hi, b_lo], -1)
    q_bias = q_bias.reshape(NT, P, H1 * BIAS_ROWS).transpose(1, 0, 2)
    k_bias = np.stack([pos, one[:, 0], one[:, 0], pos, one[:, 0], one[:, 0]], -1)
    k_bias = k_bias.reshape(NT, P, BIAS_ROWS).transpose(1, 0, 2)
    w0 = w0.reshape(NT, P, PAIRS, 2).transpose(1, 0, 3, 2)
    c = np.arange(P)
    later = np.where(c[None, :] > c[:, None], np.float32(-1e30), np.float32(0))
    masks = np.stack([np.eye(P, dtype=np.float32), later, later.T])
    return {
        "c_ident": np.eye(P, dtype=np.float32),
        "c_masks": masks.transpose(1, 0, 2),
        "c_qbias": q_bias,
        "c_kbias": k_bias,
        "c_w0": w0,
        "c_iota": np.tile(np.arange(NE, dtype=np.float32), (P, 1)),
    }


def score_pieces(t):
    kw = (t + 1) * P
    out = []
    if kw <= BANK:
        n = BANK // kw
        for j in range(0, PAIRS, n):
            out += [(p, j, n, 0, kw, 0) for p in range(2)]
    else:
        rest = kw - BANK
        n = BANK // rest
        for j in range(0, PAIRS, n):
            out += [(p, j + i, 1, 0, BANK, 0) for i in range(n) for p in range(2)]
            out += [(p, j, n, BANK, rest, 1) for p in range(2)]
    return out


def row_maxima_order():
    order = []
    for t in range(NT):
        items = [(t, n) for n in range(len(score_pieces(t)))]
        if t == 1 or t >= 3:
            order += items[:DELAY] + [(t - 1, len(score_pieces(t - 1)))] + items[DELAY:]
        else:
            order += items
        if t in (1, NT - 1):
            order.append((t, len(items)))
    return order


def attention_slots():
    slots = [[t, kb, p, None, None, None] for t in range(NT) for kb in range(t + 1) for p in range(2)]
    scores = len(slots)
    for e in range(2 * (NT + 3)):
        slots.append([None, None, None, None, None, e])
    for slot in slots:
        slot[3] = [[] for g in range(4)]
        slot[4] = [[] for g in range(5)]

    start = [t * (t + 1) for t in range(NT)]
    left = [item for item in row_maxima_order() if item[0] >= 2]
    due = [left.index((t, len(score_pieces(t)))) + 1 if t >= 2 else 0 for t in range(NT)]
    done, credit = 0, 0.0
    for n in range(4 * (start[NT - 1] - LEAD)):
        even = max((due[t] - done) / (4 * (start[t] - LEAD) - n) for t in range(2, NT) if 4 * (start[t] - LEAD) > n)
        credit += even
        take = min(int(credit + 1e-6), len(left))
        credit -= take
        slots[n // 4][3][n % 4] = left[:take]
        left = left[take:]
        done += take
    for last in left:
        slots[start[NT - 1] - LEAD][3][0].append(last)

    enter, busy, at = [], set(), 0
    for t in range(NT):
        at = max(at, (t + 1) * (t + 2) - 1 + 2)
        enter.append(at)
        busy |= set(range(at, at + 6))
        at += 6
    turn3 = []
    for t in range(NT):
        at = max(enter[t] + 8, start[NT - 1])
        while at in busy:
            at += 1
        busy.add(at)
        turn3.append(at)

    for t in range(NT):
        slots[(t + 1) * (t + 2) + 1][4][0].append((t, "copy"))
        if t < NT - 1:
            steps = (("turn0", 0, 4), ("norm0", 1, 2), ("turn1", 1, 4), ("norm1", 2, 2), ("turn2", 2, 4),
                     ("high", 3, 1), ("low", 3, 3), ("project0", 4, 0), ("project1", 4, 1), ("project2", 4, 2),
                     ("project3", 4, 3), ("stats", 5, 1), ("apply", 6, 0))
            steps3 = (("stats3", -1, 1), ("norm3", 0, 0), ("turn3", 0, 4), ("high3", 1, 1), ("low3", 1, 3))
        else:
            steps = (("turn0", 0, 4), ("norm0", 0, 4), ("turn1", 1, 4), ("norm1", 1, 4), ("turn2", 2, 4),
                     ("high", 2, 4), ("low", 2, 4), ("project0", 3, 4), ("project1", 3, 4), ("project2", 3, 4),
                     ("project3", 3, 4), ("stats", 3, 4), ("apply", 4, 0))
            steps3 = (("stats3", -2, 4), ("norm3", -1, 4), ("turn3", 0, 4), ("high3", 0, 4), ("low3", 0, 4))
        for step, after, place in steps:
            slots[enter[t] + after][4][place].append((t, step))
        for step, after, place in steps3:
            slots[turn3[t] + after][4][place].append((t, step))
    assert turn3[NT - 1] + 1 < scores + 2 * (NT - 1)
    return (slots, [sum(at < e for at in turn3) for e in enter], [sum(e < at for e in enter) for at in turn3])


def build(nc, A, out):
    ctx = ExitStack()
    with ctx:
        def sb(name, shape, dt=F32):
            return ctx.enter_context(nc.sbuf_tensor(name, shape, dt))

        def sem(name):
            return ctx.enter_context(nc.semaphore(name))

        def sems(name, n):
            return [sem(f"{name}{i}") for i in range(n)]

        x = sb("x", [P, NT, HID])
        nx = sb("nx", [P, 2, 2, HID])
        nt_hi = sb("nt_hi", [P, 2, KC, P], F32R)
        nt_lo = sb("nt_lo", [P, 2, KC, P], F32R)
        delta = sb("delta", [P, 2, HID])
        lnw = sb("lnw", [P, HID])
        ident = sb("ident", [P, P])
        masks = sb("masks", [P, 3, P], BF16)
        w0 = sb("w0", [P, NT, 2, PAIRS])
        kbias = sb("kbias", [P, NT, BIAS_ROWS])
        iota = sb("iota", [P, NE])
        bn = sb("bn", [P, 2, PHASES * NT, 6])
        mv = sb("mv", [P, 2, PHASES * NT, 2])
        ve = sb("ve", [P, 2, PHASES * NT])
        rstd = sb("rstd", [P, 2, PHASES * NT])
        mhalf = sb("mhalf", [P, 1])
        den = sb("den", [P, NT, 3, H0])
        rowmax = sb("rowmax", [P, 2, 2, 2, PAIRS])
        wshift = sb("wshift", [P, 2, 2, 2, PAIRS])
        shift = sb("shift", [P, 2, 2, 2, PAIRS])
        shift_t = sb("shift_t", [STK, 2, P], F32R)
        rsum = sb("rsum", [P, 2, 2, PAIRS])
        top = sb("top", [P, NT, 8])
        vals = sb("vals", [P, NT, VW])
        topi = sb("topi", [P, NT, 8], U32)
        prob = sb("prob", [P, NT, 8])
        gate = sb("gate", [P, 2, 3, NE])
        logit = sb("logit", [P, 2, NE])

        kib = 1024
        b_at = nc.sbuf_base
        c_at = b_at + 32 * kib + 512
        room = 158 * kib + 512
        sb("arena", [P, room // 4])

        def at(name, start, kb, shape, dt=F32):
            size = int(np.prod(shape[1:])) * mybir.dt.size(dt)
            assert start + int(kb * kib) + size <= b_at + room, (name, start + kb * kib + size - b_at - room)
            return nc.alloc_sbuf_tensor_at(name, shape, dt, offset=start + int(kb * kib))

        mt_hi = at("mt_hi", b_at, 0, [P, KC, S], F32R)
        mt_lo = at("mt_lo", b_at, 16, [P, KC, S], F32R)
        we_hi = at("we_hi", b_at, 0, [P, KC, HID + LG], F32R)
        we_lo = at("we_lo", b_at, 12, [P, KC, HID + LG], F32R)
        lb_hi = at("lb_hi", b_at, 24, [ER // 2, 2, HID], F32R)
        lb_lo = at("lb_lo", b_at, 28, [ER // 2, 2, HID], F32R)
        wq_hi = at("wq_hi", c_at, 0, [P, KC, H0 * D0], F32R)
        wq_lo = at("wq_lo", c_at, 16, [P, KC, H0 * D0], F32R)
        wo0_raw = at("wo0_raw", b_at, 0, [P, WO_BUFS, G0, HID])
        m_raw = at("m_raw", c_at, 40, [P, H0, D0])
        m_hi = at("m_hi", c_at, 44, [P, H0, D0], F32R)
        m_lo = at("m_lo", c_at, 48, [P, H0, D0], F32R)
        wsum_hi = at("wsum_hi", c_at, 32, [P, WSUM_BUFS, HID], F32R)
        wsum_lo = at("wsum_lo", c_at, 52, [P, WSUM_BUFS, HID], F32R)
        bq_b = at("bq_b", c_at, 58, [P, H0 * D0])
        z_b = at("z_b", c_at, 62, [P, H0 * D0])
        q0 = at("q0", c_at, 66, [P, H0 * D0])
        e0 = at("e0", c_at, 70, [P, H0 * D0])
        sig = at("sig", c_at, 74, [P, 2, H0 * D0])
        prod = at("prod", c_at, 82, [P, H0 * D0])
        sigt_hi = at("sigt_hi", c_at, 86, [P, H0, P], F32R)
        sigt_lo = at("sigt_lo", c_at, 90, [P, H0, P], F32R)
        mw_hi = at("mw_hi", c_at, 94, [P, H0, HID], F32R)
        mw_lo = at("mw_lo", c_at, 110, [P, H0, HID], F32R)
        wq_raw = at("wq_raw", c_at, 110, [P, KC, H0 * D0])
        mask_raw = at("mask_raw", c_at, 94, [P, 3, P])
        wf_hi = at("wf_hi", c_at, 0, [P, WBUFS, WCH], F32R)
        wf_lo = at("wf_lo", c_at, 18, [P, WBUFS, WCH], F32R)
        wf_raw = at("wf_raw", c_at, 36, [P, RAW_BUFS, WCH])
        silu = at("silu", c_at, 58, [P, 2, HALF * P])
        hid = at("hid", c_at, 62, [P, 2, HALF * P])
        hid_hi = at("hid_hi", c_at, 66, [P, 2, HALF * P], F32R)
        hid_lo = at("hid_lo", c_at, 70, [P, 2, HALF * P], F32R)
        wkv_raw = at("wkv_raw", c_at, 80, [P, KC, HID + 2 * D1])
        wkv_hi = at("wkv_hi", c_at, 89, [P, KC, HID + 2 * D1], F32R)
        wkv_lo = at("wkv_lo", c_at, 97.5, [P, KC, HID + 2 * D1], F32R)
        qbias = at("qbias", c_at, 74, [P, NT, H1, BIAS_ROWS])
        qs = at("qs", c_at, 106, [P, 2, H1, STK], F32R)
        qt = at("qt", c_at, 0, [P, PAIRS, S], F32R)
        kt = at("kt", c_at, 64, [P, 2, S], F32R)
        ks = at("ks", c_at, 72, [P, 2, 2, STK], F32R)
        wo1_raw = at("wo1_raw", c_at, 72, [P, KC, HID])
        wo1_hi = at("wo1_hi", c_at, 80, [P, KC, HID], F32R)
        wo1_lo = at("wo1_lo", c_at, 88, [P, KC, HID], F32R)
        probs = at("probs", c_at, 98, [P, P_BUFS, BANK])
        o_sb = at("o_sb", c_at, 122, [P, 2, BANK])
        we_raw = at("we_raw", c_at, 72, [P, 2, HID + LG])
        lb_raw = at("lb_raw", c_at, 78, [ER // 2, HID])
        hs = at("hs", c_at, 98, [P, 2, ER])
        ht_hi = at("ht_hi", c_at, 102, [ER // 2, 2, 2, P], F32R)
        ht_lo = at("ht_lo", c_at, 106, [ER // 2, 2, 2, P], F32R)
        attn = nx[:, 1, 0, :]
        at_hi, at_lo = nt_hi[:, 0], nt_lo[:, 0]
        delta3 = at("delta3", c_at, 110, [P, 2, HID])

        psum = ctx.enter_context(nc.psum_tensor("psum", [P, 8, BANK], F32))
        TR = [psum[:, b, :] for b in (6, 7, 6, 4)]
        Q0, SIGT, Y0 = psum[:, 0:2, :], psum[:, 2:4, :], [psum[:, 4, :], psum[:, 5, :]]
        GATE, UP, Y1 = psum[:, 0, :], psum[:, 1, :], psum[:, 2:6, :]
        QP, KVP, STKT = [psum[:, 0, :], psum[:, 1, :]], psum[:, 7, 0:2 * D1], [psum[:, 4, :], psum[:, 5, :]]
        S1 = [psum[:, b, :] for b in (2, 3, 7)]
        S2 = [psum[:, b, :] for b in range(4)]
        PV, BG = psum[:, 5:7, :], psum[:, 4, :]
        O3, L3 = [psum[:, b, :] for b in (0, 1, 5, 6)], [psum[:, 2, 0:LG], psum[:, 3, 0:LG]]
        HT = psum[:, 7, 0:2 * P]

        x_in = sems("x_in", NT)
        id_in, mask_in, bz_in, m_in, tab_in, lnw_in = map(sem, ("id_in", "mask_in", "bz_in", "m_in", "tab_in", "lnw_in"))
        wq_in = sems("wq_in", KC)
        wo0_in = sems("wo0_in", WO_BUFS)
        wf_in = sems("wf_in", RAW_BUFS)
        wkv_in, wo1_in, lb_in = sem("wkv_in"), sem("wo1_in"), sem("lb_in")
        we_in = sems("we_in", 2)
        pre_var, pre_rstd, nx_ready, tr_done, nt_hi_ready, nt_ready = (
            sems(n, PHASES) for n in ("pre_var", "pre_rstd", "nx_ready", "tr_done", "nt_hi_ready", "nt_ready"))
        nx_unscaled = sem("nx_unscaled")
        y_done, post_var, post_rstd, delta_ready, x_ready = (
            sems(n, PHASES) for n in ("y_done", "post_var", "post_rstd", "delta_ready", "x_ready"))
        dve_step, act_step, pool_step = sem("dve_step"), sem("act_step"), sem("pool_step")
        mask_ready = sem("mask_ready")
        wq_hi_ready, wq_ready, m_hi_ready, m_ready = map(sem, ("wq_hi_ready", "wq_ready", "m_hi_ready", "m_ready"))
        wsum_hi_ready, mw_done, mw_hi_ready, mw_ready = map(
            sem, ("wsum_hi_ready", "mw_done", "mw_hi_ready", "mw_ready"))
        q0_done, q0_ready, q0_exp, q0_relu, sig_ready, prod_ready, den_ready, sig_scaled = map(
            sem, ("q0_done", "q0_ready", "q0_exp", "q0_relu", "sig_ready", "prod_ready", "den_ready", "sig_scaled"))
        sigt_done, sigt_hi_ready, sigt_ready = map(sem, ("sigt_done", "sigt_hi_ready", "sigt_ready"))
        wf_hi_ready, wf_ready, g_done, u_done, silu_ready, hid_f_ready, hid_hi_ready, hid_ready, down_done = map(
            sem, ("wf_hi_ready", "wf_ready", "g_done", "u_done", "silu_ready", "hid_f_ready", "hid_hi_ready",
                  "hid_ready", "down_done"))
        wsum_ready, wsum_lo_ready = sems("wsum_ready", 2), sems("wsum_lo_ready", 2)
        wkv_hi_ready, wkv_ready, wo1_hi_ready, wo1_ready = map(
            sem, ("wkv_hi_ready", "wkv_ready", "wo1_hi_ready", "wo1_ready"))
        qkv_done, q_hi_ready, k_hi_ready, v_ready, qs_ready, ks_ready, pads_ready, qs_bias = map(
            sem, ("qkv_done", "q_hi_ready", "k_hi_ready", "v_ready", "qs_ready", "ks_ready", "pads_ready", "qs_bias"))
        ktr_done, kt_ready, qtr_done, qt_act, qt_dve = map(sem, ("ktr_done", "kt_ready", "qtr_done", "qt_act", "qt_dve"))
        s1_done, s1_read, shift_ready, shift_t_ready = map(sem, ("s1_done", "s1_read", "shift_ready", "shift_t_ready"))
        shift_in = sems("shift_in", 2)
        s2_done, p_ready, pv_done, o_read = map(sem, ("s2_done", "p_ready", "pv_done", "o_read"))
        bg_o, bg_o_read, bg_a, at_hi_ready, bg_a_read = map(sem, ("bg_o", "bg_o_read", "bg_a", "at_hi_ready", "bg_a_read"))
        we_hi_ready, we_ready, lb_hi_ready, lb_ready = map(sem, ("we_hi_ready", "we_ready", "lb_hi_ready", "lb_ready"))
        l3_done, gap_ready, gap_exp, hs_ready, ht_done, ht_hi_ready, ht_ready = map(
            sem, ("l3_done", "gap_ready", "gap_exp", "hs_ready", "ht_done", "ht_hi_ready", "ht_ready"))
        out_sem = sem("out_sem")

        slots, turned3_before, projected_before = attention_slots()
        pieces = [score_pieces(t) for t in range(NT)]
        s1_order = row_maxima_order()
        s1_use = {item: use for use, item in enumerate(s1_order)}
        s1_first = s1_use[2, 0]
        batch_base = [t * (t + 1) for t in range(NT)]

        early = s1_order[:s1_first]
        share = -(-len(early) // (NT + 1 - EARLY_FROM))
        early = [[] for t in range(EARLY_FROM)] + [early[i:i + share] for i in range(0, len(early), share)]
        early += [[] for t in range(NT + 1 - len(early))]
        early = [[items[len(items) * i // 3:len(items) * (i + 1) // 3] for i in range(3)] for items in early]

        last_use = 4 * batch_base[NT - 1]

        def s1_bank(use):
            return S1[use % (S1_BUFS if use >= s1_first else 2)]

        def s2_bank(use):
            return S2[use % (S2_BUFS if use < last_use else 4)]

        def cols(t):
            return slice(t * P, (t + 1) * P)

        def tile_transpose(p, t):
            if p in (1, 2):
                return mt_hi[:, :, cols(t)], mt_lo[:, :, cols(t)]
            if p == 3:
                return qt[:, 0:KC, cols(t)], qt[:, KC:2 * KC, cols(t)]
            return nt_hi[:, t % 2], nt_lo[:, t % 2]

        def delta_of(p, t):
            if p == 1 and t % HALF >= 2:
                return nx[:, 1, t % 2, :]
            return (delta3 if p == 3 else delta)[:, t % 2, :]

        def f32(ap):
            return ap.bitcast(F32)

        block = ctx.enter_context(nc.Block())

        @block.sync
        def _(sp):
            sp.dma_start(x[:, 0, :], A["x"][0, 0:P, :]).then_inc(x_in[0], 16)
            sp.dma_start(ident[:], A["c_ident"]).then_inc(id_in, 16)
            sp.dma_start(x[:, 1, :], A["x"][0, P:2 * P, :]).then_inc(x_in[1], 16)
            for k in range(KC):
                sp.dma_start(wq_raw[:, k, :], A["wq"][:, k, :]).then_inc(wq_in[k], 16)
            sp.dma_start(bq_b[:], A["bq"].broadcast_to([P, H0 * D0])).then_inc(bz_in, 16)
            sp.dma_start(z_b[:], A["z"].broadcast_to([P, H0 * D0])).then_inc(bz_in, 16)
            sp.dma_start(mask_raw[:], A["c_masks"]).then_inc(mask_in, 16)
            sp.dma_start(m_raw[:], A["m"]).then_inc(m_in, 16)
            for h in range(H0):
                if 1 <= h < NT - 1:
                    sp.dma_start(x[:, h + 1, :], A["x"][0, (h + 1) * P:(h + 2) * P, :]).then_inc(x_in[h + 1], 16)
                if h >= WO_BUFS:
                    sp.wait_ge(wsum_lo_ready[h % 2], (h - WO_BUFS) // 2 + 1)
                sp.dma_start(wo0_raw[:, h % WO_BUFS], A["wo0"][h].rearrange("p (g n) -> p g n", g=G0))\
                  .then_inc(wo0_in[h % WO_BUFS], 16)
                if h == 1:
                    sp.dma_start(lnw[:], A["lnw"].broadcast_to([P, HID])).then_inc(lnw_in, 16)
            sp.dma_start(kbias[:], A["c_kbias"]).then_inc(tab_in, 16)
            sp.dma_start(w0[:], A["c_w0"]).then_inc(tab_in, 16)
            sp.dma_start(iota[:], A["c_iota"]).then_inc(tab_in, 16)
            for c in range(2 * NJ):
                if c == 0:
                    sp.wait_ge(mw_ready, H0)
                    for q in range(2):
                        sp.wait_ge(wsum_lo_ready[q], H0 // 2)
                if c >= RAW_BUFS:
                    sp.wait_ge(wf_ready, c - RAW_BUFS + 1)
                sp.dma_start(wf_raw[:, c % RAW_BUFS, :], A["wf"][c % NJ]).then_inc(wf_in[c % RAW_BUFS], 16)
                if c == 4:
                    sp.wait_ge(y_done[0], NT)
                    sp.dma_start(wkv_raw[:], A["wkv"]).then_inc(wkv_in, 16)
                    sp.dma_start(qbias[:].rearrange("p t h b -> p t (h b)"), A["c_qbias"]).then_inc(tab_in, 16)
            for t in range(NT):
                sp.wait_ge(shift_t_ready, t + 1)
                for p in range(2):
                    for part in range(2):
                        row = STK * p + BIAS_ROWS - 2 + part
                        src = (2 * p + part) * PAIRS
                        sp.dma_start(f32(qt[row:row + 1, :, cols(t)]), f32(shift_t[src:src + PAIRS, t % 2, :]))\
                          .then_inc(shift_in[t % 2], 16)
                if t == 1:
                    sp.wait_ge(qs_bias, 2 * NT)
                    sp.wait_ge(ktr_done, NT)
                    sp.dma_start(wo1_raw[:], A["wo1"]).then_inc(wo1_in, 16)
                if t == 2:
                    sp.wait_ge(wo1_ready, 1)
                    for k in range(2):
                        sp.dma_start(we_raw[:, k, :], A["we"][k]).then_inc(we_in[k], 16)
                if t == 4:
                    sp.wait_ge(we_ready, 2)
                    for k in range(2):
                        sp.dma_start(we_raw[:, k, :], A["we"][k + 2]).then_inc(we_in[k], 16)
                    sp.dma_start(lb_raw[:], A["lb"][:, 0, :]).then_inc(lb_in, 16)
                if t == NT - 1:
                    sp.wait_ge(lb_ready, 1)
                    sp.dma_start(lb_raw[:], A["lb"][:, 1, :]).then_inc(lb_in, 16)
            for t in range(NT):
                sp.wait_ge(x_ready[3], t + 1)
                sp.dma_start(out[0, cols(t), :], x[:, t, :]).then_inc(out_sem, 16)
            sp.wait_ge(out_sem, 16 * NT)

        @block.vector
        def _(dve):
            steps = [0]

            def link(ins):
                steps[0] += 1
                ins.then_inc(dve_step, 1)
                dve.wait_ge(dve_step, steps[0])

            def stats(kind, i, src, ready):
                link(dve.bn_stats(bn[:, kind, i, :], src))
                link(dve.bn_aggr(mv[:, kind, i, :], bn[:, kind, i, :]))
                v = mv[:, kind, i, 1:2]
                if kind == 0 and i // NT == 1:
                    ins = dve.tensor_scalar(ve[:, kind, i:i + 1], v, 1.0 + RMS_EPS, LN_EPS * RMS_EPS, ALU.mult, ALU.add)
                else:
                    ins = dve.tensor_scalar(ve[:, kind, i:i + 1], v, LN_EPS, None, ALU.add)
                ins.then_inc(ready, 1)

            def pre_stats(p, t):
                if p == 0:
                    dve.wait_ge(x_in[t], 16)
                else:
                    dve.wait_ge(x_ready[p - 1], t + 1)
                stats(0, p * NT + t, x[:, t, :], pre_var[p])

            def pre_norm(p, t):
                i = p * NT + t
                dve.wait_ge(pre_rstd[p], t + 1)
                if t >= 2:
                    dve.wait_ge(tr_done[p], t - 1)
                dve.tensor_scalar(nx[:, int(p == 1), t % 2, :], x[:, t, :], mv[:, 0, i, 0:1], rstd[:, 0, i:i + 1],
                                  ALU.subtract, ALU.mult).then_inc(nx_unscaled if p == 1 else nx_ready[p], 1)

            def pre_lo(p, t):
                hi, lo = tile_transpose(p, t)
                dve.wait_ge(nt_hi_ready[p], t + 1)
                dve.tensor_tensor(lo, TR[p].rearrange("p (k n) -> p k n", k=KC), f32(hi), ALU.subtract)\
                   .then_inc(nt_ready[p], 1)

            def post_stats(p, t, y):
                dve.wait_ge(y_done[p], t + 1)
                stats(1, p * NT + t, y, post_var[p])

            def wq_low(k):
                dve.wait_ge(wq_hi_ready, k + 1)
                dve.tensor_tensor(wq_lo[:, k, :], wq_raw[:, k, :], f32(wq_hi[:, k, :]), ALU.subtract)\
                   .then_inc(wq_ready, 1)

            def wo_sum(h):
                dve.wait_ge(wo0_in[h % WO_BUFS], 16 * (h // WO_BUFS + 1))
                w = wo0_raw[:, h % WO_BUFS]
                link(dve.tensor_tensor(w[:, 0:2], w[:, 0:2], w[:, 2:4], ALU.add))
                dve.tensor_tensor(w[:, 0], w[:, 0], w[:, 1], ALU.add).then_inc(wsum_ready[0], 1)

            def wo_low(h):
                dve.wait_ge(wsum_hi_ready, h + 1)
                if h >= WSUM_BUFS:
                    dve.wait_ge(mw_done, h - WSUM_BUFS + 1)
                dve.tensor_tensor(wsum_lo[:, h % WSUM_BUFS], wo0_raw[:, h % WO_BUFS, 0],
                                 f32(wsum_hi[:, h % WSUM_BUFS]), ALU.subtract)\
                   .then_inc(wsum_lo_ready[0], 1)

            def mw_low(h):
                dve.wait_ge(mw_hi_ready, h + 1)
                dve.tensor_tensor(mw_lo[:, h, :], Y0[h % 2], f32(mw_hi[:, h, :]), ALU.subtract).then_inc(mw_ready, 1)

            def q_bias(t):
                dve.wait_ge(q0_done, t + 1)
                if t == 0:
                    dve.wait_ge(bz_in, 32)
                if t:
                    dve.wait_ge(q0_exp, t)
                    dve.wait_ge(q0_relu, t)
                dve.tensor_tensor(q0[:], Q0.rearrange("p a n -> p (a n)"), bq_b[:], ALU.add).then_inc(q0_ready, 1)

            def sigma(t):
                dve.wait_ge(q0_exp, t + 1)
                dve.wait_ge(q0_relu, t + 1)
                if t >= 2:
                    dve.wait_ge(sigt_done, t - 1)
                dve.scalar_tensor_tensor(sig[:, t % 2, :], e0[:], 1.0, q0[:], ALU.min, ALU.add).then_inc(sig_ready, 1)

            def denominator(t):
                dve.wait_ge(prod_ready, t + 1)
                link(dve.tensor_reduce(den[:, t, 0, :], prod[:].rearrange("p (h d) -> p h d", h=H0), X, ALU.add))
                link(dve.tensor_scalar(den[:, t, 1, :], den[:, t, 0, :], DEN_EPS, None, ALU.add))
                dve.reciprocal(den[:, t, 2, :], den[:, t, 1, :]).then_inc(den_ready, 1)

            def sig_low(t):
                dve.wait_ge(sigt_hi_ready, t + 1)
                dve.tensor_tensor(sigt_lo[:], SIGT.rearrange("p a (h n) -> p (a h) n", h=H0 // 2), f32(sigt_hi[:]),
                                  ALU.subtract).then_inc(sigt_ready, 1)

            def hidden(c):
                dve.wait_ge(silu_ready, c + 1)
                dve.wait_ge(u_done, c + 1)
                if c >= 2:
                    dve.wait_ge(hid_ready, c - 1)
                dve.tensor_tensor(hid[:, c % 2, :], silu[:, c % 2, :], UP, ALU.mult).then_inc(hid_f_ready, 1)

            def hidden_low(c):
                dve.wait_ge(hid_hi_ready, c + 1)
                dve.tensor_tensor(hid_lo[:, c % 2, :], hid[:, c % 2, :], f32(hid_hi[:, c % 2, :]), ALU.subtract)\
                   .then_inc(hid_ready, 1)

            pre_stats(0, 0)
            pre_norm(0, 0)
            pre_stats(0, 1)
            wq_low(0)
            pre_lo(0, 0)
            pre_norm(0, 1)
            for k in range(1, KC):
                wq_low(k)
            pre_lo(0, 1)
            for i in range(NT + 2):
                if i == NT + 1:
                    hidden(0)
                if 3 <= i:
                    pre_stats(1, i - 3)
                if i + 2 < NT:
                    pre_stats(0, i + 2)
                if 3 <= i:
                    pre_norm(1, i - 3)
                first, last = (HEADS_AT[i], HEADS_AT[i + 1]) if i < 3 else (0, 0)
                if i == 0:
                    wo_sum(0)
                    dve.wait_ge(mask_in, 16)
                    dve.tensor_copy(masks[:], mask_raw[:]).then_inc(mask_ready, 1)
                    wo_low(0)
                if i == 1:
                    wo_sum(4)
                    wo_low(2)
                    wo_low(4)
                if i == 2:
                    wo_low(6)
                if i < NT:
                    q_bias(i)
                for h in range(first, min(first + 2, last)):
                    mw_low(h)
                if i + 2 < NT:
                    pre_norm(0, i + 2)
                if i < NT:
                    sigma(i)
                for h in range(first + 2, last):
                    mw_low(h)
                if i == 0:
                    wo_sum(2)
                if i == 1:
                    wo_sum(6)
                if 2 <= i:
                    post_stats(0, i - 2, Y0[i % 2])
                if 3 <= i:
                    pre_lo(1, i - 3)
                if i + 2 < NT:
                    pre_lo(0, i + 2)
                if 1 <= i <= NT:
                    sig_low(i - 1)
                if i < NT:
                    denominator(i)

            def y1(t):
                return Y1[:, t % HALF, :]

            hidden_low(0)
            for c in range(1, 2 * NJ):
                turned = c - NJ - 4
                hidden(c)
                if c == 1:
                    pre_stats(1, NT - 1)
                if 0 <= turned + 1 < HALF:
                    pre_norm(2, turned + 1)
                if 0 <= turned < HALF:
                    pre_lo(2, turned)
                hidden_low(c)
                if c == 2:
                    pre_norm(1, NT - 1)
                if c == 3:
                    pre_lo(1, NT - 1)
                if c == NJ:
                    for t in range(HALF):
                        post_stats(1, t, y1(t))
                if 0 <= turned + 2 < HALF:
                    pre_stats(2, turned + 2)
            for t in range(HALF, NT):
                post_stats(1, t, y1(t))

            def q_low(t):
                dve.wait_ge(q_hi_ready, t + 1)
                s = qs[:, t % 2, :, :]
                dve.scalar_tensor_tensor(s[:, :, QLO:QLO + D1], QP[t % 2].rearrange("p (h d) -> p h d", d=D1), SCALE,
                                         f32(s[:, :, QHI:QHI + D1]), ALU.mult, ALU.subtract).then_inc(qs_ready, 1)

            def k_low(t):
                dve.wait_ge(k_hi_ready, t + 1)
                for r in range(2):
                    ins = dve.tensor_tensor(ks[:, t % 2, r, QHI + D1:QLO], KVP[:, 0:D1],
                                            f32(ks[:, t % 2, r, QHI:QHI + D1]), ALU.subtract)
                    ins.then_inc(ks_ready, 1)

            def q_turned(t, g):
                dve.wait_ge(qtr_done, 4 * t + g + 1)
                dve.tensor_copy(qt[:, 4 * g:4 * g + 4, cols(t)],
                                STKT[g % 2].rearrange("p (j n) -> p j n", j=4)).then_inc(qt_dve, 1)

            def row_maxima(t, n):
                b = t % 2
                use = s1_use[t, n]
                if n < len(pieces[t]):
                    q, j, nh, k0, kw, part = pieces[t][n]
                    dve.wait_ge(s1_done, use + 1)
                    if n == 0 and t >= 2:
                        dve.wait_ge(shift_ready, t - 1)
                    dve.tensor_reduce(rowmax[:, b, part, q, j:j + nh],
                                      s1_bank(use)[:, 0:nh * kw].rearrange("p (h k) -> p h k", h=nh), X, ALU.max)\
                       .then_inc(s1_read, 1)
                    if n < len(pieces[t]) - 1:
                        return
                    dve.wait_ge(s1_read, use + 1)
                    m = rowmax[:, b, 0, :]
                    if (t + 1) * P > BANK:
                        link(dve.tensor_tensor(wshift[:, b, 0, :], rowmax[:, b, 0, :], rowmax[:, b, 1, :], ALU.max))
                        m = wshift[:, b, 0, :]
                    link(dve.tensor_tensor(wshift[:, b, 1, :], w0[:, t, :], m, ALU.subtract))
                    w = wshift[:, b, 1, :]
                    link(dve.tensor_copy(shift[:, b, :, 0, :].bitcast(F32R), w))
                    dve.tensor_tensor(shift[:, b, :, 1, :], w, shift[:, b, :, 0, :], ALU.subtract)\
                       .then_inc(shift_ready, 1)
                else:
                    dve.wait_ge(s1_done, use + 1)
                    if t >= 2:
                        dve.wait_ge(shift_in[b], 64 * (t // 2))
                    dve.tensor_copy(shift_t[:, b, :], s1_bank(use)[0:STK, 0:P]).then_inc(s1_read, 1)
                    dve.wait_ge(s1_read, use + 1)
                    dve.sem_inc(shift_t_ready, 1)

            for t in range(NT + 1):
                if 1 <= t <= HALF:
                    pre_stats(2, t + HALF - 1)
                    pre_norm(2, t + HALF - 1)
                for place in range(3):
                    for item in early[t][place]:
                        row_maxima(*item)
                    if place < 2 and t:
                        q_turned(t - 1, 2 * place + 1)
                    if place == 1 and 2 <= t <= HALF + 1:
                        pre_lo(2, t + HALF - 2)
                    if place == 1 and t < NT:
                        k_low(t)
                if t < NT:
                    q_low(t)

            def back(t, step):
                if step in ("norm0", "norm1"):
                    q = int(step == "norm1")
                    dve.wait_ge(bg_o, 2 * t + q + 1)
                    o = BG.rearrange("p (i g v) -> p i g v", i=4, g=4)
                    r = rsum[:, t % 2, q, :].rearrange("p (i g) -> p i g", i=4)
                    link(dve.reciprocal(r, o[:, :, :, D1]))
                    to = attn.rearrange("p (g i q d) -> p i g q d", g=4, i=4, q=2)[:, :, :, q, :]
                    dve.tensor_tensor(to, o[:, :, :, 0:D1], r.unsqueeze(3).broadcast_to([P, 4, 4, D1]), ALU.mult)\
                       .then_inc(bg_o_read, 1)
                elif step == "low":
                    dve.wait_ge(at_hi_ready, t + 1)
                    dve.tensor_tensor(at_lo, BG.rearrange("p (k n) -> p k n", k=KC), f32(at_hi), ALU.subtract)\
                       .then_inc(bg_a_read, 1)
                elif step == "stats":
                    post_stats(2, t, BG)
                elif step == "stats3":
                    pre_stats(3, t)
                elif step == "norm3":
                    pre_norm(3, t)
                elif step == "low3":
                    pre_lo(3, t)

            def gates(t):
                dve.wait_ge(l3_done, t + 1)
                l = logit[:, t % 2, :]
                link(dve.tensor_copy(l, L3[t % 2][:, 0:NE]))
                link(dve.max(top[:, t, :], l))
                dve.tensor_tensor(prob[:, t, 0:1], top[:, t, 1:2], top[:, t, 0:1], ALU.subtract).then_inc(gap_ready, 1)
                link(dve.max_index(topi[:, t, :], top[:, t, :], l))
                link(dve.tensor_copy(top[:, t, 0:2], topi[:, t, 0:2]))
                dve.wait_ge(gap_exp, t + 1)
                pr = prob[:, t, :]
                link(dve.tensor_scalar(pr[:, 2:3], pr[:, 1:2], 1.0, None, ALU.add))
                link(dve.reciprocal(pr[:, 3:4], pr[:, 2:3]))
                link(dve.tensor_scalar(pr[:, 4:5], pr[:, 3:4], SCALING, None, ALU.mult))
                link(dve.tensor_scalar(pr[:, 5:6], pr[:, 1:2], pr[:, 4:5], None, ALU.mult))
                link(dve.tensor_scalar(gate[:, t % 2, 0, :], iota[:], top[:, t, 0:1], pr[:, 4:5], ALU.is_equal, ALU.mult))
                link(dve.tensor_scalar(gate[:, t % 2, 1, :], iota[:], top[:, t, 1:2], pr[:, 5:6], ALU.is_equal, ALU.mult))
                link(dve.tensor_tensor(gate[:, t % 2, 2, :], gate[:, t % 2, 0, :], gate[:, t % 2, 1, :], ALU.add))
                if t >= 2:
                    dve.wait_ge(ht_done, t - 1)
                dve.tensor_tensor(hs[:, t % 2, :].rearrange("p (e r) -> p e r", e=NE),
                                  L3[t % 2][:, NE:LG].rearrange("p (e r) -> p e r", e=NE),
                                  gate[:, t % 2, 2, :].unsqueeze(2).broadcast_to([P, NE, RANK]), ALU.mult)\
                   .then_inc(hs_ready, 1)

            def h_low(t):
                dve.wait_ge(ht_hi_ready, t + 1)
                dve.tensor_tensor(ht_lo[:, t % 2], HT[0:ER // 2, :].rearrange("p (c n) -> p c n", c=2),
                                  f32(ht_hi[:, t % 2]), ALU.subtract).then_inc(ht_ready, 1)

            def experts(e):
                i = e // 2
                if e % 2 == 0:
                    if i < NT:
                        gates(i)
                else:
                    if 3 <= i:
                        post_stats(3, i - 3, O3[(i - 3) % 4])
                    if 1 <= i <= NT:
                        h_low(i - 1)

            for t, kb, p, after, steps_back, e in slots:
                for g in range(4):
                    for u, step in steps_back[g]:
                        back(u, step)
                    for item in after[g]:
                        row_maxima(*item)
                for u, step in steps_back[4]:
                    back(u, step)
                if e is not None:
                    experts(e)

        @block.scalar
        def _(act):
            def split_hi(dst, src, sem_, scale=1.0):
                act.activation(dst, src, ACT.Copy, scale=scale).then_inc(sem_, 1)

            def pre_hi(p, t):
                hi, _ = tile_transpose(p, t)
                act.wait_ge(tr_done[p], t + 1)
                if p == 0 and t >= 2:
                    act.wait_ge(q0_done, t - 1)
                split_hi(hi, TR[p].rearrange("p (k n) -> p k n", k=KC), nt_hi_ready[p])

            def post_apply(p, t, y):
                i = p * NT + t
                act.wait_ge(post_rstd[p], t + 1)
                if p == 1:
                    if t >= HALF:
                        act.wait_ge(x_ready[p], t - HALF + 1)
                elif t >= 2:
                    act.wait_ge(x_ready[p], t - 1)
                act.activation(delta_of(p, t), y, ACT.Identity, bias=mv[:, 1, i, 0:1],
                               scale=rstd[:, 1, i:i + 1]).then_inc(delta_ready[p], 1)

            act.wait_ge(wq_in[0], 16)
            split_hi(wq_hi[:, 0, :], wq_raw[:, 0, :], wq_hi_ready)
            pre_hi(0, 0)
            for k in range(1, KC):
                act.wait_ge(wq_in[k], 16)
                split_hi(wq_hi[:, k, :], wq_raw[:, k, :], wq_hi_ready)
            pre_hi(0, 1)
            act.wait_ge(m_in, 16)
            split_hi(m_hi[:], m_raw[:], m_hi_ready)

            def sig_high(t):
                act.wait_ge(sigt_done, t + 1)
                if t:
                    act.wait_ge(y_done[0], t)
                split_hi(sigt_hi[:], SIGT.rearrange("p a (h n) -> p (a h) n", h=H0 // 2), sigt_hi_ready)

            def weight_hi(c):
                act.wait_ge(wf_in[c % RAW_BUFS], 16 * (c // RAW_BUFS + 1))
                if c >= WBUFS:
                    act.wait_ge(down_done, c - WBUFS + 1)
                elif c == 0:
                    act.wait_ge(q0_done, NT)
                split_hi(wf_hi[:, c % WBUFS, :], wf_raw[:, c % RAW_BUFS, :], wf_hi_ready)

            def gate_silu(c):
                act.wait_ge(g_done, c + 1)
                if c >= 2:
                    act.wait_ge(hid_f_ready, c - 1)
                act.activation(silu[:, c % 2, :], GATE, ACT.Silu).then_inc(silu_ready, 1)

            for i in range(NT + 2):
                first, last = (HEADS_AT[i], HEADS_AT[i + 1]) if i < 3 else (0, 0)
                for h in range(first, last):
                    act.wait_ge(wsum_ready[h % 2], h // 2 + 1)
                    if h >= WSUM_BUFS:
                        act.wait_ge(mw_done, h - WSUM_BUFS + 1)
                    split_hi(wsum_hi[:, h % WSUM_BUFS], wo0_raw[:, h % WO_BUFS, 0], wsum_hi_ready)
                if 1 <= i <= NT:
                    act.wait_ge(den_ready, i)
                    for h in range(H0):
                        w = slice(h * D0, (h + 1) * D0)
                        s = sig[:, (i - 1) % 2, w]
                        ins = act.activation(s, s, ACT.Copy, scale=den[:, i - 1, 2, h:h + 1])
                    ins.then_inc(sig_scaled, 1)

                def mw_high(h):
                    act.wait_ge(mw_done, h + 1)
                    split_hi(mw_hi[:, h, :], Y0[h % 2], mw_hi_ready)

                for h in range(first, min(first + 2, last)):
                    mw_high(h)
                if i < NT:
                    act.wait_ge(q0_ready, i + 1)
                    if i:
                        act.wait_ge(sig_ready, i)
                    act.activation(e0[:], q0[:], ACT.Exp).then_inc(q0_exp, 1)
                    act.activation(q0[:], q0[:], ACT.Relu).then_inc(q0_relu, 1)
                for h in range(first + 2, last):
                    mw_high(h)
                if i == NT - 1:
                    weight_hi(0)
                if i == NT + 1:
                    gate_silu(0)
                if 3 <= i:
                    pre_hi(1, i - 3)
                if i + 2 < NT:
                    pre_hi(0, i + 2)
                if 1 <= i <= NT:
                    sig_high(i - 1)
                if 2 <= i:
                    post_apply(0, i - 2, Y0[i % 2])
                if i == NT:
                    weight_hi(1)

            for c in range(2 * NJ):
                if c:
                    gate_silu(c)
                if c + 2 < 2 * NJ:
                    weight_hi(c + 2)
                if 0 <= c - NJ - 4 < HALF:
                    pre_hi(2, c - NJ - 4)
                act.wait_ge(hid_f_ready, c + 1)
                if c >= 2:
                    act.wait_ge(down_done, c - 1)
                split_hi(hid_hi[:, c % 2, :], hid[:, c % 2, :], hid_hi_ready)
                if c == 3:
                    pre_hi(1, NT - 1)
                if 8 <= c < 8 + KC:
                    act.wait_ge(wkv_in, 16)
                    split_hi(wkv_hi[:, c - 8], wkv_raw[:, c - 8], wkv_hi_ready)
                if c == NJ:
                    for t in range(HALF):
                        post_apply(1, t, Y1[:, t, :])

            for t in range(HALF, NT):
                post_apply(1, t, Y1[:, t - HALF, :])
            for t in range(NT + 1):
                if t >= 1:
                    u = t - 1
                    act.wait_ge(ktr_done, u + 1)
                    for p in range(2):
                        r = slice(STK * p, STK * (p + 1))
                        act.activation(kt[r, p, cols(u)], TR[2][r, 0:P], ACT.Copy).then_inc(kt_ready, 1)
                    for g in (0, 2):
                        act.wait_ge(qtr_done, 4 * u + g + 1)
                        act.activation(qt[:, 4 * g:4 * g + 4, cols(u)],
                                       STKT[g % 2].rearrange("p (j n) -> p j n", j=4), ACT.Copy).then_inc(qt_act, 1)
                if 2 <= t <= HALF + 1:
                    pre_hi(2, t + HALF - 2)
                if t < NT:
                    act.wait_ge(qkv_done, t + 1)
                    if t == 0:
                        act.wait_ge(pads_ready, 4)
                    if t >= 2:
                        act.wait_ge(ktr_done, t - 1)
                    kk = ks[:, t % 2, :, :]
                    act.activation(vals[:, t, 0:D1], KVP[:, D1:2 * D1], ACT.Copy).then_inc(v_ready, 1)
                    act.activation(kk[:, :, QHI:QHI + D1], KVP[:, 0:D1].unsqueeze(1).broadcast_to([P, 2, D1]), ACT.Copy)\
                       .then_inc(act_step, 1)
                    act.activation(kk[:, :, QLO:QLO + D1], KVP[:, 0:D1].unsqueeze(1).broadcast_to([P, 2, D1]), ACT.Copy)\
                       .then_inc(k_hi_ready, 1)
                    s = qs[:, t % 2, :, :]
                    if t >= 2:
                        act.wait_ge(qtr_done, 4 * (t - 1))
                    q = QP[t % 2].rearrange("p (h d) -> p h d", d=D1)
                    act.activation(s[:, :, QHI:QHI + 2 * D1].rearrange("p h (r d) -> p h r d", r=2),
                                   q.unsqueeze(2).broadcast_to([P, H1, 2, D1]), ACT.Copy, scale=SCALE)\
                       .then_inc(q_hi_ready, 1)

            def back(t, step):
                if step == "copy":
                    act.wait_ge(pv_done, batch_base[t] + 2 * (t + 1))
                    if t:
                        act.wait_ge(bg_o, 2 * t)
                    act.activation(o_sb[:], PV, ACT.Copy).then_inc(o_read, 1)
                elif step == "high":
                    act.wait_ge(bg_a, t + 1)
                    if t:
                        act.wait_ge(y_done[2], t)
                    split_hi(at_hi, BG.rearrange("p (k n) -> p k n", k=KC), at_hi_ready)
                elif step == "apply":
                    post_apply(2, t, BG)
                elif step == "high3":
                    pre_hi(3, t)

            def experts(e):
                i = e // 2
                if e % 2 == 0:
                    if i < NT:
                        act.wait_ge(gap_ready, i + 1)
                        act.activation(prob[:, i, 1:2], prob[:, i, 0:1], ACT.Exp).then_inc(gap_exp, 1)
                else:
                    if 1 <= i <= NT:
                        t = i - 1
                        act.wait_ge(ht_done, t + 1)
                        if t >= 2:
                            act.wait_ge(y_done[3], t - 1)
                        split_hi(ht_hi[:, t % 2], HT[0:ER // 2, :].rearrange("p (c n) -> p c n", c=2), ht_hi_ready)
                    if 3 <= i:
                        post_apply(3, i - 3, O3[(i - 3) % 4])

            batch = 0
            for t, kb, p, after, steps_back, e in slots:
                for g in range(4):
                    for u, step in steps_back[g]:
                        back(u, step)
                    if t is not None:
                        use = 4 * batch + g
                        act.wait_ge(s2_done, use + 1)
                        if batch >= P_BUFS // 4 and g == 0:
                            act.wait_ge(pv_done, batch - P_BUFS // 4 + 1)
                        act.activation(probs[:, use % P_BUFS, :], s2_bank(use), ACT.Exp).then_inc(p_ready, 1)
                batch += t is not None
                for u, step in steps_back[4]:
                    back(u, step)
                if e is not None:
                    experts(e)

        @block.gpsimd
        def _(pool):
            steps = [0]

            def link(ins):
                steps[0] += 1
                ins.then_inc(pool_step, 1)
                pool.wait_ge(pool_step, steps[0])

            def power(dst, src):
                return pool.tensor_tensor(dst, src, mhalf[:], ALU.pow)

            def pre_scale(p, t):
                i = p * NT + t
                pool.wait_ge(pre_var[p], t + 1)
                power(rstd[:, 0, i:i + 1], ve[:, 0, i:i + 1]).then_inc(pre_rstd[p], 1)

            def weigh(t):
                if t == 0:
                    pool.wait_ge(lnw_in, 16)
                pool.wait_ge(nx_unscaled, t + 1)
                n = nx[:, 1, t % 2, :]
                pool.tensor_tensor(n, n, lnw[:], ALU.mult).then_inc(nx_ready[1], 1)

            def post_scale(p, t):
                i = p * NT + t
                pool.wait_ge(post_var[p], t + 1)
                link(power(rstd[:, 1, i:i + 1], ve[:, 1, i:i + 1]))
                m = mv[:, 1, i, 0:1]
                pool.tensor_scalar(m, m, rstd[:, 1, i:i + 1], -1.0, ALU.mult, ALU.mult).then_inc(post_rstd[p], 1)

            def add(p, t):
                pool.wait_ge(delta_ready[p], t + 1)
                pool.tensor_tensor(x[:, t, :], x[:, t, :], delta_of(p, t), ALU.add).then_inc(x_ready[p], 1)

            link(pool.memset(mhalf[:], -0.5))
            link(pool.memset(vals[:], 0.0))
            pool.memset(vals[:, :, D1:D1 + 1], 1.0).then_inc(pads_ready, 1)
            pre_scale(0, 0)
            pre_scale(0, 1)

            def weight_lo(c):
                pool.wait_ge(wf_hi_ready, c + 1)
                b, r = c % WBUFS, c % RAW_BUFS
                pool.tensor_tensor(wf_lo[:, b, :], wf_raw[:, r, :], f32(wf_hi[:, b, :]), ALU.subtract)\
                    .then_inc(wf_ready, 1)

            def wo_sum(h):
                pool.wait_ge(wo0_in[h % WO_BUFS], 16 * (h // WO_BUFS + 1))
                w = wo0_raw[:, h % WO_BUFS]
                link(pool.tensor_tensor(w[:, 0:2], w[:, 0:2], w[:, 2:4], ALU.add))
                pool.tensor_tensor(w[:, 0], w[:, 0], w[:, 1], ALU.add).then_inc(wsum_ready[1], 1)

            def wo_low(h):
                pool.wait_ge(wsum_hi_ready, h + 1)
                if h >= WSUM_BUFS:
                    pool.wait_ge(mw_done, h - WSUM_BUFS + 1)
                pool.tensor_tensor(wsum_lo[:, h % WSUM_BUFS], wo0_raw[:, h % WO_BUFS, 0],
                                  f32(wsum_hi[:, h % WSUM_BUFS]), ALU.subtract)\
                    .then_inc(wsum_lo_ready[1], 1)

            pool.wait_ge(m_hi_ready, 1)
            pool.tensor_tensor(m_lo[:], m_raw[:], f32(m_hi[:]), ALU.subtract).then_inc(m_ready, 1)
            for i in range(NT + 2):
                if 3 <= i:
                    pre_scale(1, i - 3)
                if i + 2 < NT:
                    pre_scale(0, i + 2)
                if 3 <= i:
                    weigh(i - 3)
                if i == 0:
                    wo_sum(1)
                    wo_low(1)
                if i == 1:
                    wo_low(3)
                    wo_sum(5)
                if i == 2:
                    wo_low(5)
                    wo_low(7)
                if i < NT:
                    pool.wait_ge(sig_ready, i + 1)
                    if i:
                        pool.wait_ge(den_ready, i)
                    pool.tensor_tensor(prod[:], sig[:, i % 2, :], z_b[:], ALU.mult).then_inc(prod_ready, 1)
                if i < 2:
                    wo_sum((3, 7)[i])
                if 2 <= i:
                    post_scale(0, i - 2)
                    add(0, i - 2)
                if NT - 1 <= i <= NT:
                    weight_lo(i - NT + 1)

            for c in range(2 * NJ):
                if c >= 2:
                    weight_lo(c)
                if c == 3:
                    pre_scale(1, NT - 1)
                if c == 4:
                    weigh(NT - 1)
                if c == NJ + 1:
                    for t in range(HALF):
                        post_scale(1, t)
                if 0 <= c - NJ - 2 < HALF:
                    add(1, c - NJ - 2)
                if 9 <= c < 9 + KC:
                    k = c - 9
                    pool.wait_ge(wkv_hi_ready, k + 1)
                    pool.tensor_tensor(wkv_lo[:, k], wkv_raw[:, k], f32(wkv_hi[:, k]), ALU.subtract)\
                        .then_inc(wkv_ready, 1)
                if c == 9 + KC:
                    pool.memset(f32(qs[:, :, :, QLO + D1:STK]), 0.0).then_inc(pads_ready, 1)
                if 0 <= c - NJ - 4 < HALF:
                    pre_scale(2, c - NJ - 4)

            pool.wait_ge(hid_ready, 2 * NJ)
            pool.wait_ge(down_done, 2 * NJ)
            pool.memset(f32(ks[:, :, :, QLO + D1:STK]), 0.0).then_inc(pads_ready, 1)
            pool.memset(f32(kt[:]), 0.0).then_inc(pads_ready, 1)
            for t in range(HALF, NT):
                post_scale(1, t)
            for t in range(NT):
                b = t % 2
                if t >= 2:
                    pool.wait_ge(qtr_done, 4 * (t - 1))
                    pool.wait_ge(ktr_done, t - 1)
                if t == 0:
                    pool.wait_ge(tab_in, 64)
                pool.tensor_copy(qs[:, b, :, 0:BIAS_ROWS], qbias[:, t]).then_inc(qs_bias, 1)
                pool.tensor_copy(ks[:, b, :, 0:BIAS_ROWS],
                                 kbias[:, t, :].unsqueeze(1).broadcast_to([P, 2, BIAS_ROWS])).then_inc(qs_bias, 1)
                if t == 0:
                    add(1, HALF)
                if t == 1:
                    for v in range(HALF + 1, NT):
                        add(1, v)
                if 1 <= t <= HALF:
                    pre_scale(2, t + HALF - 1)
            pool.wait_ge(wo1_in, 16)
            pool.wait_ge(qkv_done, NT)
            pool.tensor_copy(wo1_hi[:], wo1_raw[:]).then_inc(wo1_hi_ready, 1)
            pool.wait_ge(wo1_hi_ready, 1)
            pool.tensor_tensor(wo1_lo[:], wo1_raw[:], f32(wo1_hi[:]), ALU.subtract).then_inc(wo1_ready, 1)

            def expert_weights(k):
                pool.wait_ge(we_in[k % 2], 16 * (k // 2 + 1))
                pool.tensor_copy(we_hi[:, k, :], we_raw[:, k % 2, :]).then_inc(we_hi_ready, 1)
                pool.wait_ge(we_hi_ready, k + 1)
                pool.tensor_tensor(we_lo[:, k, :], we_raw[:, k % 2, :], f32(we_hi[:, k, :]), ALU.subtract)\
                    .then_inc(we_ready, 1)

            def adapter_weights(c):
                pool.wait_ge(lb_in, 16 * (c + 1))
                pool.tensor_copy(lb_hi[:, c, :], lb_raw[:]).then_inc(lb_hi_ready, 1)
                pool.wait_ge(lb_hi_ready, c + 1)
                pool.tensor_tensor(lb_lo[:, c, :], lb_raw[:], f32(lb_hi[:, c, :]), ALU.subtract).then_inc(lb_ready, 1)

            for t, kb, p, after, steps_back, e in slots:
                for g in range(5):
                    for u, step in steps_back[g]:
                        if step == "stats":
                            post_scale(2, u)
                        elif step == "apply":
                            add(2, u)
                            if u in (1, 2, 4, 5):
                                expert_weights((1, 2, 4, 5).index(u))
                            if u == 5:
                                adapter_weights(0)
                        elif step == "stats3":
                            pre_scale(3, u)
                            if u == 6:
                                adapter_weights(1)
                if e is not None and e % 2 and e // 2 >= 3:
                    post_scale(3, e // 2 - 3)
                    add(3, e // 2 - 3)

        @block.tensor
        def _(pe):
            def product(dst, hi, lo, w_hi, w_lo, first, last):
                pe.matmul(dst, hi, w_hi, start=first, stop=False, skip_group_check=True)
                pe.matmul(dst, hi, w_lo, start=False, stop=False, skip_group_check=True)
                return pe.matmul(dst, lo, w_hi, start=False, stop=last, skip_group_check=True)

            def turn(dst, src):
                return pe.transpose(dst, src, ident[:])

            def pre_turn(p, t):
                pe.wait_ge(nx_ready[p], t + 1)
                if t:
                    pe.wait_ge(nt_ready[p], t)
                for k in range(KC):
                    ins = turn(TR[p][:, k * P:(k + 1) * P], nx[:, int(p == 1), t % 2, k * P:(k + 1) * P])
                ins.then_inc(tr_done[p], 1)

            def gate_up(c, part):
                b = c % WBUFS
                tok = slice(c // NJ * HALF * P, (c // NJ + 1) * HALF * P)
                pe.wait_ge(wf_ready, c + 1)
                if c % NJ == 0:
                    pe.wait_ge(nt_ready[1], HALF * (c // NJ + 1))
                dst, start, free, done = ((GATE, GW, silu_ready, g_done), (UP, UW, hid_f_ready, u_done))[part]
                if c:
                    pe.wait_ge(free, c)
                else:
                    pe.wait_ge(q0_ready, NT)
                for k in range(KC):
                    w = slice(start + k * P, start + (k + 1) * P)
                    pe.matmul(dst, wf_hi[:, b, w], mt_hi[:, k, tok], start=(k == 0), stop=False)
                    pe.matmul(dst, wf_hi[:, b, w], mt_lo[:, k, tok], start=False, stop=False)
                    ins = pe.matmul(dst, wf_lo[:, b, w], mt_hi[:, k, tok], start=False, stop=(k == KC - 1))
                ins.then_inc(done, 1)

            pe.wait_ge(id_in, 16)
            pre_turn(0, 0)
            pre_turn(0, 1)
            for i in range(NT + 2):
                if i < NT:
                    pe.wait_ge(nt_ready[0], i + 1)
                    if i:
                        pe.wait_ge(q0_ready, i)
                    for n in range(2):
                        for k in range(KC):
                            if i == 0 and n == 0:
                                pe.wait_ge(wq_ready, k + 1)
                            w = slice(n * HID, (n + 1) * HID)
                            ins = product(Q0[:, n, :], nt_hi[:, i % 2, k], nt_lo[:, i % 2, k],
                                          wq_hi[:, k, w], wq_lo[:, k, w], k == 0, k == KC - 1)
                    ins.then_inc(q0_done, 1)
                if i < 3:
                    if i == 0:
                        pe.wait_ge(m_ready, 1)
                    for h in range(HEADS_AT[i], HEADS_AT[i + 1]):
                        pe.wait_ge(wsum_lo_ready[h % 2], h // 2 + 1)
                        if h >= 2:
                            pe.wait_ge(mw_ready, h - 1)
                        product(Y0[h % 2], m_hi[:, h], m_lo[:, h], wsum_hi[:, h % WSUM_BUFS],
                                wsum_lo[:, h % WSUM_BUFS], True, True)\
                            .then_inc(mw_done, 1)
                if 2 <= i:
                    t = i - 2
                    pe.wait_ge(sigt_ready, t + 1)
                    if t == 0:
                        pe.wait_ge(mw_ready, H0)
                    if t >= 2:
                        pe.wait_ge(delta_ready[0], t - 1)
                    for h in range(H0):
                        ins = product(Y0[t % 2], sigt_hi[:, h], sigt_lo[:, h], mw_hi[:, h], mw_lo[:, h],
                                      h == 0, h == H0 - 1)
                    ins.then_inc(y_done[0], 1)
                if 3 <= i:
                    pre_turn(1, i - 3)
                if i + 2 < NT:
                    pre_turn(0, i + 2)
                if 1 <= i <= NT:
                    t = i - 1
                    pe.wait_ge(sig_scaled, t + 1)
                    if t:
                        pe.wait_ge(sigt_ready, t)
                    for h in range(H0):
                        ins = turn(SIGT[:, h // 4, (h % 4) * P:(h % 4 + 1) * P], sig[:, t % 2, h * D0:(h + 1) * D0])
                    ins.then_inc(sigt_done, 1)
                if NT <= i:
                    gate_up(i - NT, 0)
                    gate_up(i - NT, 1)

            def down(c):
                b, j = c % WBUFS, c % NJ
                pe.wait_ge(hid_ready, c + 1)
                w = slice(DW, DW + HID)
                for m in range(HALF):
                    if c == NJ:
                        pe.wait_ge(delta_ready[1], m + 1)
                    ins = product(Y1[:, m, :], hid_hi[:, c % 2, m * P:(m + 1) * P], hid_lo[:, c % 2, m * P:(m + 1) * P],
                                  wf_hi[:, b, w], wf_lo[:, b, w], j == 0, j == NJ - 1)
                    if j == NJ - 1:
                        ins.then_inc(y_done[1], 1)
                if j < NJ - 1:
                    ins.then_inc(down_done, 1)
                else:
                    pe.wait_ge(y_done[1], HALF * (c // NJ + 1))
                    pe.sem_inc(down_done, 1)

            for c in range(2 * NJ):
                if c >= 2:
                    gate_up(c, 0)
                    gate_up(c, 1)
                if 0 <= c - NJ - 4 < HALF:
                    pre_turn(2, c - NJ - 4)
                if c == 1:
                    pe.wait_ge(delta_ready[0], NT)
                if c:
                    down(c - 1)
                if c == 3:
                    pre_turn(1, NT - 1)
            down(2 * NJ - 1)

            def s1_item(t, n):
                use = s1_use[t, n]
                dst = s1_bank(use)
                if use >= s1_first + S1_BUFS:
                    pe.wait_ge(s1_read, use - S1_BUFS + 1)
                elif use >= s1_first:
                    pe.wait_ge(s1_read, s1_first)
                elif use >= 2:
                    pe.wait_ge(s1_read, use - 1)
                if n == len(pieces[t]):
                    pe.wait_ge(shift_ready, t + 1)
                    pe.transpose(dst[0:STK, 0:P], shift[:, t % 2].rearrange("p q s j -> p (q s j)"), ident[:])\
                      .then_inc(s1_done, 1)
                    return
                q, j, nh, k0, kw, part = pieces[t][n]
                diagonal = k0 + kw == (t + 1) * P
                for i in range(nh):
                    ins = pe.matmul(dst[:, i * kw:(i + 1) * kw], qt[:, j + i, cols(t)], kt[:, q, k0:k0 + kw],
                                    start=(i == 0), stop=not diagonal, skip_group_check=True)
                if diagonal:
                    ins = pe.matmul(dst[:, 0:nh * kw].rearrange("p (h k) -> p h k", h=nh)[:, :, kw - P:kw],
                                    masks[:, 0, :], masks[:, 1, :].unsqueeze(1).broadcast_to([P, nh, P]),
                                    start=False, stop=True, skip_group_check=True)
                ins.then_inc(s1_done, 1)

            def project(t, k, dst, w):
                return product(dst, mt_hi[:, k, cols(t)], mt_lo[:, k, cols(t)], wkv_hi[:, k, w], wkv_lo[:, k, w],
                               k == 0, k == KC - 1)

            def turn_keys(u):
                pe.wait_ge(nt_ready[2], min(NT, max(HALF, u + HALF - 1)))
                if u:
                    pe.wait_ge(kt_ready, 2 * u)
                pe.wait_ge(qs_bias, 2 * (u + 1))
                pe.wait_ge(ks_ready, 2 * (u + 1))
                turn(TR[2][:, 0:P], f32(ks[:, u % 2].rearrange("p r c -> p (r c)"))).then_inc(ktr_done, 1)

            def turn_queries(u, g):
                if g == 0:
                    pe.wait_ge(qs_ready, u + 1)
                    if u == 0:
                        pe.wait_ge(delta_ready[1], NT)
                    else:
                        pe.wait_ge(qt_act, 2 * u)
                if g == 1 and u:
                    pe.wait_ge(qt_dve, 2 * u)
                if g == 2:
                    pe.wait_ge(qt_act, 2 * u + 1)
                if g == 3:
                    pe.wait_ge(qt_dve, 2 * u + 1)
                for j in range(4):
                    pair = 4 * g + j
                    ins = turn(STKT[g % 2][:, j * P:(j + 1) * P],
                               f32(qs[:, u % 2, 2 * pair:2 * pair + 2, :].rearrange("p q c -> p (q c)")))
                ins.then_inc(qtr_done, 1)

            def early_items(t, place):
                items = early[t][place]
                if items:
                    pe.wait_ge(mask_ready, 1)
                    pe.wait_ge(delta_ready[1], NT)
                    pe.wait_ge(qt_act, 2 * (items[-1][0] + 1))
                    pe.wait_ge(qt_dve, 2 * (items[-1][0] + 1))
                for item in items:
                    s1_item(*item)

            pe.wait_ge(wkv_ready, KC)
            for t in range(NT + 1):
                u = t - 1
                if t < NT:
                    pe.wait_ge(nt_ready[2], t + 1)
                    if t >= 2:
                        pe.wait_ge(qs_ready, t - 1)
                    project(t, 0, QP[t % 2], slice(0, HID))
                if u >= 0:
                    turn_keys(u)
                if t < NT:
                    project(t, 1, QP[t % 2], slice(0, HID))
                early_items(t, 0)
                if t < NT:
                    project(t, 2, QP[t % 2], slice(0, HID))
                if u >= 0:
                    turn_queries(u, 0)
                if t < NT:
                    project(t, 3, QP[t % 2], slice(0, HID))
                if u >= 0:
                    turn_queries(u, 1)
                early_items(t, 1)
                if 2 <= t <= HALF + 1:
                    pe.wait_ge(kt_ready, 2 * t)
                    pre_turn(2, t + HALF - 2)
                if u >= 0:
                    turn_queries(u, 2)
                if t < NT:
                    if t:
                        pe.wait_ge(v_ready, t)
                        pe.wait_ge(ks_ready, 2 * t)
                    for k in range(KC):
                        ins = project(t, k, KVP, slice(HID, HID + 2 * D1))
                    ins.then_inc(qkv_done, 1)
                if u >= 0:
                    turn_queries(u, 3)
                    early_items(t, 2)

            def s2_piece(use, t, kb, p, g):
                dst = s2_bank(use)
                if use < last_use + 2:
                    if use >= S2_BUFS:
                        pe.wait_ge(p_ready, use - S2_BUFS + 1)
                elif use < last_use + 4:
                    pe.wait_ge(s1_read, len(s1_order))
                else:
                    pe.wait_ge(p_ready, use - 4 + 1)
                diagonal = kb == t
                ins = pe.matmul(dst, kt[:, p, cols(kb)], qt[:, 4 * g:4 * g + 4, cols(t)],
                                start=True, stop=not diagonal, skip_group_check=True)
                if diagonal:
                    ins = pe.matmul(dst, masks[:, 0, :], masks[:, 2, :].unsqueeze(1).broadcast_to([P, 4, P]),
                                    start=False, stop=True, skip_group_check=True)
                ins.then_inc(s2_done, 1)

            def values(batch, t, kb, p):
                pe.wait_ge(p_ready, 4 * batch + 4)
                if kb == 0 and p == 0 and t:
                    pe.wait_ge(o_read, t)
                for g in range(4):
                    ins = pe.matmul(PV[VW * g:VW * (g + 1), p, :], vals[:, kb, :],
                                    probs[:, (4 * batch + g) % P_BUFS, :], start=(kb == 0), stop=(kb == t),
                                    skip_group_check=True)
                ins.then_inc(pv_done, 1)

            def back(t, step):
                if step in ("turn0", "turn1"):
                    q = int(step == "turn1")
                    if q == 0:
                        pe.wait_ge(o_read, t + 1)
                        if t:
                            pe.wait_ge(delta_ready[2], t)
                        if turned3_before[t]:
                            pe.wait_ge(nt_ready[3], turned3_before[t])
                    else:
                        pe.wait_ge(bg_o_read, 2 * t + 1)
                    for i in range(4):
                        ins = turn(BG[:, i * P:(i + 1) * P], o_sb[:, q, i * P:(i + 1) * P])
                    ins.then_inc(bg_o, 1)
                elif step == "turn2":
                    pe.wait_ge(bg_o_read, 2 * t + 2)
                    for k in range(KC):
                        ins = turn(BG[:, k * P:(k + 1) * P], attn[:, k * P:(k + 1) * P])
                    ins.then_inc(bg_a, 1)
                elif step[:-1] == "project":
                    k = int(step[-1])
                    if k == 0:
                        pe.wait_ge(bg_a_read, t + 1)
                        if t == 0:
                            pe.wait_ge(wo1_ready, 1)
                    ins = product(BG, at_hi[:, k], at_lo[:, k], wo1_hi[:, k], wo1_lo[:, k], k == 0, k == KC - 1)
                    if k == KC - 1:
                        ins.then_inc(y_done[2], 1)
                elif step == "turn3":
                    pe.wait_ge(delta_ready[2], projected_before[t])
                    pre_turn(3, t)

            def experts(e):
                i = e // 2
                if e % 2 == 0 and i < NT:
                    pe.wait_ge(nt_ready[3], i + 1)
                    hi, lo = tile_transpose(3, i)
                    if i == 0:
                        pe.wait_ge(we_ready, KC)
                    if i >= 2:
                        pe.wait_ge(hs_ready, i - 1)
                    for k in range(KC):
                        ins = product(L3[i % 2], hi[:, k], lo[:, k], we_hi[:, k, HID:], we_lo[:, k, HID:],
                                      k == 0, k == KC - 1)
                    ins.then_inc(l3_done, 1)
                    if i >= 4:
                        pe.wait_ge(delta_ready[3], i - 3)
                    for k in range(KC):
                        product(O3[i % 4], hi[:, k], lo[:, k], we_hi[:, k, 0:HID], we_lo[:, k, 0:HID], k == 0, False)
                if e % 2 and 2 <= i < NT + 2:
                    t = i - 2
                    pe.wait_ge(ht_ready, t + 1)
                    if t == 0:
                        pe.wait_ge(lb_ready, 2)
                    for c in range(2):
                        ins = product(O3[t % 4], ht_hi[:, t % 2, c], ht_lo[:, t % 2, c], lb_hi[:, c], lb_lo[:, c],
                                      False, c == 1)
                    ins.then_inc(y_done[3], 1)
                if e % 2 and 1 <= i <= NT:
                    t = i - 1
                    pe.wait_ge(hs_ready, t + 1)
                    if t:
                        pe.wait_ge(ht_ready, t)
                    for c in range(2):
                        ins = turn(HT[0:ER // 2, c * P:(c + 1) * P], hs[:, t % 2, c * (ER // 2):(c + 1) * (ER // 2)])
                    ins.then_inc(ht_done, 1)

            pe.wait_ge(qt_act, 2 * NT)
            pe.wait_ge(qt_dve, 2 * NT)
            batch = 0
            before = None
            for t, kb, p, after, steps_back, e in slots:
                if kb == 0 and p == 0:
                    pe.wait_ge(shift_in[t % 2], 64 * (t // 2 + 1))
                for g in range(4):
                    if g == 3 and before is not None:
                        values(*before)
                    for u, step in steps_back[g]:
                        back(u, step)
                    if t is not None:
                        s2_piece(4 * batch + g, t, kb, p, g)
                    for item in after[g]:
                        s1_item(*item)
                before = (batch, t, kb, p) if t is not None else None
                batch += t is not None
                for u, step in steps_back[4]:
                    back(u, step)
                if e is not None:
                    experts(e)


def layouts(i):
    def hidden_major(w):
        return w.T.reshape(KC, P, w.shape[0]).transpose(1, 0, 2)

    heads = i["L0_attn_Wq"].reshape(H0, G0, D0, HID)[:, 0].reshape(H0 * D0, HID)
    gate, up = (i[f"L0_ffn_{n}_w"].reshape(NJ, P, KC, P).transpose(0, 3, 2, 1).reshape(NJ, P, KC * P)
                for n in ("gate", "up"))
    down = i["L0_ffn_down_w"].T.reshape(NJ, P, HID)
    experts = np.concatenate([i["L1_ffn_base_W"], i["L1_ffn_gate_W"], i["L1_ffn_lora_A"].reshape(ER, HID)])
    return {
        "x": i["L0_attn_hidden_states"],
        "wq": hidden_major(heads),
        "bq": i["L0_attn_bq"].reshape(H0, G0, D0)[:, 0].reshape(1, H0 * D0),
        "z": i["L0_attn_z"].reshape(1, H0 * D0),
        "m": i["L0_attn_M"].transpose(2, 0, 1),
        "wo0": i["L0_attn_Wo"].reshape(HID, H0, G0, D0).transpose(1, 3, 2, 0).reshape(H0, D0, G0 * HID),
        "lnw": i["L0_ffn_ln_w"].reshape(1, HID),
        "wf": np.concatenate([gate, up, down], axis=2),
        "wkv": i["L1_attn_Wqkv"].reshape(KC, P, HID + 2 * D1).transpose(1, 0, 2),
        "wo1": i["L1_attn_Wo"].reshape(KC, P, HID).transpose(1, 0, 2),
        "we": experts.T.reshape(KC, P, HID + LG),
        "lb": i["L1_ffn_lora_B"].transpose(0, 2, 1).reshape(2, ER // 2, HID).transpose(1, 0, 2),
    }


def kernel(**inputs):
    import concourse.bacc as _bacc
    from concourse.bass_utils import run_bass_kernel_spmd as _run

    nc = _bacc.Bacc("TRN2", target_bir_lowering=False, num_devices=1)
    arrays, aps = {}, {}
    for name, a in {**layouts({n: np.asarray(v) for n, v in inputs.items()}), **constants()}.items():
        a = np.ascontiguousarray(a)
        arrays[f"in_{name}"] = a
        aps[name] = nc.dram_tensor(f"in_{name}", a.shape, mybir.dt.from_np(a.dtype), kind="ExternalInput").ap()
    out = nc.dram_tensor("out_0", (1, S, HID), F32, kind="ExternalOutput").ap()
    build(nc, aps, out)
    r = _run(nc, [arrays], core_ids=[0])
    return r.results[0]["out_0"]
```
